# Optimizing a Trainium2 kernel written in Bass

```python
import numpy as np
import jax
import jax.numpy as jnp

def _softmax(x, axis=-1):
    return jax.nn.softmax(x, axis=axis)

def _gelu(x):
    return jax.nn.gelu(x, approximate=True)

def _silu(x):
    return jax.nn.silu(x)

def _sigmoid(x):
    return jax.nn.sigmoid(x)

def _layernorm(x, axis=-1, eps=1e-05):
    m = jnp.mean(x, axis=axis, keepdims=True)
    v = jnp.var(x, axis=axis, keepdims=True)
    return (x - m) / jnp.sqrt(v + eps)

def _scatter_add(tgt, idx, src, axis=0):
    return tgt.at[idx].add(src)

def _segment_sum(src, seg, n):
    return jax.ops.segment_sum(src, seg, n)
kernel_name = 'mk_decoder_preln_d1_seqx_r4_6592c0'

def setup_inputs(seed: int=0):
    np.random.seed(seed)
    _w = jnp.asarray

    def _rec_inputs():
        import jax
        import jax.numpy as jnp
        _rk = jax.random.key(seed)
        x = -0.0002928 + 1 * jax.random.normal(jax.random.fold_in(_rk, 1), (32, 100, 256), jnp.float32)
        _lenS = 100 - jax.random.randint(jax.random.fold_in(_rk, 7), (32,), 0, max(1, 100 // 4) + 1, jnp.int32)
        _lenS2 = 361 - jax.random.randint(jax.random.fold_in(_rk, 8), (32,), 0, max(1, 361 // 4) + 1, jnp.int32)
        _ctx_1024P = jax.random.normal(jax.random.fold_in(_rk, 11), (32, 16, 256), jnp.float32)
        _ctx_1024c = jax.random.dirichlet(jax.random.fold_in(_rk, 511), 0.3 * jnp.ones((16,), jnp.float32), (32, 361))
        _ctx_1024t = jnp.einsum('bsk,bkd->bsd', _ctx_1024c, _ctx_1024P)
        _ctx_1024t = _ctx_1024t * jax.lax.rsqrt(jnp.mean(jnp.square(_ctx_1024t)) + 1e-12) * 0.953939
        ctx_1024 = 4.13588e-05 + 0.999923 * (_ctx_1024t + 0.3 * jax.random.normal(jax.random.fold_in(_rk, 611), (32, 361, 256), jnp.float32))
        _validS = jnp.arange(100)[None, :] < _lenS[:, None]
        _validS2 = jnp.arange(361)[None, :] < _lenS2[:, None]
        _causal = jnp.tril(jnp.ones((100, 100), dtype=bool))
        mask_Bx1x1xS2_if1 = jnp.where(jnp.ones((32, 1, 1, 361), dtype=bool), 1, 0).astype(jnp.int32)
        return (x, ctx_1024, mask_Bx1x1xS2_if1)
    x, ctx_1024, mask_Bx1x1xS2_if1 = _rec_inputs()

    def _L0_attn_setup():
        import jax, jax.numpy as jnp
        import numpy as np
        N_HEADS = 16
        HIDDEN = 256
        HEAD_DIM = 64
        BSZ = 4
        SEQ = 256
        SCALE = HEAD_DIM ** (-0.5)
        key = jax.random.key(seed)
        k_x, k_q, k_k, k_v, k_o = jax.random.split(key, 5)
        s = HIDDEN ** (-0.5)
        return {'x': jax.random.normal(k_x, (BSZ, SEQ, HIDDEN), dtype=jnp.float32), 'wq': jax.random.normal(k_q, (N_HEADS * HEAD_DIM, HIDDEN), dtype=jnp.float32) * s, 'wk': jax.random.normal(k_k, (N_HEADS * HEAD_DIM, HIDDEN), dtype=jnp.float32) * s, 'wv': jax.random.normal(k_v, (N_HEADS * HEAD_DIM, HIDDEN), dtype=jnp.float32) * s, 'wo': jax.random.normal(k_o, (HIDDEN, N_HEADS * HEAD_DIM), dtype=jnp.float32) * s}
    _L0_attn_all = _L0_attn_setup()
    _L0_attn_in = {k: v for k, v in _L0_attn_all.items() if k in ('wq', 'wk', 'wv', 'wo')}
    del _L0_attn_all

    def _L0_xattn_setup():
        import jax, jax.numpy as jnp
        import numpy as np
        D_MODEL = 256
        NUM_HEADS = 16
        HEAD_DIM = D_MODEL // NUM_HEADS

        def _split_heads(x):
            B, L, _ = x.shape
            return x.reshape(B, L, NUM_HEADS, HEAD_DIM).transpose(0, 2, 1, 3)
        key = jax.random.key(seed)
        ks = jax.random.split(key, 12)
        B, Lq, Lkv = (4, 256, 512)
        s = 1.0 / np.sqrt(D_MODEL)
        inp = {'decoder_hidden': jax.random.normal(ks[0], (B, Lq, D_MODEL), jnp.float32), 'encoder_hidden': jax.random.normal(ks[1], (B, Lkv, D_MODEL), jnp.float32), 'encoder_mask': jnp.ones((B, 1, 1, Lkv), jnp.int32), 'Wq': jax.random.normal(ks[2], (D_MODEL, D_MODEL), jnp.float32) * s, 'bq': jnp.zeros((D_MODEL,), jnp.float32), 'Wk': jax.random.normal(ks[3], (D_MODEL, D_MODEL), jnp.float32) * s, 'bk': jnp.zeros((D_MODEL,), jnp.float32), 'Wv': jax.random.normal(ks[4], (D_MODEL, D_MODEL), jnp.float32) * s, 'bv': jnp.zeros((D_MODEL,), jnp.float32), 'Wo': jax.random.normal(ks[5], (D_MODEL, D_MODEL), jnp.float32) * s, 'bo': jnp.zeros((D_MODEL,), jnp.float32)}
        return inp
    _L0_xattn_all = _L0_xattn_setup()
    _L0_xattn_in = {k: v for k, v in _L0_xattn_all.items() if k in ('Wq', 'bq', 'Wk', 'bk', 'Wv', 'bv', 'Wo', 'bo')}
    del _L0_xattn_all

    def _L0_ffn_setup():
        import jax, jax.numpy as jnp
        import numpy as np
        E = 8
        EPS = 1e-05
        key = jax.random.key(seed)
        ks = jax.random.split(key, 6)
        d, f = (256, 1024)
        B, S = (2, 256)
        x = jax.random.normal(ks[0], (B, S, d), dtype=jnp.float32)
        c = jax.random.normal(ks[1], (d, E), dtype=jnp.float32)
        q, _ = jnp.linalg.qr(c)
        centroids = (0.1 * q.T).astype(jnp.float32)
        w1 = jax.random.normal(ks[2], (E, d, f), dtype=jnp.float32) / np.sqrt(d).astype(np.float32)
        b1 = jnp.zeros((E, f), dtype=jnp.float32)
        w2 = jax.random.normal(ks[3], (E, f, d), dtype=jnp.float32) * 0.02
        b2 = jnp.zeros((E, d), dtype=jnp.float32)
        gamma = jnp.ones((E, d), dtype=jnp.float32)
        beta = jnp.zeros((E, d), dtype=jnp.float32)
        return dict(x=x, centroids=centroids, w1=w1, b1=b1, w2=w2, b2=b2, gamma=gamma, beta=beta)
    _L0_ffn_all = _L0_ffn_setup()
    _L0_ffn_in = {k: v for k, v in _L0_ffn_all.items() if k in ('centroids', 'w1', 'b1', 'w2', 'b2', 'gamma', 'beta')}
    del _L0_ffn_all
    return {'x': x, 'ctx_1024': ctx_1024, 'mask_Bx1x1xS2_if1': mask_Bx1x1xS2_if1, 'L0_attn_wq': _L0_attn_in['wq'], 'L0_attn_wk': _L0_attn_in['wk'], 'L0_attn_wv': _L0_attn_in['wv'], 'L0_attn_wo': _L0_attn_in['wo'], 'L0_xattn_Wq': _L0_xattn_in['Wq'], 'L0_xattn_bq': _L0_xattn_in['bq'], 'L0_xattn_Wk': _L0_xattn_in['Wk'], 'L0_xattn_bk': _L0_xattn_in['bk'], 'L0_xattn_Wv': _L0_xattn_in['Wv'], 'L0_xattn_bv': _L0_xattn_in['bv'], 'L0_xattn_Wo': _L0_xattn_in['Wo'], 'L0_xattn_bo': _L0_xattn_in['bo'], 'L0_ffn_centroids': _L0_ffn_in['centroids'], 'L0_ffn_w1': _L0_ffn_in['w1'], 'L0_ffn_b1': _L0_ffn_in['b1'], 'L0_ffn_w2': _L0_ffn_in['w2'], 'L0_ffn_b2': _L0_ffn_in['b2'], 'L0_ffn_gamma': _L0_ffn_in['gamma'], 'L0_ffn_beta': _L0_ffn_in['beta']}

def reference(x, ctx_1024, mask_Bx1x1xS2_if1, L0_attn_wq, L0_attn_wk, L0_attn_wv, L0_attn_wo, L0_xattn_Wq, L0_xattn_bq, L0_xattn_Wk, L0_xattn_bk, L0_xattn_Wv, L0_xattn_bv, L0_xattn_Wo, L0_xattn_bo, L0_ffn_centroids, L0_ffn_w1, L0_ffn_b1, L0_ffn_w2, L0_ffn_b2, L0_ffn_gamma, L0_ffn_beta):
    import jax
    import jax.numpy as jnp

    def _L0_attn_ref(x, wq, wk, wv, wo):
        import jax, jax.numpy as jnp
        import numpy as np
        N_HEADS = 16
        HIDDEN = 256
        HEAD_DIM = 64
        BSZ = 4
        SEQ = 256
        SCALE = HEAD_DIM ** (-0.5)
        bsz, seqlen, _ = x.shape
        xq = jnp.einsum('bsh,oh->bso', x, wq)
        xk = jnp.einsum('bsh,oh->bso', x, wk)
        xv = jnp.einsum('bsh,oh->bso', x, wv)
        xq = xq.reshape(bsz, N_HEADS, seqlen, HEAD_DIM)
        xk = xk.reshape(bsz, N_HEADS, seqlen, HEAD_DIM)
        xv = xv.reshape(bsz, N_HEADS, seqlen, HEAD_DIM)
        scores = jnp.einsum('bhid,bhjd->bhij', xq, xk) * SCALE
        scores = jax.nn.softmax(scores, axis=-1)
        out = jnp.einsum('bhij,bhjd->bhid', scores, xv)
        out = out.reshape(bsz, seqlen, N_HEADS * HEAD_DIM)
        return jnp.einsum('bso,ho->bsh', out, wo)

    def _L0_xattn_ref(decoder_hidden, encoder_hidden, encoder_mask, Wq, bq, Wk, bk, Wv, bv, Wo, bo):
        import jax, jax.numpy as jnp
        import numpy as np
        D_MODEL = 256
        NUM_HEADS = 16
        HEAD_DIM = D_MODEL // NUM_HEADS

        def _split_heads(x):
            B, L, _ = x.shape
            return x.reshape(B, L, NUM_HEADS, HEAD_DIM).transpose(0, 2, 1, 3)
        B, Lq, _ = decoder_hidden.shape
        q = _split_heads(decoder_hidden @ Wq.T + bq)
        k = _split_heads(encoder_hidden @ Wk.T + bk)
        v = _split_heads(encoder_hidden @ Wv.T + bv)
        scale = 1.0 / np.sqrt(HEAD_DIM).astype(np.float32)
        scores = jnp.einsum('bhqd,bhkd->bhqk', q, k) * scale
        scores = jnp.where(encoder_mask == 0, jnp.float32(-jnp.inf), scores)
        attn = jax.nn.softmax(scores, axis=-1)
        out = jnp.einsum('bhqk,bhkd->bhqd', attn, v)
        out = out.transpose(0, 2, 1, 3).reshape(B, Lq, D_MODEL)
        return out @ Wo.T + bo

    def _L0_ffn_ref(x, centroids, w1, b1, w2, b2, gamma, beta):
        import jax, jax.numpy as jnp
        import numpy as np
        E = 8
        EPS = 1e-05
        B, S, d = x.shape
        feats = x.reshape(-1, d)
        aff = feats @ centroids.T
        eid = jnp.argmax(aff, axis=1)
        mu = jnp.mean(feats, axis=-1, keepdims=True)
        var = jnp.var(feats, axis=-1, keepdims=True)
        xhat = (feats - mu) * jax.lax.rsqrt(var + EPS)
        out = jnp.zeros_like(feats)
        for e in range(E):
            mask = (eid == e).astype(feats.dtype)[:, None]
            h = xhat * gamma[e] + beta[e]
            y = feats + jax.nn.relu(h @ w1[e] + b1[e]) @ w2[e] + b2[e]
            alpha = jax.nn.sigmoid(feats @ centroids[e])[:, None]
            out = out + mask * (alpha * y + (1.0 - alpha) * feats)
        return out.reshape(B, S, d)
    x = x + _L0_attn_ref(_layernorm(x, axis=-1), L0_attn_wq, L0_attn_wk, L0_attn_wv, L0_attn_wo)
    x = x + _L0_xattn_ref(_layernorm(x, axis=-1), ctx_1024, mask_Bx1x1xS2_if1, L0_xattn_Wq, L0_xattn_bq, L0_xattn_Wk, L0_xattn_bk, L0_xattn_Wv, L0_xattn_bv, L0_xattn_Wo, L0_xattn_bo)
    x = x + _L0_ffn_ref(_layernorm(x, axis=-1), L0_ffn_centroids, L0_ffn_w1, L0_ffn_b1, L0_ffn_w2, L0_ffn_b2, L0_ffn_gamma, L0_ffn_beta)
    return x

_drawn_inputs = setup_inputs


def setup_inputs(seed=0):
    import zlib

    import numpy as np

    out = dict(_drawn_inputs(seed))
    spreads = {'L0_xattn_bq': (0.0, 0.289),
     'L0_xattn_bk': (0.0, 0.8),
     'L0_xattn_bv': (0.0, 0.1),
     'L0_xattn_bo': (0.0, 0.1),
     'L0_ffn_b1': (0.0, 0.709),
     'L0_ffn_b2': (0.0, 0.328),
     'L0_ffn_gamma': (1.0, 0.6),
     'L0_ffn_beta': (0.0, 0.734)}
    factors = {}
    for name, (base, spread) in spreads.items():
        noise = np.random.default_rng([zlib.crc32(name.encode()), seed]).standard_normal(out[name].shape)
        drawn = base * np.exp(spread * noise) if base else spread * noise
        out[name] = jnp.asarray(drawn.astype(out[name].dtype))
    for name, factor in factors.items():
        out[name] = (out[name] * factor).astype(out[name].dtype)
    return out
```

```python
from contextlib import ExitStack

import concourse.bass as bass
from concourse import mybir

F32 = mybir.dt.float32
F32R = mybir.dt.float32r
I32 = mybir.dt.int32
U32 = mybir.dt.uint32
ALU = mybir.AluOpType
ACT = mybir.ActivationFunctionType
AX_X = mybir.AxisListType.X

B, S, D = 32, 100, 256
KD = D // 128
EPS = 1e-5

H1, HD1 = 16, 64
O1 = H1 * HD1
QUAD = 4
QUADS = B // QUAD
QT_TOK = QUAD * S
GH = 4
GB = H1 // GH
GQ = QUAD * GB
ROWS = S * O1 // HD1
NT = O1 // 128

S2 = 361
S2E = S2 + 1
H2, HD2 = 16, 16
KT = [121, 121, 119]
KT0 = [0, 121, 242]
HG = 8
NEG = -1.0e30

E, F = 8, 1024
NF = F // 128
T = 256
TILES = (B * S + E * (T - 1)) // T
SLOTS = TILES * T
ROWW = D + 1
NO_TOKEN = 100000.0


def split3(pe, out, hi_l, lo_l, hi_r, lo_r, first, last):
    pe.matmul(out, hi_l, lo_r, start=first, stop=False)
    pe.matmul(out, lo_l, hi_r, start=False, stop=False)
    return pe.matmul(out, hi_l, hi_r, start=False, stop=last)


def constants(nc, c, xs):
    with nc.semaphore("pool_step") as pool_step, nc.semaphore("empty_ready") as empty_ready, nc.Block() as block:
        @block.sync
        def _(sp):
            sp.wait_ge(empty_ready, 2)
            sp.dma_start(xs.rearrange("(k p) d -> p k d", p=128),
                         c.empty[:].unsqueeze(1).to_broadcast([128, SLOTS // 128, ROWW])).then_inc(c.xs_cleared, 16)

        @block.gpsimd
        def _(pool):
            pool.memset(c.empty[:, 0:D], 0.0).then_inc(empty_ready, 1)
            pool.memset(c.empty[:, D:ROWW], NO_TOKEN).then_inc(empty_ready, 1)
            pool.memset(c.ident[:], 0.0).then_inc(pool_step, 1)
            pool.memset(c.neg_ident[:], 0.0).then_inc(pool_step, 1)
            pool.memset(c.minus_half[:], -0.5).then_inc(pool_step, 1)
            pool.memset(c.ones_f[:], 1.0).then_inc(pool_step, 1)
            pool.memset(c.before[:], 1.0).then_inc(pool_step, 1)
            pool.memset(c.head_of[:], 1.0).then_inc(pool_step, 1)
            pool.wait_ge(pool_step, 6)
            pool.affine_select(out=c.ident[:], in_=c.ident[:], compare_op=ALU.not_equal, fill=1.0, base=0,
                               pattern=[[-1, 128]], channel_multiplier=1).then_inc(pool_step, 1)
            pool.affine_select(out=c.neg_ident[:], in_=c.neg_ident[:], compare_op=ALU.not_equal, fill=-1.0, base=0,
                               pattern=[[-1, 128]], channel_multiplier=1).then_inc(pool_step, 1)
            pool.affine_select(out=c.before[:], in_=c.before[:], compare_op=ALU.is_gt, fill=0.0, base=0,
                               pattern=[[1, S]], channel_multiplier=-1).then_inc(pool_step, 1)
            pool.affine_select(out=c.head_of[:], in_=c.head_of[:], compare_op=ALU.is_ge, fill=0.0, base=0,
                               pattern=[[-HD2, HG]], channel_multiplier=1).then_inc(pool_step, 1)
            pool.wait_ge(pool_step, 10)
            pool.affine_select(out=c.head_of[:], in_=c.head_of[:], compare_op=ALU.is_ge, fill=0.0, base=HD2 - 1,
                               pattern=[[HD2, HG]], channel_multiplier=-1).then_inc(pool_step, 1)

        @block.vector
        def _(dve):
            dve.wait_ge(pool_step, 6)
            dve.tensor_copy(c.ones_r[:], c.ones_f[:])


class Shared:
    pass


def self_attention(nc, c, x, wqkT, wvT, woT, v_dram):
    with ExitStack() as ctx:
        def sb(name, shape, dt=F32):
            return ctx.enter_context(nc.sbuf_tensor(name, shape, dt))

        def psum(name, shape, dt=F32):
            return ctx.enter_context(nc.psum_tensor(name, shape, dt))

        def sem(name):
            return ctx.enter_context(nc.semaphore(name))

        w_stage = sb("w_stage", [128, KD, O1])
        w_hi = sb("w_hi", [128, 3, KD, O1], F32R)
        w_lo = sb("w_lo", [128, 3, KD, O1], F32R)
        wo_sb = sb("wo_sb", [128, NT, D])
        stats = sb("stats", [S, B, 6])
        mv = sb("mv", [S, B, 2])
        var_eps = sb("var_eps", [S, B])
        rstd = sb("rstd", [S, B])
        xn = sb("xn", [S, QUAD, D])
        x_hi = sb("x_hi", [128, KD, QT_TOK], F32R)
        x_lo = sb("x_lo", [128, KD, QT_TOK], F32R)
        q_t = sb("q_t", [128, 2, ROWS])
        k_t = sb("k_t", [128, 2, ROWS])
        v_tok = sb("v_tok", [S, QUAD, O1])
        v_ext = sb("v_ext", [S, QUAD, H1, HD1 + 1])
        row_max = sb("row_max", [S, 2, GH])
        diag = sb("diag", [S, 2, GH, S], F32R)
        probs = sb("probs", [S, 2, GH * S])
        recip = sb("recip", [S, GH])
        o_norm = sb("o_norm", [S, 2, GH * HD1])
        o_t = sb("o_t", [128, 2, ROWS // 2])

        ps_p = [psum(f"ps_p{i}", [128, 512]) for i in range(2)]
        ps_s = [psum(f"ps_s{i}", [128, 512]) for i in range(2)]
        ps_t = [psum(f"ps_t{i}", [128, 512]) for i in range(2)]
        ps_o = psum("ps_o", [128, 512])
        ps_ot = psum("ps_ot", [128, 512])

        x_loaded = sem("x_loaded")
        w_loaded = sem("w_loaded")
        w_hi_ready = sem("w_hi_ready")
        w_lo_ready = sem("w_lo_ready")
        wo_loaded = sem("wo_loaded")
        ones_ready = sem("ones_ready")
        stats_ready = sem("stats_ready")
        mv_ready = sem("mv_ready")
        eps_added = sem("eps_added")
        rstd_ready = sem("rstd_ready")
        xn_ready = sem("xn_ready")
        filled = sem("filled")
        drained_act = sem("drained_act")
        drained_dve = sem("drained_dve")
        v_stored = [sem(f"v_stored{i}") for i in range(QUAD)]
        v_loaded = [sem(f"v_loaded{i}") for i in range(QUAD)]
        scores_ready = sem("scores_ready")
        max_ready = sem("max_ready")
        diag_ready = sem("diag_ready")
        shifted_ready = sem("shifted_ready")
        probs_ready = sem("probs_ready")
        pv_ready = sem("pv_ready")
        recip_ready = sem("recip_ready")
        o_ready = sem("o_ready")
        ot_ready = sem("ot_ready")
        ot_copied_act = sem("ot_copied_act")
        ot_copied_dve = sem("ot_copied_dve")
        y_ready = sem("y_ready")
        x1_ready = sem("x1_ready")

        FX, FV = KD, KD + 2 * QUAD
        FILLS = FV + 2 * NT
        TAIL = 4

        def spread(copy, f, a):
            t, dst = (f - FV) // 2, (q_t if (f - FV) % 2 == 0 else k_t)
            src = ps_p[f % 2][64 * a:64 * a + 64, 0:QT_TOK].rearrange("p (i s) -> p i s", s=S)
            for odd in range(2):
                out = dst[64 * odd:64 * odd + 64, :, :].rearrange("p i (s c) -> p i s c", c=H1)[:, :, :, 2 * t + a]
                ins = copy(out, src[:, odd::2, :])
            return ins

        def copy_ot(copy, g, a):
            src = ps_ot[64 * a:64 * a + 64, 0:2 * S].rearrange("p (w k two) -> p w k two", w=2, two=2)
            for odd in range(2):
                base = (g % GB) * GH * S // 2
                out = o_t[64 * odd:64 * odd + 64, (g // GB) % 2, base:base + GH * S // 2].rearrange(
                    "p (w a k) -> p w a k", w=2, a=2)[:, :, a, :]
                ins = copy(out, src[:, :, :, odd])
            return ins

        block = ctx.enter_context(nc.Block())

        @block.sync
        def _(sp):
            for q in range(QUADS):
                sp.dma_start(c.x[:, QUAD * q:QUAD * (q + 1), 0:D],
                             x[QUAD * q:QUAD * (q + 1)].rearrange("b s d -> s b d")).then_inc(x_loaded, 16)
            sp.dma_start(wo_sb[:], woT.rearrange("(t p) n -> p t n", p=128)).then_inc(wo_loaded, 16)
            with sp.Fori(0, QUADS) as q:
                for i in range(QUAD):
                    sp.wait_ge(drained_act, q * FILLS + (FX + 2 * i + 2))
                    sp.wait_ge(drained_dve, q * FILLS + (FX + 2 * i + 2))
                    sp.dma_start(v_dram[bass.ds(q * QUAD + i, 1)].rearrange("b s n -> s (b n)"),
                                 v_tok[:, i, :]).then_inc(v_stored[i], 16)
                for i in range(QUAD):
                    sp.wait_ge(v_stored[i], q * 16 + 16)
                    sp.dma_start(v_ext[:, i, :, 0:HD1],
                                 v_dram[bass.ds(q * QUAD + i, 1)].rearrange(
                                     "b s n -> (b s n)").rearrange(
                                     "(h j d) -> j h d", j=S, d=HD1)).then_inc(v_loaded[i], 16)

        @block.scalar
        def _(act):
            for j, w in enumerate((wqkT[:, 0:O1], wqkT[:, O1:2 * O1], wvT)):
                if j:
                    act.wait_ge(w_lo_ready, j)
                act.dma_start(w_stage[:], w.rearrange("(k p) n -> p k n", p=128)).then_inc(w_loaded, 16)
                act.wait_ge(w_loaded, 16 * (j + 1))
                act.copy(w_hi[:, j], w_stage[:]).then_inc(w_hi_ready, 1)

            with act.Fori(0, QUADS) as q:
                for k in range(KD):
                    act.wait_ge(filled, q * FILLS + (k + 1))
                    act.copy(x_hi[:, k], ps_p[k % 2][:, 0:QT_TOK]).then_inc(drained_act, 1)
                for f in range(FX, FV):
                    i, v = (f - FX) // 2, (f - FX) % 2
                    act.wait_ge(filled, q * FILLS + (f + 1))
                    act.copy(v_tok[0:64, i, 512 * v:512 * (v + 1)], ps_p[f % 2][0:64, :]).then_inc(drained_act, 1)
                for f in range(FV, FILLS):
                    act.wait_ge(filled, q * FILLS + (f + 1))
                    ins = spread(act.copy, f, 0)
                    ins.then_inc(drained_act, 1)
                for j in range(GQ + TAIL):
                    if 0 <= j - 1 < GQ:
                        g = j - 1
                        act.wait_ge(shifted_ready, q * GQ + (g + 1))
                        if g >= 2:
                            act.wait_ge(pv_ready, q * GQ + (g - 1))
                        act.activation(probs[:, g % 2], ps_t[g % 2][0:S, 0:GH * S], ACT.Exp,
                                       scale=HD1 ** -0.5).then_inc(probs_ready, 1)
                    if 0 <= j - 3 < GQ:
                        g = j - 3
                        act.wait_ge(ot_ready, q * GQ + (g + 1))
                        if g >= 2 * GB and g % GB == 0:
                            act.wait_ge(y_ready, q * QUAD + (g // GB - 1))
                        copy_ot(act.copy, g, 0).then_inc(ot_copied_act, 1)

        @block.gpsimd
        def _(pool):
            pool.memset(v_ext[:, :, :, HD1:HD1 + 1], 1.0).then_inc(ones_ready, 1)
            pool.wait_ge(mv_ready, B)
            pool.tensor_scalar(var_eps[:], mv[:, :, 1], EPS, None, ALU.add).then_inc(eps_added, 1)
            pool.wait_ge(eps_added, 1)
            pool.tensor_tensor(rstd[:], var_eps[:], c.minus_half[0:S, :], ALU.pow).then_inc(rstd_ready, 1)
            with pool.Fori(0, QUADS) as q:
                for g in range(GQ):
                    pool.wait_ge(max_ready, q * GQ + (g + 1))
                    if g >= 2:
                        pool.wait_ge(shifted_ready, q * GQ + (g - 1))
                    pool.tensor_tensor(diag[:, g % 2],
                                       c.neg_ident[0:S, 0:S].unsqueeze(1).to_broadcast([S, GH, S]),
                                       row_max[:, g % 2].unsqueeze(2).to_broadcast([S, GH, S]),
                                       ALU.mult).then_inc(diag_ready, 1)

        @block.vector
        def _(dve):
            for j in range(3):
                dve.wait_ge(w_hi_ready, j + 1)
                dve.tensor_tensor(w_lo[:, j], w_stage[:], w_hi[:, j].bitcast(F32),
                                  ALU.subtract).then_inc(w_lo_ready, 1)
            dve.wait_ge(x_loaded, 16 * QUADS)
            with dve.Fori(0, B) as b:
                dve.bn_stats(stats[:, bass.ds(b, 1), :].rearrange("s b k -> s (b k)"),
                             c.x[:, bass.ds(b, 1), 0:D].rearrange("s b d -> s (b d)")).then_inc(stats_ready, 1)
            dve.wait_ge(stats_ready, B)
            for b in range(B):
                dve.bn_aggr(mv[:, b, :], stats[:, b, :]).then_inc(mv_ready, 1)
            dve.wait_ge(rstd_ready, 1)

            with dve.Fori(0, QUADS) as q:
                for i in range(QUAD):
                    b = q * QUAD + i
                    dve.tensor_scalar(xn[:, i], c.x[:, bass.ds(b, 1), 0:D].rearrange("s b d -> s (b d)"),
                                      mv[:, bass.ds(b, 1), 0:1].rearrange("s b k -> s (b k)"),
                                      rstd[:, bass.ds(b, 1)], ALU.subtract, ALU.mult).then_inc(xn_ready, 1)
                for k in range(KD):
                    dve.wait_ge(drained_act, q * FILLS + (k + 1))
                    dve.tensor_tensor(x_lo[:, k], ps_p[k % 2][:, 0:QT_TOK], x_hi[:, k].bitcast(F32),
                                      ALU.subtract).then_inc(drained_dve, 1)
                for f in range(FX, FV):
                    i, v = (f - FX) // 2, (f - FX) % 2
                    dve.wait_ge(filled, q * FILLS + (f + 1))
                    dve.tensor_copy(v_tok[64:S, i, 512 * v:512 * (v + 1)],
                                    ps_p[f % 2][64:S, :]).then_inc(drained_dve, 1)
                for f in range(FV, FILLS):
                    dve.wait_ge(filled, q * FILLS + (f + 1))
                    spread(dve.tensor_copy, f, 1).then_inc(drained_dve, 1)
                for j in range(GQ + TAIL):
                    if j < GQ:
                        g = j
                        dve.wait_ge(scores_ready, q * GQ + (g + 1))
                        if g >= 2:
                            dve.wait_ge(diag_ready, q * GQ + (g - 1))
                        dve.reduce_max(row_max[:, g % 2], ps_s[g % 2][0:S, 0:GH * S].rearrange(
                            "p (h j) -> p h j", h=GH), AX_X).then_inc(max_ready, 1)
                    if 0 <= j - 2 < GQ:
                        g = j - 2
                        dve.wait_ge(pv_ready, q * GQ + (g + 1))
                        o = ps_o[0:S, 0:GH * (HD1 + 1)].rearrange("p (h d) -> p h d", h=GH)
                        dve.reciprocal(recip[:], o[:, :, HD1]).then_inc(recip_ready, 1)
                        dve.wait_ge(recip_ready, q * GQ + (g + 1))
                        if g >= 2:
                            dve.wait_ge(ot_ready, q * GQ + (g - 1))
                        dve.tensor_tensor(o_norm[:, g % 2].rearrange("p (h d) -> p h d", h=GH), o[:, :, 0:HD1],
                                          recip[:].unsqueeze(2).to_broadcast([S, GH, HD1]),
                                          ALU.mult).then_inc(o_ready, 1)
                    if 0 <= j - 3 < GQ:
                        g = j - 3
                        dve.wait_ge(ot_ready, q * GQ + (g + 1))
                        if g >= 2 * GB and g % GB == 0:
                            dve.wait_ge(y_ready, q * QUAD + (g // GB - 1))
                        copy_ot(dve.tensor_copy, g, 1).then_inc(ot_copied_dve, 1)
                    if 0 <= j - 4 < GQ and (j - 4) % GB == GB - 1:
                        i = (j - 4) // GB
                        dve.wait_ge(y_ready, q * QUAD + (i + 1))
                        xb = c.x[:, bass.ds(q * QUAD + i, 1), 0:D].rearrange("s b d -> s (b d)")
                        dve.tensor_tensor(xb, ps_p[i % 2][0:S, 0:D], xb, ALU.add).then_inc(x1_ready, 1)

        @block.tensor
        def _(pe):
            pe.wait_ge(w_hi_ready, 3)
            pe.wait_ge(w_lo_ready, 3)
            pe.wait_ge(wo_loaded, 16)
            pe.wait_ge(ones_ready, 1)
            with pe.Fori(0, QUADS) as q:
                pe.wait_ge(xn_ready, q * QUAD + QUAD)
                for k in range(KD):
                    for i in range(QUAD):
                        ins = pe.transpose(ps_p[k % 2][:, S * i:S * (i + 1)], xn[:, i, 128 * k:128 * (k + 1)],
                                           c.ident[0:S, 0:S])
                    ins.then_inc(filled, 1)
                for f in range(FX, FV):
                    i, v = (f - FX) // 2, (f - FX) % 2
                    pe.wait_ge(drained_act, q * FILLS + (f - 1))
                    pe.wait_ge(drained_dve, q * FILLS + (f - 1))
                    if f == FX:
                        pe.wait_ge(drained_dve, q * FILLS + KD)
                    for k in range(KD):
                        ins = split3(pe, ps_p[f % 2][0:S, :], x_hi[:, k, S * i:S * (i + 1)],
                                     x_lo[:, k, S * i:S * (i + 1)], w_hi[:, 2, k, 512 * v:512 * (v + 1)],
                                     w_lo[:, 2, k, 512 * v:512 * (v + 1)], k == 0, k == KD - 1)
                    ins.then_inc(filled, 1)
                for f in range(FV, FILLS):
                    t, qk = (f - FV) // 2, (f - FV) % 2
                    pe.wait_ge(drained_act, q * FILLS + (f - 1))
                    pe.wait_ge(drained_dve, q * FILLS + (f - 1))
                    for k in range(KD):
                        ins = split3(pe, ps_p[f % 2][:, 0:QT_TOK], w_hi[:, qk, k, 128 * t:128 * (t + 1)],
                                     w_lo[:, qk, k, 128 * t:128 * (t + 1)], x_hi[:, k], x_lo[:, k],
                                     k == 0, k == KD - 1)
                    ins.then_inc(filled, 1)
                pe.wait_ge(drained_act, q * FILLS + FILLS)
                pe.wait_ge(drained_dve, q * FILLS + FILLS)

                def head(src, g, h):
                    i, lo = g // GB, 64 * ((g // GB) % 2)
                    r = ((g % GB) * GH + h) * S
                    return src[lo:lo + 64, i // 2, r:r + S]

                for j in range(GQ + TAIL):
                    if j < GQ:
                        g = j
                        if g >= 2:
                            pe.wait_ge(max_ready, q * GQ + (g - 1))
                        for h in range(GH):
                            ins = pe.matmul(ps_s[g % 2][0:S, S * h:S * (h + 1)], head(q_t, g, h), head(k_t, g, h),
                                            start=True, stop=True)
                        ins.then_inc(scores_ready, 1)
                    if 0 <= j - 1 < GQ:
                        g = j - 1
                        if g >= 2:
                            pe.wait_ge(probs_ready, q * GQ + (g - 1))
                        for h in range(GH):
                            pe.matmul(ps_t[g % 2][0:S, S * h:S * (h + 1)], head(k_t, g, h), head(q_t, g, h),
                                      start=(h == 0), stop=False, skip_group_check=True)
                        pe.wait_ge(diag_ready, q * GQ + (g + 1))
                        ins = pe.matmul(ps_t[g % 2][0:S, 0:GH * S], c.ones_r[0:S, 0:S],
                                        diag[:, g % 2].rearrange("p h j -> p (h j)"), start=False, stop=True,
                                        skip_group_check=True)
                        ins.then_inc(shifted_ready, 1)
                    if 0 <= j - 2 < GQ:
                        g = j - 2
                        if g % GB == 0:
                            pe.wait_ge(v_loaded[g // GB], q * 16 + 16)
                        pe.wait_ge(probs_ready, q * GQ + (g + 1))
                        if g >= 1:
                            pe.wait_ge(o_ready, q * GQ + g)
                        for h in range(GH):
                            ins = pe.matmul(ps_o[0:S, (HD1 + 1) * h:(HD1 + 1) * (h + 1)],
                                            probs[:, g % 2, S * h:S * (h + 1)],
                                            v_ext[:, g // GB, (g % GB) * GH + h, :], start=True, stop=True)
                        ins.then_inc(pv_ready, 1)
                    if 0 <= j - 3 < GQ:
                        g = j - 3
                        pe.wait_ge(o_ready, q * GQ + (g + 1))
                        if g >= 1:
                            pe.wait_ge(ot_copied_act, q * GQ + g)
                            pe.wait_ge(ot_copied_dve, q * GQ + g)
                        for w in range(2):
                            ins = pe.transpose(ps_ot[:, S * w:S * (w + 1)], o_norm[:, g % 2, 128 * w:128 * (w + 1)],
                                               c.ident[0:S, 0:S])
                        ins.then_inc(ot_ready, 1)
                    if 0 <= j - 4 < GQ and (j - 4) % GB == GB - 1:
                        i = (j - 4) // GB
                        pe.wait_ge(ot_copied_act, q * GQ + (j - 3))
                        pe.wait_ge(ot_copied_dve, q * GQ + (j - 3))
                        if i >= 2:
                            pe.wait_ge(x1_ready, q * QUAD + (i - 1))
                        heads = o_t[:, i % 2, :].rearrange("p (s t) -> p t s", t=NT)
                        for t in range(NT):
                            ins = pe.matmul(ps_p[i % 2][0:S, 0:D], heads[:, t, :], wo_sb[:, t, :],
                                            start=(t == 0), stop=(t == NT - 1))
                        ins.then_inc(y_ready, 1)
                pe.wait_ge(x1_ready, q * QUAD + QUAD)


def reach(eng, semaphore, value):
    if isinstance(value, int) and value <= 0:
        return
    eng.wait_ge(semaphore, value)


def paired(eng, emit):
    emit(0, 0, False)
    emit(1, 1, False)
    with eng.Fori(1, B // 2 - 1) as i:
        emit(i * 2, 0, False)
        emit(i * 2 + 1, 1, False)
    emit(B - 2, 0, False)
    emit(B - 1, 1, True)


def row(b):
    return b if isinstance(b, int) else bass.ds(b, 1)


def at_batch(tensor, b, cols):
    if isinstance(b, int):
        return tensor[:, b, cols]
    return tensor[:, bass.ds(b, 1), cols].rearrange("p b d -> p (b d)")


def cross_attention(nc, c, ctx_in, mask, maskT, wq, wk, wv, wo, bq, bk, bv, bo):
    with ExitStack() as ctx:
        def sb(name, shape, dt=F32):
            return ctx.enter_context(nc.sbuf_tensor(name, shape, dt))

        def psum(name, shape, dt=F32):
            return ctx.enter_context(nc.psum_tensor(name, shape, dt))

        def sem(name):
            return ctx.enter_context(nc.semaphore(name))

        KP = KT[0]
        wq_sb = sb("wq2", [128, KD, D])
        wk_st = sb("wk_stage", [128, KD, D])
        wv_st = sb("wv_stage", [128, KD, D])
        wk_hi = sb("wk_hi", [128, KD, D], F32R)
        wk_lo = sb("wk_lo", [128, KD, D], F32R)
        wv_hi = sb("wv_hi", [128, KD, D], F32R)
        wv_lo = sb("wv_lo", [128, KD, D], F32R)
        wo_sb = sb("wo2", [128, KD, D])
        bq_sb = sb("bq", [128, KD])
        bk_sb = sb("bk", [128, KD])
        bv_sb = sb("bv", [KP, D])
        bo_sb = sb("bo", [S, D])
        mask_t = sb("mask_t", [KP, 3, B], I32)
        key_live = sb("key_live", [KP, 3, B])
        key_bias = sb("key_bias", [KP, 3, B])
        mask_i = sb("mask_i", [S, 2, S2], I32)
        mask_f = sb("mask_f", [S, 2, S2])
        c_tok = sb("c_tok", [KP, 2, 3, D])
        c_hi = sb("c_hi", [128, KD, S2E], F32R)
        c_lo = sb("c_lo", [128, KD, S2E], F32R)
        stats = sb("stats2", [S, 6])
        mv = sb("mv2", [S, 2])
        var_eps = sb("var_eps2", [S, 1])
        rstd = sb("rstd2", [S, 1])
        xn = sb("xn2", [S, D])
        x_t = sb("x_t2", [128, KD * S])
        q_b = sb("q_b", [128, KD * S])
        q_hi = sb("q_hi", [128, KD * S])
        q_lo = sb("q_lo", [128, KD * S])
        qd_hi = sb("qd_hi", [128, 2, KD, HG, S], F32R)
        qd_lo = sb("qd_lo", [128, 2, KD, HG, S], F32R)
        k_hi = sb("k_hi", [128, 2, KD, S2E], F32R)
        k_lo = sb("k_lo", [128, 2, KD, S2E], F32R)
        v_ext = sb("v_ext2", [KP, 2, 3, H2, HD2 + 1])
        masked = sb("masked", [S, 2, S2])
        row_max = sb("row_max2", [S, 2, 4])
        diag = sb("diag2", [S, 2, 4, S], F32R)
        probs = sb("probs2", [KP, 2, 3, 4 * S])
        recip = sb("recip2", [S, H2])
        o_norm = sb("o_norm2", [S, D])
        o_t = sb("o_t2", [128, KD * S])

        ps_p = [psum(f"psb_p{i}", [128, 512]) for i in range(2)]
        ps_s = [psum(f"psb_s{i}", [128, 512]) for i in range(2)]
        ps_t = [psum(f"psb_t{i}", [128, 512]) for i in range(2)]
        ps_o = psum("psb_o", [128, 512])
        ps_f = psum("psb_f", [128, 512])

        act_passed = sem("act_passed")
        dve_passed = sem("dve_passed")
        pool_passed = sem("pool_passed")
        w_loaded = sem("w2_loaded")
        w_hi_ready = sem("w2_hi_ready")
        w_lo_ready = sem("w2_lo_ready")
        mask_t_loaded = sem("mask_t_loaded")
        key_mask_cleared = sem("key_mask_cleared")
        key_mask_ready = sem("key_mask_ready")
        pad_ready = sem("pad_ready")
        ctx_loaded = [sem(f"ctx_loaded{p}") for p in range(2)]
        mask_loaded = [sem(f"mask_loaded{p}") for p in range(2)]
        mask_ready = sem("mask_ready")
        ones_ready = sem("ones2_ready")
        stats_ready = sem("stats2_ready")
        mv_ready = sem("mv2_ready")
        eps_added = sem("eps2_added")
        rstd_ready = sem("rstd2_ready")
        xn_ready = sem("xn2_ready")
        bo_added = sem("bo_added")
        filled = sem("filled2")
        drained_act = sem("drained2_act")
        drained_dve = sem("drained2_dve")
        q_rounded = sem("q_rounded")
        q_split = sem("q_split")
        qd_ready = sem("qd_ready")
        scores_ready = sem("scores2_ready")
        max_ready = sem("max2_ready")
        diag_ready = sem("diag2_ready")
        shifted_ready = sem("shifted2_ready")
        probs_ready = sem("probs2_ready")
        pv_ready = sem("pv2_ready")
        recip_ready = sem("recip2_ready")
        o_ready = sem("o2_ready")
        ot_ready = sem("ot2_ready")
        ot_copied = sem("ot2_copied")
        y_ready = sem("y2_ready")
        x2_ready = sem("x2_ready")

        C0, XT, Q0, K0, V0, FILLS = 0, 2, 3, 4, 6, 9
        ACT_OF = {0: 1, 1: 2, XT: 3, Q0: 4, K0: 5, K0 + 1: 6}
        DVE_OF = {0: 1, 1: 2, K0: 3, K0 + 1: 4, V0: 5, V0 + 1: 6, V0 + 2: 7}
        NA, ND = len(ACT_OF), len(DVE_OF)

        def bank(pp, f):
            return ps_p[(FILLS * pp + f) % 2]

        def bank_free(pe, pb, f):
            pb, f = (pb, f - 2) if f >= 2 else (pb - 1, f - 2 + FILLS)
            if f in DVE_OF:
                reach(pe, drained_dve, pb * ND + DVE_OF[f])
            else:
                reach(pe, drained_act, pb * NA + ACT_OF[f])

        block = ctx.enter_context(nc.Block())

        @block.sync
        def _(sp):
            for dst, src in ((wk_st, wk), (wv_st, wv), (wq_sb, wq), (wo_sb, wo)):
                sp.dma_start(dst[:], src.rearrange("(k p) n -> p k n", p=128)).then_inc(w_loaded, 16)
            sp.dma_start(bq_sb[:], bq).then_inc(w_loaded, 16)
            sp.dma_start(bk_sb[:], bk).then_inc(w_loaded, 16)
            sp.dma_start(bv_sb[:], bv.rearrange("(o n) -> o n", o=1).to_broadcast([KP, D])).then_inc(w_loaded, 16)
            sp.dma_start(bo_sb[:], bo.rearrange("(o n) -> o n", o=1).to_broadcast([S, D])).then_inc(w_loaded, 16)
            sp.wait_ge(key_mask_cleared, 1)
            for kt in range(3):
                sp.dma_start(mask_t[0:KT[kt], kt, :], maskT[KT0[kt]:KT0[kt] + KT[kt], :]).then_inc(mask_t_loaded, 16)

            def load(pb, p, _):
                reach(sp, filled, (pb - 2) * FILLS + 2)
                sp.dma_start(c_tok[:, p, 0:2, :], ctx_in[row(pb), 0:2 * KP, :].rearrange(
                    "(k r) d -> r k d" if isinstance(pb, int) else "b (k r) d -> r (b k) d",
                    r=KP)).then_inc(ctx_loaded[p], 16)
                last = ctx_in[row(pb), 2 * KP:S2, :]
                sp.dma_start(c_tok[0:KT[2], p, 2, :],
                             last if isinstance(pb, int) else last.rearrange("b r d -> (b r) d")
                             ).then_inc(ctx_loaded[p], 16)
                reach(sp, mask_ready, pb - 1)
                m = mask[row(pb), :]
                m = m.rearrange("(o n) -> o n", o=1) if isinstance(pb, int) else m
                sp.dma_start(mask_i[:, p, :], m.to_broadcast([S, S2])).then_inc(mask_loaded[p], 16)

            paired(sp, load)

        @block.gpsimd
        def _(pool):
            pool.memset(mask_t[:], 0).then_inc(key_mask_cleared, 1)
            pool.memset(c_hi[:, :, S2:S2E].bitcast(F32), 0.0).then_inc(pad_ready, 1)
            pool.memset(c_lo[:, :, S2:S2E].bitcast(F32), 0.0).then_inc(pad_ready, 1)
            pool.wait_ge(mask_t_loaded, 48)
            pool.wait_ge(w_loaded, 16 * 8)
            pool.tensor_scalar(key_bias[:], mask_t[:], 0.0, NEG, ALU.is_equal, ALU.mult).then_inc(key_mask_ready, 1)
            pool.wait_ge(key_mask_ready, 1)
            pool.tensor_scalar(key_live[:], key_bias[:], 0.0, None, ALU.is_equal).then_inc(key_mask_ready, 1)
            pool.wait_ge(key_mask_ready, 2)

            def ln_step(pb):
                pool.wait_ge(mv_ready, pb + 1)
                pool.sem_inc(pool_passed, 1)
                pool.tensor_scalar(var_eps[:], mv[:, 1:2], EPS, None, ALU.add).then_inc(eps_added, 1)
                pool.wait_ge(eps_added, pb + 1)
                pool.tensor_tensor(rstd[:], var_eps[:], c.minus_half[0:S, 0:1], ALU.pow).then_inc(rstd_ready, 1)

            def mask_step(pb, pp):
                pool.wait_ge(mask_loaded[pp], (pb - pp) * 8 + 16)
                pool.sem_inc(pool_passed, 1)
                pool.tensor_scalar(mask_f[:, pp], mask_i[:, pp], 0.0, NEG, ALU.is_equal,
                                   ALU.mult).then_inc(mask_ready, 1)
                live = (key_live[:, :, pb:pb + 1] if isinstance(pb, int) else key_live[:, :, bass.ds(pb, 1)])
                pool.tensor_copy(v_ext[:, pp, :, :, HD2:HD2 + 1].rearrange("p k h o -> p k (h o)"),
                                 live.to_broadcast([KP, 3, H2])).then_inc(ones_ready, 1)

            def bo_step(pb):
                pool.wait_ge(xn_ready, pb + 1)
                xb = at_batch(c.x, pb, slice(0, D))
                pool.tensor_tensor(xb, xb, bo_sb[:], ALU.add).then_inc(bo_added, 1)

            def place(pb, pp, g):
                pool.wait_ge(q_split, 2 * pb + 2)
                for src, dst in ((q_hi, qd_hi), (q_lo, qd_lo)):
                    pool.tensor_tensor(dst[:, pp, g], src[:, S * g:S * (g + 1)].unsqueeze(1).to_broadcast([128, HG, S]),
                                       c.head_of[:].unsqueeze(2).to_broadcast([128, HG, S]),
                                       ALU.mult).then_inc(qd_ready, 1)

            def diagonal(b, u):
                pool.wait_ge(max_ready, b * H2 + 4 * (u + 1))
                reach(pool, shifted_ready, b * 12 + 3 * (u - 1))
                pool.tensor_tensor(diag[:, u % 2], c.neg_ident[0:S, 0:S].unsqueeze(1).to_broadcast([S, 4, S]),
                                   row_max[:, u % 2].unsqueeze(2).to_broadcast([S, 4, S]),
                                   ALU.mult).then_inc(diag_ready, 1)

            ln_step(0)
            mask_step(0, 0)
            bo_step(0)
            place(0, 0, 0)
            place(0, 0, 1)
            diagonal(0, 0)

            def step(b, p, last):
                if not last:
                    ln_step(b + 1)
                diagonal(b, 1)
                if not last:
                    bo_step(b + 1)
                diagonal(b, 2)
                if not last:
                    place(b + 1, 1 - p, 0)
                diagonal(b, 3)
                if not last:
                    mask_step(b + 1, 1 - p)
                    place(b + 1, 1 - p, 1)
                    diagonal(b + 1, 0)

            paired(pool, step)

        @block.scalar
        def _(act):
            act.wait_ge(w_loaded, 16 * 8)
            act.copy(wk_hi[:], wk_st[:]).then_inc(w_hi_ready, 1)
            act.copy(wv_hi[:], wv_st[:]).then_inc(w_hi_ready, 1)
            act.wait_ge(key_mask_ready, 2)

            def context(pb, pp):
                for k in range(KD):
                    act.wait_ge(filled, pb * FILLS + (k + 1))
                    act.copy(c_hi[:, k, 0:S2], bank(pp, k)[:, 0:S2]).then_inc(drained_act, 1)

            def queries(pb, pp):
                act.wait_ge(filled, pb * FILLS + (XT + 1))
                act.copy(x_t[:], bank(pp, XT)[:, 0:KD * S]).then_inc(drained_act, 1)
                act.wait_ge(filled, pb * FILLS + (Q0 + 1))
                reach(act, q_split, 2 * pb)
                for g in range(KD):
                    ins = act.activation(q_b[:, S * g:S * (g + 1)], bank(pp, Q0)[:, S * g:S * (g + 1)], ACT.Identity,
                                         bias=bq_sb[:, g:g + 1])
                ins.then_inc(drained_act, 1)

            def keys(pb, pp):
                for g in range(KD):
                    act.wait_ge(filled, pb * FILLS + (K0 + g + 1))
                    act.activation(k_hi[:, pp, g], bank(pp, K0 + g)[:, 0:S2E], ACT.Identity,
                                   bias=bk_sb[:, g:g + 1]).then_inc(drained_act, 1)

            def exps(b, u):
                reach(act, pv_ready, b * 4 + (u - 1))
                for kt in range(3):
                    i = 3 * u + kt
                    act.wait_ge(shifted_ready, b * 12 + (i + 1))
                    act.sem_inc(act_passed, 1)
                    bias = key_bias[0:KT[kt], kt, b:b + 1] if isinstance(b, int) else key_bias[0:KT[kt], kt, bass.ds(b, 1)]
                    act.activation(probs[0:KT[kt], u % 2, kt], ps_t[i % 2][0:KT[kt], 0:4 * S], ACT.Exp,
                                   bias=bias, scale=HD2 ** -0.5).then_inc(probs_ready, 1)

            context(0, 0)
            queries(0, 0)
            keys(0, 0)

            def step(b, p, last):
                exps(b, 0)
                if not last:
                    context(b + 1, 1 - p)
                exps(b, 1)
                if not last:
                    queries(b + 1, 1 - p)
                exps(b, 2)
                if not last:
                    keys(b + 1, 1 - p)
                exps(b, 3)
                act.wait_ge(ot_ready, b + 1)
                act.copy(o_t[:], ps_f[:, 0:KD * S]).then_inc(ot_copied, 1)

            paired(act, step)

        @block.vector
        def _(dve):
            for j, (hi, lo, st) in enumerate(((wk_hi, wk_lo, wk_st), (wv_hi, wv_lo, wv_st))):
                dve.wait_ge(w_hi_ready, j + 1)
                dve.tensor_tensor(lo[:], st[:], hi[:].bitcast(F32), ALU.subtract).then_inc(w_lo_ready, 1)

            def norm_stats(pb):
                dve.bn_stats(stats[:], at_batch(c.x, pb, slice(0, D))).then_inc(stats_ready, 1)
                dve.wait_ge(stats_ready, pb + 1)
                dve.sem_inc(dve_passed, 1)
                dve.bn_aggr(mv[:], stats[:]).then_inc(mv_ready, 1)

            def normalize(pb):
                dve.wait_ge(rstd_ready, pb + 1)
                dve.tensor_scalar(xn[:], at_batch(c.x, pb, slice(0, D)), mv[:, 0:1], rstd[:], ALU.subtract,
                                  ALU.mult).then_inc(xn_ready, 1)

            def context(pb, pp):
                for k in range(KD):
                    dve.wait_ge(drained_act, pb * NA + ACT_OF[k])
                    dve.tensor_tensor(c_lo[:, k, 0:S2], bank(pp, k)[:, 0:S2], c_hi[:, k, 0:S2].bitcast(F32),
                                      ALU.subtract).then_inc(drained_dve, 1)

            def queries(pb, pp):
                dve.wait_ge(drained_act, pb * NA + ACT_OF[Q0])
                reach(dve, qd_ready, 4 * pb)
                dve.tensor_copy(q_hi[:].bitcast(F32R), q_b[:]).then_inc(q_split, 1)
                dve.wait_ge(q_split, 2 * pb + 1)
                dve.tensor_tensor(q_lo[:], q_b[:], q_hi[:], ALU.subtract).then_inc(q_split, 1)

            def keys(pb, pp):
                for g in range(KD):
                    dve.wait_ge(drained_act, pb * NA + ACT_OF[K0 + g])
                    dve.scalar_tensor_tensor(out=k_lo[:, pp, g], in0=bank(pp, K0 + g)[:, 0:S2E],
                                             scalar=bk_sb[:, g:g + 1], in1=k_hi[:, pp, g].bitcast(F32),
                                             op0=ALU.add, op1=ALU.subtract).then_inc(drained_dve, 1)

            def values(pb, pp):
                for kt in range(3):
                    dve.wait_ge(filled, pb * FILLS + (V0 + kt + 1))
                    n = KT[kt]
                    dve.tensor_tensor(v_ext[0:n, pp, kt, :, 0:HD2],
                                      bank(pp, V0 + kt)[0:n, 0:D].rearrange("p (h d) -> p h d", h=H2),
                                      bv_sb[0:n, :].rearrange("p (h d) -> p h d", h=H2),
                                      ALU.add).then_inc(drained_dve, 1)

            def maxima(b, p, u):
                if u == 0:
                    dve.wait_ge(mask_ready, b + 1)
                reach(dve, diag_ready, b * 4 + (u - 1))
                for h in range(4 * u, 4 * u + 4):
                    dve.wait_ge(scores_ready, b * H2 + (h + 1))
                    dve.sem_inc(dve_passed, 1)
                    dve.tensor_tensor_reduce(masked[:, h % 2], ps_s[h % 2][0:S, 0:S2], mask_f[:, p], 1.0, -3.0e38,
                                             ALU.add, ALU.max, row_max[:, u % 2, h % 4:h % 4 + 1]).then_inc(max_ready, 1)

            dve.wait_ge(w_lo_ready, 2)
            norm_stats(0)
            normalize(0)
            context(0, 0)
            queries(0, 0)
            keys(0, 0)
            values(0, 0)
            maxima(0, 0, 0)

            def step(b, p, last):
                if not last:
                    norm_stats(b + 1)
                maxima(b, p, 1)
                if not last:
                    normalize(b + 1)
                    context(b + 1, 1 - p)
                maxima(b, p, 2)
                if not last:
                    queries(b + 1, 1 - p)
                maxima(b, p, 3)
                if not last:
                    keys(b + 1, 1 - p)
                    values(b + 1, 1 - p)
                o = ps_o[0:S, 0:H2 * (HD2 + 1)].rearrange("p (h d) -> p h d", h=H2)
                dve.wait_ge(pv_ready, b * 4 + 4)
                dve.reciprocal(recip[:], o[:, :, HD2]).then_inc(recip_ready, 1)
                dve.wait_ge(recip_ready, b + 1)
                reach(dve, ot_ready, b)
                dve.tensor_tensor(o_norm[:].rearrange("p (h d) -> p h d", h=H2), o[:, :, 0:HD2],
                                  recip[:].unsqueeze(2).to_broadcast([S, H2, HD2]), ALU.mult).then_inc(o_ready, 1)
                if not last:
                    maxima(b + 1, 1 - p, 0)
                dve.wait_ge(y_ready, b + 1)
                dve.wait_ge(bo_added, b + 1)
                xb = at_batch(c.x, b, slice(0, D))
                dve.tensor_tensor(xb, ps_f[0:S, 0:D], xb, ALU.add).then_inc(x2_ready, 1)

            paired(dve, step)

        @block.tensor
        def _(pe):
            pe.wait_ge(w_loaded, 16 * 8)
            pe.wait_ge(w_hi_ready, 2)
            pe.wait_ge(w_lo_ready, 2)
            pe.wait_ge(pad_ready, 2)

            def context(pb, pp):
                reach(pe, ctx_loaded[pp], (pb - pp) * 16 + 32)
                for k in range(KD):
                    bank_free(pe, pb, C0 + k)
                    for kt in range(3):
                        ins = pe.transpose(bank(pp, k)[:, KT0[kt]:KT0[kt] + KT[kt]],
                                           c_tok[0:KT[kt], pp, kt, 128 * k:128 * (k + 1)],
                                           c.ident[0:KT[kt], 0:KT[kt]])
                    ins.then_inc(filled, 1)

            def queries(pb, pp):
                bank_free(pe, pb, XT)
                pe.wait_ge(xn_ready, pb + 1)
                for k in range(KD):
                    ins = pe.transpose(bank(pp, XT)[:, S * k:S * (k + 1)], xn[:, 128 * k:128 * (k + 1)],
                                       c.ident[0:S, 0:S])
                ins.then_inc(filled, 1)
                bank_free(pe, pb, Q0)
                pe.wait_ge(drained_act, pb * NA + ACT_OF[XT])
                for g in range(KD):
                    for k in range(KD):
                        ins = pe.matmul(bank(pp, Q0)[:, S * g:S * (g + 1)], wq_sb[:, k, 128 * g:128 * (g + 1)],
                                        x_t[:, S * k:S * (k + 1)], start=(k == 0), stop=(k == KD - 1))
                ins.then_inc(filled, 1)

            def keys(pb, pp):
                pe.wait_ge(drained_dve, pb * ND + DVE_OF[1])
                for g in range(KD):
                    bank_free(pe, pb, K0 + g)
                    for k in range(KD):
                        cols = slice(128 * g, 128 * (g + 1))
                        ins = split3(pe, bank(pp, K0 + g)[:, 0:S2E], wk_hi[:, k, cols], wk_lo[:, k, cols],
                                     c_hi[:, k], c_lo[:, k], k == 0, k == KD - 1)
                    ins.then_inc(filled, 1)

            def values(pb, pp):
                for kt in range(3):
                    bank_free(pe, pb, V0 + kt)
                    rows = slice(KT0[kt], KT0[kt] + KT[kt])
                    for k in range(KD):
                        ins = split3(pe, bank(pp, V0 + kt)[0:KT[kt], 0:D], c_hi[:, k, rows], c_lo[:, k, rows],
                                     wv_hi[:, k], wv_lo[:, k], k == 0, k == KD - 1)
                    ins.then_inc(filled, 1)

            def scores(b, p, u):
                if u == 0:
                    pe.wait_ge(drained_act, b * NA + ACT_OF[K0 + 1])
                if u % 2 == 0:
                    pe.wait_ge(qd_ready, 4 * b + u + 2)
                for h in range(4 * u, 4 * u + 4):
                    reach(pe, max_ready, b * H2 + (h - 1))
                    pe.matmul(ps_s[h % 2][0:S, 0:S2E], qd_hi[:, p, h // HG, h % HG, :], k_hi[:, p, h // HG],
                              start=True, stop=True).then_inc(scores_ready, 1)

            def shifted(b, p, u):
                if u == 0:
                    pe.wait_ge(drained_dve, b * ND + DVE_OF[K0 + 1])
                g, heads = u // 2, slice(4 * (u % 2), 4 * (u % 2) + 4)
                for kt in range(3):
                    i, n = 3 * u + kt, KT[kt]
                    reach(pe, probs_ready, b * 12 + (i - 1))
                    rows = slice(KT0[kt], KT0[kt] + n)
                    out = ps_t[i % 2][0:n, 0:4 * S]
                    split3(pe, out, k_hi[:, p, g, rows], k_lo[:, p, g, rows],
                           qd_hi[:, p, g, heads].rearrange("p h s -> p (h s)"),
                           qd_lo[:, p, g, heads].rearrange("p h s -> p (h s)"), True, False)
                    if kt == 0:
                        pe.wait_ge(diag_ready, b * 4 + (u + 1))
                    pe.matmul(out, c.ones_r[0:S, 0:n], diag[:, u % 2].rearrange("p h s -> p (h s)"),
                              start=False, stop=True).then_inc(shifted_ready, 1)

            def weighted(b, p, u):
                if u == 0:
                    reach(pe, o_ready, b)
                    pe.wait_ge(drained_dve, b * ND + ND)
                    pe.wait_ge(ones_ready, b + 1)
                pe.wait_ge(probs_ready, b * 12 + (3 * u + 3))
                for h in range(4):
                    hh = 4 * u + h
                    for kt in range(3):
                        n = KT[kt]
                        ins = pe.matmul(ps_o[0:S, (HD2 + 1) * hh:(HD2 + 1) * (hh + 1)],
                                        probs[0:n, u % 2, kt, S * h:S * (h + 1)], v_ext[0:n, p, kt, hh, :],
                                        start=(kt == 0), stop=(kt == 2))
                ins.then_inc(pv_ready, 1)

            context(0, 0)
            queries(0, 0)
            keys(0, 0)
            values(0, 0)
            scores(0, 0, 0)

            def step(b, p, last):
                shifted(b, p, 0)
                scores(b, p, 1)
                if not last:
                    context(b + 1, 1 - p)
                shifted(b, p, 1)
                weighted(b, p, 0)
                scores(b, p, 2)
                if not last:
                    queries(b + 1, 1 - p)
                shifted(b, p, 2)
                weighted(b, p, 1)
                scores(b, p, 3)
                if not last:
                    keys(b + 1, 1 - p)
                shifted(b, p, 3)
                weighted(b, p, 2)
                if not last:
                    values(b + 1, 1 - p)
                weighted(b, p, 3)
                if not last:
                    scores(b + 1, 1 - p, 0)
                pe.wait_ge(o_ready, b + 1)
                reach(pe, x2_ready, b)
                for k in range(KD):
                    ins = pe.transpose(ps_f[:, S * k:S * (k + 1)], o_norm[:, 128 * k:128 * (k + 1)],
                                       c.ident[0:S, 0:S])
                ins.then_inc(ot_ready, 1)
                pe.wait_ge(ot_copied, b + 1)
                for k in range(KD):
                    ins = pe.matmul(ps_f[0:S, 0:D], o_t[:, S * k:S * (k + 1)], wo_sb[:, k, :],
                                    start=(k == 0), stop=(k == KD - 1))
                ins.then_inc(y_ready, 1)

            paired(pe, step)


def route(nc, c, centT, xs):
    with ExitStack() as ctx:
        def sb(name, shape, dt=F32):
            return ctx.enter_context(nc.sbuf_tensor(name, shape, dt))

        def psum(name, shape, dt=F32):
            return ctx.enter_context(nc.psum_tensor(name, shape, dt))

        def sem(name):
            return ctx.enter_context(nc.semaphore(name))

        MAXT = (B * S + T - 1) // T
        cent = sb("cent", [128, KD, E])
        stats = sb("stats3", [S, B, 6])
        mv = sb("mv3", [S, B, 2])
        var_eps = sb("var_eps3", [S, B])
        rstd = sb("rstd3", [S, B])
        feats = sb("feats3", [S, 2, QUAD, D])
        f_t = sb("f_t3", [128, 2, KD, QT_TOK])
        aff = sb("aff", [S, B, E])
        top = sb("top", [S, B])
        best = sb("best", [S, B, E])
        onehot = sb("onehot", [S, B, E])
        first_w = sb("first_w", [S, E])
        nan_w = sb("nan_w", [S, E])
        steps = sb("steps", [S, MAXT])
        tile_no = sb("tile_no", [1, TILES + 1])
        scan = [sb(f"scan{i}", [S, B, E]) for i in range(2)]
        totals = sb("totals", [S, B, E])
        more = sb("more", [S, E, MAXT])
        n_tiles = sb("n_tiles", [S, E])
        ends = [sb(f"ends{i}", [S, E]) for i in range(2)]
        start = sb("start", [S, E])
        pos = sb("pos", [S, B, E])
        slot_f = sb("slot_f", [S, B])
        slot = sb("slot", [S, B], U32)
        past = sb("past", [1, TILES + 1, E])
        expert_f = sb("expert_f", [1, TILES + 1])

        ps_x = [psum(f"psc_x{i}", [128, 512]) for i in range(4)]
        ps_a = [psum(f"psc_a{i}", [128, 512]) for i in range(2)]
        ps_b = psum("psc_b", [128, 512])
        ps_n = psum("psc_n", [128, 512])

        cent_loaded = sem("cent_loaded")
        tables_ready = sem("tables_ready")
        stats_ready = sem("stats3_ready")
        mv_ready = sem("mv3_ready")
        eps_added = sem("eps3_added")
        rstd_ready = sem("rstd3_ready")
        feats_ready = sem("feats3_ready")
        turned = sem("turned3")
        copied = sem("copied3")
        aff_ready = sem("aff_ready")
        aff_copied = sem("aff_copied")
        chain = sem("route_chain")
        onehot_ready = sem("onehot_ready")
        before_ready = sem("before_ready")
        slot_ready = sem("slot_ready")
        routed = sem("routed")

        block = ctx.enter_context(nc.Block())

        @block.sync
        def _(sp):
            sp.dma_start(cent[:], centT.rearrange("(k p) e -> p k e", p=128)).then_inc(cent_loaded, 16)

        @block.gpsimd
        def _(pool):
            pool.iota(c.x[:, :, D:ROWW].rearrange("s b o -> s (b o)"), pattern=[[S, B]], base=0, channel_multiplier=1,
                      allow_small_or_imprecise_dtypes=True).then_inc(tables_ready, 1)
            pool.iota(first_w[:], pattern=[[-1, E]], base=E, channel_multiplier=0,
                      allow_small_or_imprecise_dtypes=True).then_inc(tables_ready, 1)
            pool.memset(nan_w[:, 0:1], 0.5).then_inc(tables_ready, 1)
            pool.memset(nan_w[:, 1:E], 0.0).then_inc(tables_ready, 1)
            pool.iota(steps[:], pattern=[[T, MAXT]], base=0, channel_multiplier=0,
                      allow_small_or_imprecise_dtypes=True).then_inc(tables_ready, 1)
            pool.iota(tile_no[:], pattern=[[1, TILES + 1]], base=0, channel_multiplier=0,
                      allow_small_or_imprecise_dtypes=True).then_inc(tables_ready, 1)
            pool.wait_ge(mv_ready, B)
            pool.tensor_scalar(var_eps[:], mv[:, :, 1], EPS, None, ALU.add).then_inc(eps_added, 1)
            pool.wait_ge(eps_added, 1)
            pool.tensor_tensor(rstd[:], var_eps[:], c.minus_half[0:S, :], ALU.pow).then_inc(rstd_ready, 1)
            pool.wait_ge(slot_ready, 1)
            pool.wait_ge(c.xs_cleared, 16)
            pool.wait_ge(tables_ready, 1)
            for b in range(B):
                pool.indirect_dma_start(out=xs, out_offset=bass.IndirectOffsetOnAxis(ap=slot[:, b:b + 1], axis=0),
                                        in_=c.x[:, b, :], in_offset=None).then_inc(routed, 16)
            pool.wait_ge(routed, 16 * B)

        @block.scalar
        def _(act):
            for q in range(QUADS):
                act.wait_ge(turned, q + 1)
                if q >= 2:
                    act.wait_ge(aff_ready, q - 1)
                for k in range(KD):
                    ins = act.copy(f_t[:, q % 2, k], ps_x[2 * (q % 2) + k][:, 0:QT_TOK])
                ins.then_inc(copied, 1)

        @block.tensor
        def _(pe):
            def turn(q):
                pe.wait_ge(feats_ready, q + 1)
                if q >= 2:
                    pe.wait_ge(copied, q - 1)
                for k in range(KD):
                    for i in range(QUAD):
                        ins = pe.transpose(ps_x[2 * (q % 2) + k][:, S * i:S * (i + 1)],
                                           feats[:, q % 2, i, 128 * k:128 * (k + 1)], c.ident[0:S, 0:S])
                ins.then_inc(turned, 1)

            def affinity(q):
                pe.wait_ge(copied, q + 1)
                if q >= 2:
                    pe.wait_ge(aff_copied, q - 1)
                for i in range(QUAD):
                    for k in range(KD):
                        ins = pe.matmul(ps_a[q % 2][0:S, E * i:E * (i + 1)], f_t[:, q % 2, k, S * i:S * (i + 1)],
                                        cent[:, k, :], start=(k == 0), stop=(k == KD - 1))
                ins.then_inc(aff_ready, 1)

            pe.wait_ge(cent_loaded, 16)
            turn(0)
            for q in range(QUADS):
                if q + 1 < QUADS:
                    turn(q + 1)
                affinity(q)
            pe.wait_ge(onehot_ready, 1)
            one = onehot[:].rearrange("s b e -> s (b e)")
            pe.matmul(ps_b[0:S, 0:B * E], c.before[:], one, start=True, stop=True)
            pe.matmul(ps_n[0:S, 0:B * E], c.ones_f[0:S, 0:S], one, start=True, stop=True).then_inc(before_ready, 1)

        @block.vector
        def _(dve):
            for b in range(B):
                dve.bn_stats(stats[:, b], c.x[:, b, 0:D]).then_inc(stats_ready, 1)
            for b in range(B):
                dve.wait_ge(stats_ready, b + 1)
                dve.bn_aggr(mv[:, b], stats[:, b]).then_inc(mv_ready, 1)
            dve.wait_ge(rstd_ready, 1)
            def collect(q):
                dve.wait_ge(aff_ready, q + 1)
                dve.tensor_copy(aff[:, QUAD * q:QUAD * (q + 1)],
                                ps_a[q % 2][0:S, 0:QUAD * E].rearrange("p (b e) -> p b e", e=E)).then_inc(aff_copied, 1)

            for q in range(QUADS):
                if q >= 2:
                    dve.wait_ge(turned, q - 1)
                for i in range(QUAD):
                    b = QUAD * q + i
                    ins = dve.tensor_scalar(feats[:, q % 2, i], c.x[:, b, 0:D], mv[:, b, 0:1], rstd[:, b:b + 1],
                                            ALU.subtract, ALU.mult)
                ins.then_inc(feats_ready, 1)
                if q >= 1:
                    collect(q - 1)
            collect(QUADS - 1)

            n = [0]

            def link(ins):
                n[0] += 1
                ins.then_inc(chain, 1)
                dve.wait_ge(chain, n[0])

            def over_e(t):
                return t.unsqueeze(2).to_broadcast([S, B, E])

            def over_b(t):
                return t.unsqueeze(1).to_broadcast([S, B, E])

            dve.wait_ge(aff_copied, QUADS)
            dve.wait_ge(tables_ready, 6)
            link(dve.tensor_reduce(top[:], aff[:], AX_X, ALU.max))
            link(dve.tensor_tensor(best[:], aff[:], over_e(top[:]), ALU.is_ge))
            link(dve.tensor_tensor(best[:], best[:], over_b(first_w[:]), ALU.mult))
            link(dve.tensor_tensor(best[:], best[:], over_b(nan_w[:]), ALU.add))
            link(dve.tensor_reduce(top[:], best[:], AX_X, ALU.max))
            dve.tensor_tensor(onehot[:], best[:], over_e(top[:]), ALU.is_equal).then_inc(onehot_ready, 1)
            dve.wait_ge(before_ready, 1)
            link(dve.tensor_copy(totals[:], ps_n[0:S, 0:B * E].rearrange("p (b e) -> p b e", e=E)))
            src, step, k = totals, 1, 0
            while step < B:
                dst = scan[k % 2]
                dve.tensor_copy(dst[:, 0:step], src[:, 0:step])
                link(dve.tensor_tensor(dst[:, step:B], src[:, step:B], src[:, 0:B - step], ALU.add))
                src, step, k = dst, 2 * step, k + 1
            link(dve.tensor_tensor(more[:], src[:, B - 1].unsqueeze(2).to_broadcast([S, E, MAXT]),
                                   steps[:].unsqueeze(1).to_broadcast([S, E, MAXT]), ALU.is_gt))
            link(dve.tensor_reduce(n_tiles[:], more[:], AX_X, ALU.add))
            end, step, j = n_tiles, 1, 0
            while step < E:
                dst = ends[j % 2]
                dve.tensor_copy(dst[:, 0:step], end[:, 0:step])
                link(dve.tensor_tensor(dst[:, step:E], end[:, step:E], end[:, 0:E - step], ALU.add))
                end, step, j = dst, 2 * step, j + 1
            link(dve.tensor_tensor(start[:], end[:], n_tiles[:], ALU.subtract))
            link(dve.tensor_scalar(start[:], start[:], float(T), None, ALU.mult))
            link(dve.tensor_tensor(pos[:], src[:], totals[:], ALU.subtract))
            link(dve.tensor_tensor(pos[:], ps_b[0:S, 0:B * E].rearrange("p (b e) -> p b e", e=E), pos[:], ALU.add))
            link(dve.tensor_tensor(pos[:], pos[:], over_b(start[:]), ALU.add))
            link(dve.tensor_tensor(pos[:], pos[:], onehot[:], ALU.mult))
            link(dve.tensor_reduce(slot_f[:], pos[:], AX_X, ALU.add))
            dve.tensor_copy(slot[:], slot_f[:]).then_inc(slot_ready, 1)
            link(dve.tensor_tensor(past[:], end[0:1].unsqueeze(1).to_broadcast([1, TILES + 1, E]),
                                   tile_no[:].unsqueeze(2).to_broadcast([1, TILES + 1, E]), ALU.is_le))
            link(dve.tensor_reduce(expert_f[:], past[:], AX_X, ALU.add))
            link(dve.tensor_scalar(expert_f[:], expert_f[:], float(E - 1), None, ALU.min))
            dve.tensor_copy(c.tile_expert[:], expert_f[:])


def experts(nc, c, xs, w1, w2, gamma, beta, b1, b2, centroids, out):
    with ExitStack() as ctx:
        def sb(name, shape, dt=F32):
            return ctx.enter_context(nc.sbuf_tensor(name, shape, dt))

        def psum(name, shape, dt=F32):
            return ctx.enter_context(nc.psum_tensor(name, shape, dt))

        def sem(name):
            return ctx.enter_context(nc.semaphore(name))

        NH = T // 128
        w1_sb = sb("w1_sb", [128, 2, KD, F])
        w2_sb = sb("w2_sb", [128, 2, NF, D])
        gam = sb("gam", [128, KD, E])
        bet = sb("bet", [128, KD, E])
        b1_sb = sb("b1_sb", [128, NF, E])
        b2_sb = sb("b2_sb", [128, E, D])
        cen = sb("cen", [128, E, D])
        rows = sb("rows", [128, 2, NH, ROWW])
        stats = sb("stats4", [128, NH, 6])
        mv = sb("mv4", [128, NH, 2])
        var_eps = sb("var_eps4", [128, NH])
        rstd = sb("rstd4", [128, NH])
        feats = sb("feats4", [128, NH, D])
        xhat = sb("xhat", [128, NH, D])
        prod = sb("prod", [128, NH, D])
        z = sb("z", [128, NH])
        ez = sb("ez", [128, NH])
        alpha = sb("alpha", [128, 2, NH])
        xf = sb("xf", [128, 2, NH, D])
        token = sb("token", [128, 2, NH], U32)
        h_in = sb("h_in", [128, 2, KD, T])
        hid = sb("hid", [128, NF, T])
        y = sb("y", [128, NH, D])
        res = sb("res", [128, 2, NH, D])

        ps_x = psum("psd_x", [128, KD * T])
        ps_h = [psum(f"psd_h{i}", [128, 512]) for i in range(4)]
        ps_y = [psum(f"psd_y{i}", [128, 512]) for i in range(NH)]

        act_passed = sem("act_passed4")
        dve_passed = sem("dve_passed4")
        pool_passed = sem("pool_passed4")
        tables = sem("tables4")
        w_loaded = [sem(f"w4_loaded{p}") for p in range(2)]
        rows_loaded = [sem(f"rows4_loaded{p}") for p in range(2)]
        stats_ready = sem("stats4_ready")
        mv_ready = sem("mv4_ready")
        eps_added = sem("eps4_added")
        rstd_ready = sem("rstd4_ready")
        feats_ready = sem("feats4_ready")
        xhat_ready = sem("xhat_ready")
        prod_ready = sem("prod_ready")
        z_ready = sem("z_ready")
        ez_ready = sem("ez_ready")
        alpha_step = sem("alpha_step")
        xf_ready = sem("xf_ready")
        token_ready = sem("token_ready")
        turned = sem("turned4")
        h_in_ready = sem("h_in_ready")
        hid_filled = sem("hid_filled")
        hid_act = sem("hid_act")
        hid_dve = sem("hid_dve")
        y_filled = sem("y_filled")
        y_ready = sem("y4_ready")
        res_ready = sem("res_ready")
        scattered = [sem(f"scattered{p}") for p in range(2)]

        def over_tiles(eng, emit):
            emit(0, 0, False)
            emit(1, 1, False)
            with eng.Fori(1, TILES // 2 - 1) as i:
                emit(i * 2, 0, False)
                emit(i * 2 + 1, 1, False)
            emit(TILES - 2, 0, False)
            emit(TILES - 1, 1, True)

        def expert_of(eng, j):
            return eng.value_load(c.tile_expert[0:1, j:j + 1] if isinstance(j, int)
                                  else c.tile_expert[0:1, bass.ds(j, 1)], min_val=0, max_val=E - 1)

        block = ctx.enter_context(nc.Block())

        @block.sync
        def _(sp):
            def load_rows(j, p):
                reach(sp, xf_ready, j - 1)
                reach(sp, token_ready, j - 1)
                src = xs[j * T:(j + 1) * T, :] if isinstance(j, int) else xs[bass.ds(j * T, T), :]
                sp.dma_start(rows[:, p], src.rearrange("(t r) d -> r t d", r=128)).then_inc(rows_loaded[p], 16)

            load_rows(0, 0)
            sp.dma_start(gam[:], gamma).then_inc(tables, 16)
            sp.dma_start(bet[:], beta).then_inc(tables, 16)
            sp.dma_start(b1_sb[:], b1).then_inc(tables, 16)
            sp.dma_start(cen[:], centroids.rearrange("(o e) d -> o e d", o=1).to_broadcast([128, E, D])
                         ).then_inc(tables, 16)
            sp.dma_start(b2_sb[:], b2.rearrange("(o e) d -> o e d", o=1).to_broadcast([128, E, D])
                         ).then_inc(tables, 16)

            def load(j, p, last):
                e = expert_of(sp, j)
                reach(sp, y_filled, NH * (j - 1))
                sp.dma_start(w1_sb[:, p], w1[bass.ds(e, 1)].rearrange("o (k p) n -> p (o k) n", p=128)
                             ).then_inc(w_loaded[p], 16)
                sp.dma_start(w2_sb[:, p], w2[bass.ds(e, 1)].rearrange("o (k p) n -> p (o k) n", p=128)
                             ).then_inc(w_loaded[p], 16)
                if not last:
                    load_rows(j + 1, 1 - p)

            over_tiles(sp, load)

        @block.gpsimd
        def _(pool):
            def inverse_root(n):
                pool.wait_ge(mv_ready, n * NH + NH)
                pool.sem_inc(pool_passed, 1)
                pool.tensor_scalar(var_eps[:], mv[:, :, 1], EPS, None, ALU.add).then_inc(eps_added, 1)
                pool.wait_ge(eps_added, n + 1)
                pool.tensor_tensor(rstd[:], var_eps[:], c.minus_half[:, 0:NH], ALU.pow).then_inc(rstd_ready, 1)

            def prepare(j, p):
                inverse_root(j * 2)
                pool.wait_ge(feats_ready, j + 1)
                reach(pool, res_ready, NH * (j - 1))
                pool.tensor_tensor(xf[:, p], rows[:, p, :, 0:D], feats[:], ALU.add).then_inc(xf_ready, 1)
                inverse_root(j * 2 + 1)

            def finish(j, p):
                for t in range(NH):
                    pool.wait_ge(res_ready, NH * j + (t + 1))
                    pool.sem_inc(pool_passed, 1)
                    pool.indirect_dma_start(
                        out=out, out_offset=bass.IndirectOffsetOnAxis(ap=token[:, p, t:t + 1], axis=0),
                        in_=res[:, p, t, :], in_offset=None, bounds_check=B * S - 1,
                        oob_is_err=False).then_inc(scattered[p], 16)

            prepare(0, 0)

            def step(j, p, last):
                if not last:
                    prepare(j + 1, 1 - p)
                finish(j, p)

            over_tiles(pool, step)
            for p in range(2):
                pool.wait_ge(scattered[p], 16 * NH * (TILES // 2))

        @block.scalar
        def _(act):
            act.wait_ge(tables, 16 * 5)

            def prepare(j, p):
                e = expert_of(act, j)
                act.wait_ge(turned, j + 1)
                act.sem_inc(act_passed, 1)
                for k in range(KD):
                    ins = act.activation(h_in[:, p, k], ps_x[:, T * k:T * (k + 1)], ACT.Identity,
                                         bias=bet[:, k, bass.ds(e, 1)], scale=gam[:, k, bass.ds(e, 1)])
                ins.then_inc(h_in_ready, 1)
                act.wait_ge(z_ready, j + 1)
                act.activation(ez[:], z[:], ACT.Exp, scale=-1.0).then_inc(ez_ready, 1)

            prepare(0, 0)

            def step(j, p, last):
                e = expert_of(act, j)
                for f in range(0, NF, 2):
                    act.wait_ge(hid_filled, NF * j + (f + 1))
                    if f == 0:
                        reach(act, y_filled, NH * j)
                    act.sem_inc(act_passed, 1)
                    act.activation(hid[:, f], ps_h[f % 4][:, 0:T], ACT.Relu,
                                   bias=b1_sb[:, f, bass.ds(e, 1)]).then_inc(hid_act, 1)
                if not last:
                    prepare(j + 1, 1 - p)

            over_tiles(act, step)

        @block.vector
        def _(dve):
            dve.wait_ge(tables, 16 * 5)

            def moments(n, src):
                for t in range(NH):
                    dve.bn_stats(stats[:, t], src[:, t, 0:D]).then_inc(stats_ready, 1)
                dve.wait_ge(stats_ready, n * NH + NH)
                dve.sem_inc(dve_passed, 1)
                for t in range(NH):
                    dve.bn_aggr(mv[:, t], stats[:, t]).then_inc(mv_ready, 1)

            def normalize(n, dst, src, ready):
                dve.wait_ge(rstd_ready, n + 1)
                for t in range(NH):
                    ins = dve.tensor_scalar(dst[:, t], src[:, t, 0:D], mv[:, t, 0:1], rstd[:, t:t + 1], ALU.subtract,
                                            ALU.mult)
                ins.then_inc(ready, 1)

            def features(j, p):
                dve.wait_ge(rows_loaded[p], (j - p) * 8 + 16)
                reach(dve, xf_ready, j)
                moments(j * 2, rows[:, p])

            def again(j, p):
                normalize(j * 2, feats, rows[:, p], feats_ready)
                dve.wait_ge(feats_ready, j + 1)
                dve.sem_inc(dve_passed, 1)
                moments(j * 2 + 1, feats)

            def gate(j, p):
                reach(dve, turned, j)
                normalize(j * 2 + 1, xhat, feats, xhat_ready)
                e = expert_of(dve, j)
                reach(dve, ez_ready, j)
                dve.tensor_tensor(prod[:], feats[:], cen[:, bass.ds(e, 1), :].to_broadcast([128, NH, D]),
                                  ALU.mult).then_inc(prod_ready, 1)
                dve.wait_ge(prod_ready, j + 1)
                dve.tensor_reduce(z[:], prod[:], AX_X, ALU.add).then_inc(z_ready, 1)
                reach(dve, res_ready, NH * (j - 1))
                dve.wait_ge(rows_loaded[p], (j - p) * 8 + 16)
                reach(dve, scattered[p], (j - p) * 16)
                dve.tensor_copy(token[:, p], rows[:, p, :, D]).then_inc(token_ready, 1)
                dve.wait_ge(ez_ready, j + 1)
                dve.tensor_scalar(ez[:], ez[:], 1.0, None, ALU.add).then_inc(alpha_step, 1)
                dve.wait_ge(alpha_step, 2 * j + 1)
                dve.reciprocal(alpha[:, p], ez[:]).then_inc(alpha_step, 1)

            features(0, 0)
            again(0, 0)
            gate(0, 0)

            def step(j, p, last):
                if not last:
                    features(j + 1, 1 - p)
                e = expert_of(dve, j)
                for f in range(1, NF, 2):
                    dve.wait_ge(hid_filled, NF * j + (f + 1))
                    if f == 1:
                        reach(dve, y_filled, NH * j)
                    dve.tensor_scalar(hid[:, f], ps_h[f % 4][:, 0:T], b1_sb[:, f, bass.ds(e, 1)], 0.0, ALU.add,
                                      ALU.max).then_inc(hid_dve, 1)
                    if f == 1 and not last:
                        again(j + 1, 1 - p)
                    if f == 5 and not last:
                        gate(j + 1, 1 - p)
                e = expert_of(dve, j)
                dve.wait_ge(alpha_step, 2 * j + 2)
                dve.wait_ge(xf_ready, j + 1)
                reach(dve, scattered[p], (j - p) * 16)
                for t in range(NH):
                    dve.wait_ge(y_filled, NH * j + (t + 1))
                    dve.tensor_tensor(y[:, t], ps_y[t][:, 0:D], b2_sb[:, bass.ds(e, 1), :].rearrange(
                        "p o d -> p (o d)"), ALU.add).then_inc(y_ready, 1)
                for t in range(NH):
                    dve.wait_ge(y_ready, NH * j + (t + 1))
                    dve.scalar_tensor_tensor(out=res[:, p, t], in0=y[:, t], scalar=alpha[:, p, t:t + 1],
                                             in1=xf[:, p, t], op0=ALU.mult, op1=ALU.add).then_inc(res_ready, 1)

            over_tiles(dve, step)

        @block.tensor
        def _(pe):
            def turn(j, p):
                pe.wait_ge(xhat_ready, j + 1)
                reach(pe, h_in_ready, j)
                for k in range(KD):
                    for t in range(NH):
                        ins = pe.transpose(ps_x[:, T * k + 128 * t:T * k + 128 * (t + 1)],
                                           xhat[:, t, 128 * k:128 * (k + 1)], c.ident[:])
                ins.then_inc(turned, 1)

            turn(0, 0)

            def step(j, p, last):
                pe.wait_ge(w_loaded[p], (j - p) * 16 + 32)
                pe.wait_ge(h_in_ready, j + 1)
                for f in range(NF):
                    reach(pe, hid_act if f % 2 == 0 else hid_dve, NF // 2 * j + (f // 2 - 1))
                    for k in range(KD):
                        ins = pe.matmul(ps_h[f % 4][:, 0:T], w1_sb[:, p, k, 128 * f:128 * (f + 1)], h_in[:, p, k],
                                        start=(k == 0), stop=(k == KD - 1))
                    ins.then_inc(hid_filled, 1)
                if not last:
                    turn(j + 1, 1 - p)
                pe.wait_ge(hid_act, NF // 2 * (j + 1))
                pe.wait_ge(hid_dve, NF // 2 * (j + 1))
                reach(pe, y_ready, NH * j)
                for t in range(NH):
                    for f in range(NF):
                        ins = pe.matmul(ps_y[t][:, 0:D], hid[:, f, 128 * t:128 * (t + 1)], w2_sb[:, p, f, :],
                                        start=(f == 0), stop=(f == NF - 1))
                    ins.then_inc(y_filled, 1)

            over_tiles(pe, step)


def build(nc, ins, out):
    c = Shared()
    with ExitStack() as ctx:
        def sb(name, shape, dt=F32):
            return ctx.enter_context(nc.sbuf_tensor(name, shape, dt))

        c.x = sb("x_all", [S, B, ROWW])
        c.ident = sb("ident", [128, 128])
        c.neg_ident = sb("neg_ident", [128, 128])
        c.ones_f = sb("ones_f", [128, 128])
        c.ones_r = sb("ones_r", [128, 128], F32R)
        c.before = sb("before", [S, S])
        c.head_of = sb("head_of", [128, HG])
        c.minus_half = sb("minus_half", [128, B])
        v_dram = nc.dram_tensor("v_rows", (B, S, O1), F32, kind="Internal").ap()
        xs = nc.dram_tensor("routed_rows", (SLOTS, ROWW), F32, kind="Internal").ap()
        c.tile_expert = sb("tile_expert", [1, TILES + 1], I32)
        c.empty = sb("empty", [128, ROWW])
        c.xs_cleared = ctx.enter_context(nc.semaphore("xs_cleared"))
        constants(nc, c, xs)
        self_attention(nc, c, ins["x"], ins["wqkT"], ins["wvT"], ins["woT"], v_dram)
        cross_attention(nc, c, ins["context"], ins["mask"], ins["maskT"], ins["wq2T"], ins["wk2T"], ins["wv2T"],
                        ins["wo2T"], ins["bq"], ins["bk"], ins["bv"], ins["bo"])
        route(nc, c, ins["centT"], xs)
        experts(nc, c, xs, ins["w1"], ins["w2"], ins["gamma"], ins["beta"], ins["b1"], ins["b2"], ins["centroids"],
                out.rearrange("b s d -> (b s) d"))


def kernel(**inputs):
    import numpy as _np
    import concourse.bacc as _bacc
    from concourse import mybir as _mybir
    from concourse.bass_utils import run_bass_kernel_spmd as _run

    a = {k: _np.asarray(v) for k, v in inputs.items()}
    lay = {
        "x": a["x"],
        "wqkT": _np.concatenate([a["L0_attn_wq"].T, a["L0_attn_wk"].T], axis=1),
        "wvT": a["L0_attn_wv"].T,
        "woT": a["L0_attn_wo"].T,
        "context": a["ctx_1024"],
        "mask": a["mask_Bx1x1xS2_if1"].reshape(B, S2),
        "maskT": a["mask_Bx1x1xS2_if1"].reshape(B, S2).T,
        "wq2T": a["L0_xattn_Wq"].T,
        "wk2T": a["L0_xattn_Wk"].T,
        "wv2T": a["L0_xattn_Wv"].T,
        "wo2T": a["L0_xattn_Wo"].T,
        "bq": a["L0_xattn_bq"].reshape(KD, 128).T,
        "bk": a["L0_xattn_bk"].reshape(KD, 128).T,
        "bv": a["L0_xattn_bv"],
        "bo": a["L0_xattn_bo"],
        "centT": a["L0_ffn_centroids"].T,
        "centroids": a["L0_ffn_centroids"],
        "w1": a["L0_ffn_w1"],
        "w2": a["L0_ffn_w2"],
        "gamma": a["L0_ffn_gamma"].reshape(E, KD, 128).transpose(2, 1, 0),
        "beta": a["L0_ffn_beta"].reshape(E, KD, 128).transpose(2, 1, 0),
        "b1": a["L0_ffn_b1"].reshape(E, NF, 128).transpose(2, 1, 0),
        "b2": a["L0_ffn_b2"],
    }
    nc = _bacc.Bacc("TRN2", target_bir_lowering=False, num_devices=1)
    arrays, ins = {}, {}
    for name, v in lay.items():
        v = _np.ascontiguousarray(v)
        arrays[f"in_{name}"] = v
        ins[name] = nc.dram_tensor(f"in_{name}", v.shape, _mybir.dt.from_np(v.dtype), kind="ExternalInput").ap()
    out = nc.dram_tensor("out_0", (B, S, D), F32, kind="ExternalOutput").ap()
    build(nc, ins, out)
    r = _run(nc, [arrays], core_ids=[0])
    return r.results[0]["out_0"]
```

```python
from contextlib import ExitStack

import concourse.bass as bass
from concourse import mybir

F32 = mybir.dt.float32
F32R = mybir.dt.float32r
I32 = mybir.dt.int32
U32 = mybir.dt.uint32
ALU = mybir.AluOpType
ACT = mybir.ActivationFunctionType
AX_X = mybir.AxisListType.X

B, S, D = 32, 100, 256
KD = D // 128
EPS = 1e-5

H1, HD1 = 16, 64
O1 = H1 * HD1
QUAD = 4
QUADS = B // QUAD
QT_TOK = QUAD * S
GH = 4
GB = H1 // GH
GQ = QUAD * GB
ROWS = S * O1 // HD1
NT = O1 // 128

S2 = 361
S2E = S2 + 1
H2, HD2 = 16, 16
KT = [121, 121, 119]
KT0 = [0, 121, 242]
HG = 8
NEG = -1.0e30

E, F = 8, 1024
NF = F // 128
T = 256
TILES = (B * S + E * (T - 1)) // T
SLOTS = TILES * T
ROWW = D + 1
NO_TOKEN = 100000.0


def split3(pe, out, hi_l, lo_l, hi_r, lo_r, first, last):
    pe.matmul(out, hi_l, lo_r, start=first, stop=False)
    pe.matmul(out, lo_l, hi_r, start=False, stop=False)
    return pe.matmul(out, hi_l, hi_r, start=False, stop=last)


def constants(nc, c):
    with nc.semaphore("pool_step") as pool_step, nc.Block() as block:
        @block.gpsimd
        def _(pool):
            pool.memset(c.empty[:, 0:D], 0.0).then_inc(pool_step, 1)
            pool.memset(c.empty[:, D:ROWW], NO_TOKEN).then_inc(pool_step, 1)
            pool.memset(c.ident[:], 0.0).then_inc(pool_step, 1)
            pool.memset(c.neg_ident[:], 0.0).then_inc(pool_step, 1)
            pool.memset(c.minus_half[:], -0.5).then_inc(pool_step, 1)
            pool.memset(c.ones_f[:], 1.0).then_inc(pool_step, 1)
            pool.memset(c.before[:], 1.0).then_inc(pool_step, 1)
            pool.memset(c.head_of[:], 1.0).then_inc(pool_step, 1)
            pool.wait_ge(pool_step, 8)
            pool.affine_select(out=c.ident[:], in_=c.ident[:], compare_op=ALU.not_equal, fill=1.0, base=0,
                               pattern=[[-1, 128]], channel_multiplier=1).then_inc(pool_step, 1)
            pool.affine_select(out=c.neg_ident[:], in_=c.neg_ident[:], compare_op=ALU.not_equal, fill=-1.0, base=0,
                               pattern=[[-1, 128]], channel_multiplier=1).then_inc(pool_step, 1)
            pool.affine_select(out=c.before[:], in_=c.before[:], compare_op=ALU.is_gt, fill=0.0, base=0,
                               pattern=[[1, S]], channel_multiplier=-1).then_inc(pool_step, 1)
            pool.affine_select(out=c.head_of[:], in_=c.head_of[:], compare_op=ALU.is_ge, fill=0.0, base=0,
                               pattern=[[-HD2, HG]], channel_multiplier=1).then_inc(pool_step, 1)
            pool.wait_ge(pool_step, 12)
            pool.affine_select(out=c.head_of[:], in_=c.head_of[:], compare_op=ALU.is_ge, fill=0.0, base=HD2 - 1,
                               pattern=[[HD2, HG]], channel_multiplier=-1).then_inc(pool_step, 1)

        @block.vector
        def _(dve):
            dve.wait_ge(pool_step, 8)
            dve.tensor_copy(c.ones_r[:], c.ones_f[:])


class Shared:
    pass


def reach(eng, semaphore, value):
    if isinstance(value, int) and value <= 0:
        return
    eng.wait_ge(semaphore, value)


def at_batch(tensor, b, cols):
    if isinstance(b, int):
        return tensor[:, b, cols]
    return tensor[:, bass.ds(b, 1), cols].rearrange("p b d -> p (b d)")


def self_attention(nc, c, x, wqkT, wvT, woT, v_dram, xs):
    with ExitStack() as ctx:
        def sb(name, shape, dt=F32):
            return ctx.enter_context(nc.sbuf_tensor(name, shape, dt))

        def psum(name, shape, dt=F32):
            return ctx.enter_context(nc.psum_tensor(name, shape, dt))

        def sem(name):
            return ctx.enter_context(nc.semaphore(name))

        w_stage = sb("w_stage", [128, 2, KD, O1])
        w_hi = sb("w_hi", [128, 3, KD, O1], F32R)
        w_lo = sb("w_lo", [128, 3, KD, O1], F32R)
        wo_sb = sb("wo_sb", [128, NT, D])
        stats = sb("stats", [S, QUAD, 6])
        mv = sb("mv", [S, QUAD, 2])
        var_eps = sb("var_eps", [S, QUAD])
        rstd = sb("rstd", [S, QUAD])
        xn = sb("xn", [S, QUAD, D])
        x_hi = sb("x_hi", [128, KD, QT_TOK], F32R)
        x_lo = sb("x_lo", [128, KD, QT_TOK], F32R)
        q_t = sb("q_t", [128, 2, ROWS])
        k_t = sb("k_t", [128, 2, ROWS])
        v_tok = sb("v_tok", [S, QUAD, O1])
        v_ext = sb("v_ext", [S, QUAD, H1, HD1 + 1])
        row_max = sb("row_max", [S, 2, GH])
        diag = sb("diag", [S, 2, GH, S], F32R)
        probs = sb("probs", [S, 2, GH * S])
        recip = sb("recip", [S, GH])
        o_norm = sb("o_norm", [S, 2, GH * HD1])
        o_t = sb("o_t", [128, 2, ROWS // 2])

        ps_p = [psum(f"ps_p{i}", [128, 512]) for i in range(2)]
        ps_s = [psum(f"ps_s{i}", [128, 512]) for i in range(2)]
        ps_t = [psum(f"ps_t{i}", [128, 512]) for i in range(2)]
        ps_o = psum("ps_o", [128, 512])
        ps_ot = psum("ps_ot", [128, 512])

        dve_passed = sem("dve_passed_a")
        pool_passed = sem("pool_passed_a")
        x_first = sem("x_first")
        x_loaded = sem("x_loaded")
        w_loaded = [sem(f"w_loaded{i}") for i in range(3)]
        w_hi_ready = sem("w_hi_ready")
        w_lo_ready = sem("w_lo_ready")
        wo_loaded = sem("wo_loaded")
        ones_ready = sem("ones_ready")
        stats_ready = sem("stats_ready")
        mv_ready = sem("mv_ready")
        eps_added = sem("eps_added")
        rstd_ready = sem("rstd_ready")
        xn_ready = sem("xn_ready")
        filled = sem("filled")
        drained_act = sem("drained_act")
        drained_dve = sem("drained_dve")
        v_stored = [sem(f"v_stored{i}") for i in range(QUAD)]
        v_loaded = [sem(f"v_loaded{i}") for i in range(QUAD)]
        scores_ready = sem("scores_ready")
        max_ready = sem("max_ready")
        diag_ready = sem("diag_ready")
        shifted_ready = sem("shifted_ready")
        probs_ready = sem("probs_ready")
        pv_ready = sem("pv_ready")
        recip_ready = sem("recip_ready")
        o_ready = sem("o_ready")
        ot_ready = sem("ot_ready")
        ot_copied_act = sem("ot_copied_act")
        ot_copied_dve = sem("ot_copied_dve")
        y_ready = sem("y_ready")
        x1_ready = sem("x1_ready")

        FX, FV = KD, KD + 2 * QUAD
        FILLS = FV + 2 * NT
        TAIL = 4

        def spread(copy, f, a):
            t, dst = (f - FV) // 2, (q_t if (f - FV) % 2 == 0 else k_t)
            src = ps_p[f % 2][64 * a:64 * a + 64, 0:QT_TOK].rearrange("p (i s) -> p i s", s=S)
            for odd in range(2):
                out = dst[64 * odd:64 * odd + 64, :, :].rearrange("p i (s c) -> p i s c", c=H1)[:, :, :, 2 * t + a]
                ins = copy(out, src[:, odd::2, :])
            return ins

        def copy_ot(copy, g, a):
            src = ps_ot[64 * a:64 * a + 64, 0:2 * S].rearrange("p (w k two) -> p w k two", w=2, two=2)
            for odd in range(2):
                base = (g % GB) * GH * S // 2
                out = o_t[64 * odd:64 * odd + 64, (g // GB) % 2, base:base + GH * S // 2].rearrange(
                    "p (w a k) -> p w a k", w=2, a=2)[:, :, a, :]
                ins = copy(out, src[:, :, :, odd])
            return ins

        block = ctx.enter_context(nc.Block())

        @block.sync
        def _(sp):
            for q in range(QUADS):
                sp.dma_start(c.x[:, QUAD * q:QUAD * (q + 1), 0:D],
                             x[QUAD * q:QUAD * (q + 1)].rearrange("b s d -> s b d")
                             ).then_inc(x_loaded if q else x_first, 16)
            sp.dma_start(wo_sb[:], woT.rearrange("(t p) n -> p t n", p=128)).then_inc(wo_loaded, 16)
            sp.wait_ge(wo_loaded, 16)
            sp.dma_start(xs.rearrange("(k p) d -> p k d", p=128),
                         c.empty[:].unsqueeze(1).to_broadcast([128, SLOTS // 128, ROWW])).then_inc(c.xs_cleared, 16)
            with sp.Fori(0, QUADS) as q:
                for i in range(QUAD):
                    sp.wait_ge(drained_act, q * FILLS + (FX + 2 * i + 2))
                    sp.wait_ge(drained_dve, q * FILLS + (FX + 2 * i + 2))
                    sp.dma_start(v_dram[bass.ds(q * QUAD + i, 1)].rearrange("b s n -> s (b n)"),
                                 v_tok[:, i, :]).then_inc(v_stored[i], 16)
                for i in range(QUAD):
                    sp.wait_ge(v_stored[i], q * 16 + 16)
                    sp.dma_start(v_ext[:, i, :, 0:HD1],
                                 v_dram[bass.ds(q * QUAD + i, 1)].rearrange(
                                     "b s n -> (b s n)").rearrange(
                                     "(h j d) -> j h d", j=S, d=HD1)).then_inc(v_loaded[i], 16)

        @block.scalar
        def _(act):
            for i, (j, w) in enumerate(((2, wvT), (0, wqkT[:, 0:O1]), (1, wqkT[:, O1:2 * O1]))):
                if i >= 2:
                    act.wait_ge(w_lo_ready, i - 1)
                act.dma_start(w_stage[:, i % 2], w.rearrange("(k p) n -> p k n", p=128)).then_inc(w_loaded[i], 16)
                if i == 0:
                    continue
                act.wait_ge(w_loaded[i - 1], 16)
                act.copy(w_hi[:, (i + 1) % 3], w_stage[:, (i - 1) % 2]).then_inc(w_hi_ready, 1)
            act.wait_ge(w_loaded[2], 16)
            act.copy(w_hi[:, 1], w_stage[:, 0]).then_inc(w_hi_ready, 1)

            with act.Fori(0, QUADS) as q:
                for k in range(KD):
                    act.wait_ge(filled, q * FILLS + (k + 1))
                    act.copy(x_hi[:, k], ps_p[k % 2][:, 0:QT_TOK]).then_inc(drained_act, 1)
                for f in range(FX, FV):
                    i, v = (f - FX) // 2, (f - FX) % 2
                    act.wait_ge(filled, q * FILLS + (f + 1))
                    act.copy(v_tok[0:64, i, 512 * v:512 * (v + 1)], ps_p[f % 2][0:64, :]).then_inc(drained_act, 1)
                for f in range(FV, FILLS):
                    act.wait_ge(filled, q * FILLS + (f + 1))
                    ins = spread(act.copy, f, 0)
                    ins.then_inc(drained_act, 1)
                for j in range(GQ + TAIL):
                    if 0 <= j - 1 < GQ:
                        g = j - 1
                        act.wait_ge(shifted_ready, q * GQ + (g + 1))
                        if g >= 2:
                            act.wait_ge(pv_ready, q * GQ + (g - 1))
                        act.activation(probs[:, g % 2], ps_t[g % 2][0:S, 0:GH * S], ACT.Exp,
                                       scale=HD1 ** -0.5).then_inc(probs_ready, 1)
                    if 0 <= j - 3 < GQ:
                        g = j - 3
                        act.wait_ge(ot_ready, q * GQ + (g + 1))
                        if g >= 2 * GB and g % GB == 0:
                            act.wait_ge(y_ready, q * QUAD + (g // GB - 1))
                        copy_ot(act.copy, g, 0).then_inc(ot_copied_act, 1)

        @block.gpsimd
        def _(pool):
            pool.memset(v_ext[:, :, :, HD1:HD1 + 1], 1.0).then_inc(ones_ready, 1)
            def inverse_root(q):
                pool.wait_ge(mv_ready, q * QUAD + QUAD)
                pool.sem_inc(pool_passed, 1)
                pool.tensor_scalar(var_eps[:], mv[:, :, 1], EPS, None, ALU.add).then_inc(eps_added, 1)
                pool.wait_ge(eps_added, q + 1)
                pool.tensor_tensor(rstd[:], var_eps[:], c.minus_half[0:S, 0:QUAD], ALU.pow).then_inc(rstd_ready, 1)

            inverse_root(0)

            def quad(q, last):
                for g in range(GQ):
                    pool.wait_ge(max_ready, q * GQ + (g + 1))
                    if g >= 2:
                        pool.wait_ge(shifted_ready, q * GQ + (g - 1))
                    pool.tensor_tensor(diag[:, g % 2],
                                       c.neg_ident[0:S, 0:S].unsqueeze(1).to_broadcast([S, GH, S]),
                                       row_max[:, g % 2].unsqueeze(2).to_broadcast([S, GH, S]),
                                       ALU.mult).then_inc(diag_ready, 1)
                    if g == 6 and not last:
                        inverse_root(q + 1)

            with pool.Fori(0, QUADS - 1) as q:
                quad(q, False)
            quad(QUADS - 1, True)

        @block.vector
        def _(dve):
            def moments(q):
                for i in range(QUAD):
                    dve.bn_stats(stats[:, i], at_batch(c.x, q * QUAD + i, slice(0, D))).then_inc(stats_ready, 1)
                dve.wait_ge(stats_ready, q * QUAD + QUAD)
                dve.sem_inc(dve_passed, 1)
                for i in range(QUAD):
                    dve.bn_aggr(mv[:, i], stats[:, i]).then_inc(mv_ready, 1)

            def low_bits(i):
                dve.wait_ge(w_hi_ready, i + 1)
                dve.tensor_tensor(w_lo[:, (i + 2) % 3], w_stage[:, i % 2], w_hi[:, (i + 2) % 3].bitcast(F32),
                                  ALU.subtract).then_inc(w_lo_ready, 1)

            dve.wait_ge(x_first, 16)
            moments(0)
            low_bits(0)

            def normalize(q):
                dve.wait_ge(rstd_ready, q + 1)
                for i in range(QUAD):
                    dve.tensor_scalar(xn[:, i], at_batch(c.x, q * QUAD + i, slice(0, D)), mv[:, i, 0:1],
                                      rstd[:, i:i + 1], ALU.subtract, ALU.mult).then_inc(xn_ready, 1)

            normalize(0)
            low_bits(1)
            low_bits(2)
            dve.wait_ge(x_loaded, 16 * (QUADS - 1))
            def quad(q, last):
                for k in range(KD):
                    dve.wait_ge(drained_act, q * FILLS + (k + 1))
                    dve.tensor_tensor(x_lo[:, k], ps_p[k % 2][:, 0:QT_TOK], x_hi[:, k].bitcast(F32),
                                      ALU.subtract).then_inc(drained_dve, 1)
                for f in range(FX, FV):
                    i, v = (f - FX) // 2, (f - FX) % 2
                    dve.wait_ge(filled, q * FILLS + (f + 1))
                    dve.tensor_copy(v_tok[64:S, i, 512 * v:512 * (v + 1)],
                                    ps_p[f % 2][64:S, :]).then_inc(drained_dve, 1)
                for f in range(FV, FILLS):
                    dve.wait_ge(filled, q * FILLS + (f + 1))
                    spread(dve.tensor_copy, f, 1).then_inc(drained_dve, 1)
                for j in range(GQ + TAIL):
                    if j < GQ:
                        g = j
                        dve.wait_ge(scores_ready, q * GQ + (g + 1))
                        if g >= 2:
                            dve.wait_ge(diag_ready, q * GQ + (g - 1))
                        dve.reduce_max(row_max[:, g % 2], ps_s[g % 2][0:S, 0:GH * S].rearrange(
                            "p (h j) -> p h j", h=GH), AX_X).then_inc(max_ready, 1)
                    if 0 <= j - 2 < GQ:
                        g = j - 2
                        dve.wait_ge(pv_ready, q * GQ + (g + 1))
                        o = ps_o[0:S, 0:GH * (HD1 + 1)].rearrange("p (h d) -> p h d", h=GH)
                        dve.reciprocal(recip[:], o[:, :, HD1]).then_inc(recip_ready, 1)
                        dve.wait_ge(recip_ready, q * GQ + (g + 1))
                        if g >= 2:
                            dve.wait_ge(ot_ready, q * GQ + (g - 1))
                        dve.tensor_tensor(o_norm[:, g % 2].rearrange("p (h d) -> p h d", h=GH), o[:, :, 0:HD1],
                                          recip[:].unsqueeze(2).to_broadcast([S, GH, HD1]),
                                          ALU.mult).then_inc(o_ready, 1)
                    if 0 <= j - 3 < GQ:
                        g = j - 3
                        dve.wait_ge(ot_ready, q * GQ + (g + 1))
                        if g >= 2 * GB and g % GB == 0:
                            dve.wait_ge(y_ready, q * QUAD + (g // GB - 1))
                        copy_ot(dve.tensor_copy, g, 1).then_inc(ot_copied_dve, 1)
                    if 0 <= j - 4 < GQ and (j - 4) % GB == GB - 1:
                        i = (j - 4) // GB
                        dve.wait_ge(y_ready, q * QUAD + (i + 1))
                        xb = at_batch(c.x, q * QUAD + i, slice(0, D))
                        dve.tensor_tensor(xb, ps_p[i % 2][0:S, 0:D], xb, ALU.add).then_inc(x1_ready, 1)
                    if j == 6 and not last:
                        moments(q + 1)
                    if j == 9 and not last:
                        normalize(q + 1)

            with dve.Fori(0, QUADS - 1) as q:
                quad(q, False)
            quad(QUADS - 1, True)

        @block.tensor
        def _(pe):
            pe.wait_ge(ones_ready, 1)

            def quad(q):
                pe.wait_ge(xn_ready, q * QUAD + QUAD)
                for k in range(KD):
                    for i in range(QUAD):
                        ins = pe.transpose(ps_p[k % 2][:, S * i:S * (i + 1)], xn[:, i, 128 * k:128 * (k + 1)],
                                           c.ident[0:S, 0:S])
                    ins.then_inc(filled, 1)
                for f in range(FX, FV):
                    i, v = (f - FX) // 2, (f - FX) % 2
                    pe.wait_ge(drained_act, q * FILLS + (f - 1))
                    pe.wait_ge(drained_dve, q * FILLS + (f - 1))
                    if f == FX and isinstance(q, int):
                        pe.wait_ge(w_lo_ready, 1)
                    if f == FX:
                        pe.wait_ge(drained_dve, q * FILLS + KD)
                    for k in range(KD):
                        ins = split3(pe, ps_p[f % 2][0:S, :], x_hi[:, k, S * i:S * (i + 1)],
                                     x_lo[:, k, S * i:S * (i + 1)], w_hi[:, 2, k, 512 * v:512 * (v + 1)],
                                     w_lo[:, 2, k, 512 * v:512 * (v + 1)], k == 0, k == KD - 1)
                    ins.then_inc(filled, 1)
                for f in range(FV, FILLS):
                    t, qk = (f - FV) // 2, (f - FV) % 2
                    if f == FV and isinstance(q, int):
                        pe.wait_ge(w_lo_ready, 3)
                        pe.wait_ge(wo_loaded, 16)
                    pe.wait_ge(drained_act, q * FILLS + (f - 1))
                    pe.wait_ge(drained_dve, q * FILLS + (f - 1))
                    for k in range(KD):
                        ins = split3(pe, ps_p[f % 2][:, 0:QT_TOK], w_hi[:, qk, k, 128 * t:128 * (t + 1)],
                                     w_lo[:, qk, k, 128 * t:128 * (t + 1)], x_hi[:, k], x_lo[:, k],
                                     k == 0, k == KD - 1)
                    ins.then_inc(filled, 1)
                pe.wait_ge(drained_act, q * FILLS + FILLS)
                pe.wait_ge(drained_dve, q * FILLS + FILLS)

                def head(src, g, h):
                    i, lo = g // GB, 64 * ((g // GB) % 2)
                    r = ((g % GB) * GH + h) * S
                    return src[lo:lo + 64, i // 2, r:r + S]

                for j in range(GQ + TAIL):
                    if j < GQ:
                        g = j
                        if g >= 2:
                            pe.wait_ge(max_ready, q * GQ + (g - 1))
                        for h in range(GH):
                            ins = pe.matmul(ps_s[g % 2][0:S, S * h:S * (h + 1)], head(q_t, g, h), head(k_t, g, h),
                                            start=True, stop=True)
                        ins.then_inc(scores_ready, 1)
                    if 0 <= j - 1 < GQ:
                        g = j - 1
                        if g >= 2:
                            pe.wait_ge(probs_ready, q * GQ + (g - 1))
                        for h in range(GH):
                            pe.matmul(ps_t[g % 2][0:S, S * h:S * (h + 1)], head(k_t, g, h), head(q_t, g, h),
                                      start=(h == 0), stop=False, skip_group_check=True)
                        pe.wait_ge(diag_ready, q * GQ + (g + 1))
                        ins = pe.matmul(ps_t[g % 2][0:S, 0:GH * S], c.ones_r[0:S, 0:S],
                                        diag[:, g % 2].rearrange("p h j -> p (h j)"), start=False, stop=True,
                                        skip_group_check=True)
                        ins.then_inc(shifted_ready, 1)
                    if 0 <= j - 2 < GQ:
                        g = j - 2
                        if g % GB == 0:
                            pe.wait_ge(v_loaded[g // GB], q * 16 + 16)
                        pe.wait_ge(probs_ready, q * GQ + (g + 1))
                        if g >= 1:
                            pe.wait_ge(o_ready, q * GQ + g)
                        for h in range(GH):
                            ins = pe.matmul(ps_o[0:S, (HD1 + 1) * h:(HD1 + 1) * (h + 1)],
                                            probs[:, g % 2, S * h:S * (h + 1)],
                                            v_ext[:, g // GB, (g % GB) * GH + h, :], start=True, stop=True)
                        ins.then_inc(pv_ready, 1)
                    if 0 <= j - 3 < GQ:
                        g = j - 3
                        pe.wait_ge(o_ready, q * GQ + (g + 1))
                        if g >= 1:
                            pe.wait_ge(ot_copied_act, q * GQ + g)
                            pe.wait_ge(ot_copied_dve, q * GQ + g)
                        for w in range(2):
                            ins = pe.transpose(ps_ot[:, S * w:S * (w + 1)], o_norm[:, g % 2, 128 * w:128 * (w + 1)],
                                               c.ident[0:S, 0:S])
                        ins.then_inc(ot_ready, 1)
                    if 0 <= j - 4 < GQ and (j - 4) % GB == GB - 1:
                        i = (j - 4) // GB
                        pe.wait_ge(ot_copied_act, q * GQ + (j - 3))
                        pe.wait_ge(ot_copied_dve, q * GQ + (j - 3))
                        if i >= 2:
                            pe.wait_ge(x1_ready, q * QUAD + (i - 1))
                        heads = o_t[:, i % 2, :].rearrange("p (s t) -> p t s", t=NT)
                        for t in range(NT):
                            ins = pe.matmul(ps_p[i % 2][0:S, 0:D], heads[:, t, :], wo_sb[:, t, :],
                                            start=(t == 0), stop=(t == NT - 1))
                        ins.then_inc(y_ready, 1)
                pe.wait_ge(x1_ready, q * QUAD + QUAD)

            quad(0)
            with pe.Fori(1, QUADS) as q:
                quad(q)


def paired(eng, emit):
    emit(0, 0, False)
    emit(1, 1, False)
    with eng.Fori(1, B // 2 - 1) as i:
        emit(i * 2, 0, False)
        emit(i * 2 + 1, 1, False)
    emit(B - 2, 0, False)
    emit(B - 1, 1, True)


def row(b):
    return b if isinstance(b, int) else bass.ds(b, 1)


def cross_attention(nc, c, ctx_in, mask, maskT, wq, wk, wv, wo, bq, bk, bv, bo):
    with ExitStack() as ctx:
        def sb(name, shape, dt=F32):
            return ctx.enter_context(nc.sbuf_tensor(name, shape, dt))

        def psum(name, shape, dt=F32):
            return ctx.enter_context(nc.psum_tensor(name, shape, dt))

        def sem(name):
            return ctx.enter_context(nc.semaphore(name))

        KP = KT[0]
        wq_sb = sb("wq2", [128, KD, D])
        wk_st = sb("wk_stage", [128, KD, D])
        wv_st = sb("wv_stage", [128, KD, D])
        wk_hi = sb("wk_hi", [128, KD, D], F32R)
        wk_lo = sb("wk_lo", [128, KD, D], F32R)
        wv_hi = sb("wv_hi", [128, KD, D], F32R)
        wv_lo = sb("wv_lo", [128, KD, D], F32R)
        wo_sb = sb("wo2", [128, KD, D])
        bq_sb = sb("bq", [128, KD])
        bk_sb = sb("bk", [128, KD])
        bv_sb = sb("bv", [KP, D])
        bo_sb = sb("bo", [S, D])
        mask_t = sb("mask_t", [KP, 3, B], I32)
        key_live = sb("key_live", [KP, 3, B])
        key_bias = sb("key_bias", [KP, 3, B])
        mask_i = sb("mask_i", [S, 2, S2], I32)
        mask_f = sb("mask_f", [S, 2, S2])
        c_tok = sb("c_tok", [KP, 2, 3, D])
        c_hi = sb("c_hi", [128, KD, S2E], F32R)
        c_lo = sb("c_lo", [128, KD, S2E], F32R)
        stats = sb("stats2", [S, 6])
        mv = sb("mv2", [S, 2])
        var_eps = sb("var_eps2", [S, 1])
        rstd = sb("rstd2", [S, 1])
        xn = sb("xn2", [S, D])
        x_t = sb("x_t2", [128, KD * S])
        q_b = sb("q_b", [128, KD * S])
        q_hi = sb("q_hi", [128, KD * S])
        q_lo = sb("q_lo", [128, KD * S])
        qd_hi = sb("qd_hi", [128, 2, KD, HG, S], F32R)
        qd_lo = sb("qd_lo", [128, 2, KD, HG, S], F32R)
        k_hi = sb("k_hi", [128, 2, KD, S2E], F32R)
        k_lo = sb("k_lo", [128, 2, KD, S2E], F32R)
        v_ext = sb("v_ext2", [KP, 2, 3, H2, 32])
        masked = sb("masked", [S, 2, S2])
        row_max = sb("row_max2", [S, 2, 4])
        diag = sb("diag2", [S, 2, 4, S], F32R)
        probs = sb("probs2", [KP, 2, 3, 4 * S])
        recip = sb("recip2", [S, H2])
        o_raw = sb("o_raw", [128, 4 * S])
        o_norm = sb("o_norm2", [S, D])
        o_t = sb("o_t2", [128, KD * S])

        ps_p = [psum(f"psb_p{i}", [128, 512]) for i in range(2)]
        ps_s = [psum(f"psb_s{i}", [128, 512]) for i in range(2)]
        ps_t = [psum(f"psb_t{i}", [128, 512]) for i in range(2)]
        ps_o = psum("psb_o", [128, 512])
        ps_f = psum("psb_f", [128, 512])

        act_passed = sem("act_passed")
        dve_passed = sem("dve_passed")
        pool_passed = sem("pool_passed")
        w_loaded = sem("w2_loaded")
        w_hi_ready = sem("w2_hi_ready")
        w_lo_ready = sem("w2_lo_ready")
        mask_t_loaded = sem("mask_t_loaded")
        key_mask_cleared = sem("key_mask_cleared")
        key_mask_ready = sem("key_mask_ready")
        pad_ready = sem("pad_ready")
        ctx_loaded = [sem(f"ctx_loaded{p}") for p in range(2)]
        mask_loaded = [sem(f"mask_loaded{p}") for p in range(2)]
        mask_ready = sem("mask_ready")
        ones_ready = sem("ones2_ready")
        stats_ready = sem("stats2_ready")
        mv_ready = sem("mv2_ready")
        eps_added = sem("eps2_added")
        rstd_ready = sem("rstd2_ready")
        xn_ready = sem("xn2_ready")
        bo_added = sem("bo_added")
        filled = sem("filled2")
        drained_act = sem("drained2_act")
        drained_dve = sem("drained2_dve")
        q_rounded = sem("q_rounded")
        q_split = sem("q_split")
        qd_ready = sem("qd_ready")
        scores_ready = sem("scores2_ready")
        max_ready = sem("max2_ready")
        diag_ready = sem("diag2_ready")
        shifted_ready = sem("shifted2_ready")
        probs_ready = sem("probs2_ready")
        pv_ready = sem("pv2_ready")
        raw_copied = sem("raw_copied")
        raw_turned = sem("raw_turned")
        recip_ready = sem("recip2_ready")
        o_ready = sem("o2_ready")
        ot_ready = sem("ot2_ready")
        ot_copied = sem("ot2_copied")
        y_ready = sem("y2_ready")
        x2_ready = sem("x2_ready")

        C0, XT, Q0, K0, V0, FILLS = 0, 2, 3, 4, 6, 9
        ACT_OF = {0: 1, 1: 2, XT: 3, Q0: 4, K0: 5, K0 + 1: 6}
        DVE_OF = {0: 1, 1: 2, K0: 3, K0 + 1: 4, V0: 5, V0 + 1: 6, V0 + 2: 7}
        NA, ND = len(ACT_OF), len(DVE_OF)

        def bank(pp, f):
            return ps_p[(FILLS * pp + f) % 2]

        def bank_free(pe, pb, f):
            pb, f = (pb, f - 2) if f >= 2 else (pb - 1, f - 2 + FILLS)
            if f in DVE_OF:
                reach(pe, drained_dve, pb * ND + DVE_OF[f])
            else:
                reach(pe, drained_act, pb * NA + ACT_OF[f])

        block = ctx.enter_context(nc.Block())

        @block.sync
        def _(sp):
            for dst, src in ((wk_st, wk), (wv_st, wv), (wq_sb, wq), (wo_sb, wo)):
                sp.dma_start(dst[:], src.rearrange("(k p) n -> p k n", p=128)).then_inc(w_loaded, 16)
            sp.dma_start(bq_sb[:], bq).then_inc(w_loaded, 16)
            sp.dma_start(bk_sb[:], bk).then_inc(w_loaded, 16)
            sp.dma_start(bv_sb[:], bv.rearrange("(o n) -> o n", o=1).to_broadcast([KP, D])).then_inc(w_loaded, 16)
            sp.dma_start(bo_sb[:], bo.rearrange("(o n) -> o n", o=1).to_broadcast([S, D])).then_inc(w_loaded, 16)
            sp.wait_ge(key_mask_cleared, 1)
            for kt in range(3):
                sp.dma_start(mask_t[0:KT[kt], kt, :], maskT[KT0[kt]:KT0[kt] + KT[kt], :]).then_inc(mask_t_loaded, 16)

            def load(pb, p, _):
                reach(sp, filled, (pb - 2) * FILLS + 2)
                sp.dma_start(c_tok[:, p, 0:2, :], ctx_in[row(pb), 0:2 * KP, :].rearrange(
                    "(k r) d -> r k d" if isinstance(pb, int) else "b (k r) d -> r (b k) d",
                    r=KP)).then_inc(ctx_loaded[p], 16)
                last = ctx_in[row(pb), 2 * KP:S2, :]
                sp.dma_start(c_tok[0:KT[2], p, 2, :],
                             last if isinstance(pb, int) else last.rearrange("b r d -> (b r) d")
                             ).then_inc(ctx_loaded[p], 16)
                reach(sp, mask_ready, pb - 1)
                m = mask[row(pb), :]
                m = m.rearrange("(o n) -> o n", o=1) if isinstance(pb, int) else m
                sp.dma_start(mask_i[:, p, :], m.to_broadcast([S, S2])).then_inc(mask_loaded[p], 16)

            paired(sp, load)

        @block.gpsimd
        def _(pool):
            pool.memset(mask_t[:], 0).then_inc(key_mask_cleared, 1)
            pool.memset(c_hi[:, :, S2:S2E].bitcast(F32), 0.0).then_inc(pad_ready, 1)
            pool.memset(c_lo[:, :, S2:S2E].bitcast(F32), 0.0).then_inc(pad_ready, 1)
            pool.memset(v_ext[:, :, :, :, HD2:32], 0.0).then_inc(pad_ready, 1)
            pool.wait_ge(pad_ready, 3)
            pool.wait_ge(mask_t_loaded, 48)
            pool.wait_ge(w_loaded, 16 * 8)
            pool.tensor_scalar(key_bias[:], mask_t[:], 0.0, NEG, ALU.is_equal, ALU.mult).then_inc(key_mask_ready, 1)
            pool.wait_ge(key_mask_ready, 1)
            pool.tensor_scalar(key_live[:], key_bias[:], 0.0, None, ALU.is_equal).then_inc(key_mask_ready, 1)
            pool.wait_ge(key_mask_ready, 2)

            def ln_step(pb):
                pool.wait_ge(mv_ready, pb + 1)
                pool.sem_inc(pool_passed, 1)
                pool.tensor_scalar(var_eps[:], mv[:, 1:2], EPS, None, ALU.add).then_inc(eps_added, 1)
                pool.wait_ge(eps_added, pb + 1)
                pool.tensor_tensor(rstd[:], var_eps[:], c.minus_half[0:S, 0:1], ALU.pow).then_inc(rstd_ready, 1)

            def mask_step(pb, pp):
                pool.wait_ge(mask_loaded[pp], (pb - pp) * 8 + 16)
                pool.sem_inc(pool_passed, 1)
                pool.tensor_scalar(mask_f[:, pp], mask_i[:, pp], 0.0, NEG, ALU.is_equal,
                                   ALU.mult).then_inc(mask_ready, 1)
                live = (key_live[:, :, pb:pb + 1] if isinstance(pb, int) else key_live[:, :, bass.ds(pb, 1)])
                pool.tensor_copy(v_ext[:, pp, :, :, HD2:HD2 + 1].rearrange("p k h o -> p k (h o)"),
                                 live.to_broadcast([KP, 3, H2])).then_inc(ones_ready, 1)

            def bo_step(pb):
                pool.wait_ge(xn_ready, pb + 1)
                xb = at_batch(c.x, pb, slice(0, D))
                pool.tensor_tensor(xb, xb, bo_sb[:], ALU.add).then_inc(bo_added, 1)

            def place(pb, pp, g):
                pool.wait_ge(q_split, 2 * pb + 2)
                for src, dst in ((q_hi, qd_hi), (q_lo, qd_lo)):
                    pool.tensor_tensor(dst[:, pp, g], src[:, S * g:S * (g + 1)].unsqueeze(1).to_broadcast([128, HG, S]),
                                       c.head_of[:].unsqueeze(2).to_broadcast([128, HG, S]),
                                       ALU.mult).then_inc(qd_ready, 1)

            def diagonal(b, u):
                pool.wait_ge(max_ready, b * H2 + 4 * (u + 1))
                reach(pool, shifted_ready, b * 12 + 3 * (u - 1))
                pool.tensor_tensor(diag[:, u % 2], c.neg_ident[0:S, 0:S].unsqueeze(1).to_broadcast([S, 4, S]),
                                   row_max[:, u % 2].unsqueeze(2).to_broadcast([S, 4, S]),
                                   ALU.mult).then_inc(diag_ready, 1)

            ln_step(0)
            mask_step(0, 0)
            bo_step(0)
            place(0, 0, 0)
            place(0, 0, 1)
            diagonal(0, 0)

            def step(b, p, last):
                if not last:
                    ln_step(b + 1)
                diagonal(b, 1)
                if not last:
                    bo_step(b + 1)
                diagonal(b, 2)
                if not last:
                    place(b + 1, 1 - p, 0)
                    mask_step(b + 1, 1 - p)
                diagonal(b, 3)
                if not last:
                    place(b + 1, 1 - p, 1)
                    diagonal(b + 1, 0)

            paired(pool, step)

        @block.scalar
        def _(act):
            act.wait_ge(w_loaded, 16 * 8)
            act.copy(wk_hi[:], wk_st[:]).then_inc(w_hi_ready, 1)
            act.copy(wv_hi[:], wv_st[:]).then_inc(w_hi_ready, 1)
            act.wait_ge(key_mask_ready, 2)

            def context(pb, pp):
                for k in range(KD):
                    act.wait_ge(filled, pb * FILLS + (k + 1))
                    act.copy(c_hi[:, k, 0:S2], bank(pp, k)[:, 0:S2]).then_inc(drained_act, 1)

            def x_turned(pb, pp):
                act.wait_ge(filled, pb * FILLS + (XT + 1))
                act.copy(x_t[:], bank(pp, XT)[:, 0:KD * S]).then_inc(drained_act, 1)

            def queries(pb, pp):
                act.wait_ge(filled, pb * FILLS + (Q0 + 1))
                reach(act, q_split, 2 * pb)
                for g in range(KD):
                    ins = act.activation(q_b[:, S * g:S * (g + 1)], bank(pp, Q0)[:, S * g:S * (g + 1)], ACT.Identity,
                                         bias=bq_sb[:, g:g + 1])
                ins.then_inc(drained_act, 1)

            def keys(pb, pp):
                for g in range(KD):
                    act.wait_ge(filled, pb * FILLS + (K0 + g + 1))
                    act.activation(k_hi[:, pp, g], bank(pp, K0 + g)[:, 0:S2E], ACT.Identity,
                                   bias=bk_sb[:, g:g + 1]).then_inc(drained_act, 1)

            def exps(b, u, kt):
                if kt == 0:
                    reach(act, pv_ready, b * 4 + (u - 1))
                i = 3 * u + kt
                act.wait_ge(shifted_ready, b * 12 + (i + 1))
                act.sem_inc(act_passed, 1)
                bias = key_bias[0:KT[kt], kt, b:b + 1] if isinstance(b, int) else key_bias[0:KT[kt], kt, bass.ds(b, 1)]
                act.activation(probs[0:KT[kt], u % 2, kt], ps_t[i % 2][0:KT[kt], 0:4 * S], ACT.Exp,
                               bias=bias, scale=HD2 ** -0.5).then_inc(probs_ready, 1)

            def raw_out(b):
                act.wait_ge(pv_ready, b * 4 + 4)
                act.copy(o_raw[:], ps_o[:, 0:4 * S]).then_inc(raw_copied, 1)

            def turned_out(b):
                act.wait_ge(ot_ready, b + 1)
                act.copy(o_t[:], ps_f[:, 0:KD * S]).then_inc(ot_copied, 1)

            context(0, 0)
            x_turned(0, 0)
            queries(0, 0)
            keys(0, 0)

            def step(b, p, last):
                first = isinstance(b, int) and b == 0
                for kt in range(3):
                    exps(b, 0, kt)
                if not last:
                    context(b + 1, 1 - p)
                if not first:
                    raw_out(b - 1)
                exps(b, 1, 0)
                if not last:
                    x_turned(b + 1, 1 - p)
                exps(b, 1, 1)
                if not last:
                    queries(b + 1, 1 - p)
                exps(b, 1, 2)
                if not last:
                    keys(b + 1, 1 - p)
                for kt in range(3):
                    exps(b, 2, kt)
                if not first:
                    turned_out(b - 1)
                for kt in range(3):
                    exps(b, 3, kt)

            paired(act, step)
            raw_out(B - 1)
            turned_out(B - 1)

        @block.vector
        def _(dve):
            for j, (hi, lo, st) in enumerate(((wk_hi, wk_lo, wk_st), (wv_hi, wv_lo, wv_st))):
                dve.wait_ge(w_hi_ready, j + 1)
                dve.tensor_tensor(lo[:], st[:], hi[:].bitcast(F32), ALU.subtract).then_inc(w_lo_ready, 1)

            def norm_stats(pb):
                dve.bn_stats(stats[:], at_batch(c.x, pb, slice(0, D))).then_inc(stats_ready, 1)
                dve.wait_ge(stats_ready, pb + 1)
                dve.sem_inc(dve_passed, 1)
                dve.bn_aggr(mv[:], stats[:]).then_inc(mv_ready, 1)

            def normalize(pb):
                dve.wait_ge(rstd_ready, pb + 1)
                dve.tensor_scalar(xn[:], at_batch(c.x, pb, slice(0, D)), mv[:, 0:1], rstd[:], ALU.subtract,
                                  ALU.mult).then_inc(xn_ready, 1)

            def context(pb, pp):
                for k in range(KD):
                    dve.wait_ge(drained_act, pb * NA + ACT_OF[k])
                    dve.tensor_tensor(c_lo[:, k, 0:S2], bank(pp, k)[:, 0:S2], c_hi[:, k, 0:S2].bitcast(F32),
                                      ALU.subtract).then_inc(drained_dve, 1)

            def queries(pb, pp):
                dve.wait_ge(drained_act, pb * NA + ACT_OF[Q0])
                reach(dve, qd_ready, 4 * pb)
                dve.tensor_copy(q_hi[:].bitcast(F32R), q_b[:]).then_inc(q_split, 1)
                dve.wait_ge(q_split, 2 * pb + 1)
                dve.tensor_tensor(q_lo[:], q_b[:], q_hi[:], ALU.subtract).then_inc(q_split, 1)

            def keys(pb, pp):
                for g in range(KD):
                    dve.wait_ge(drained_act, pb * NA + ACT_OF[K0 + g])
                    dve.scalar_tensor_tensor(out=k_lo[:, pp, g], in0=bank(pp, K0 + g)[:, 0:S2E],
                                             scalar=bk_sb[:, g:g + 1], in1=k_hi[:, pp, g].bitcast(F32),
                                             op0=ALU.add, op1=ALU.subtract).then_inc(drained_dve, 1)

            def values(pb, pp):
                for kt in range(3):
                    dve.wait_ge(filled, pb * FILLS + (V0 + kt + 1))
                    n = KT[kt]
                    dve.tensor_tensor(v_ext[0:n, pp, kt, :, 0:HD2],
                                      bank(pp, V0 + kt)[0:n, 0:D].rearrange("p (h d) -> p h d", h=H2),
                                      bv_sb[0:n, :].rearrange("p (h d) -> p h d", h=H2),
                                      ALU.add).then_inc(drained_dve, 1)

            def maximum(b, p, h):
                if h == 0:
                    dve.wait_ge(mask_ready, b + 1)
                if h % 4 == 0:
                    reach(dve, diag_ready, b * 4 + (h // 4 - 1))
                dve.wait_ge(scores_ready, b * H2 + (h + 1))
                dve.sem_inc(dve_passed, 1)
                dve.tensor_tensor_reduce(masked[:, h % 2], ps_s[h % 2][0:S, 0:S2], mask_f[:, p], 1.0, -3.0e38,
                                         ALU.add, ALU.max,
                                         row_max[:, (h // 4) % 2, h % 4:h % 4 + 1]).then_inc(max_ready, 1)

            def maxima(b, p, u):
                for h in range(4 * u, 4 * u + 4):
                    maximum(b, p, h)

            def quotients(b):
                o = ps_f[0:S, 0:H2 * 32].rearrange("p (h d) -> p h d", h=H2)
                dve.wait_ge(raw_turned, b + 1)
                dve.reciprocal(recip[:], o[:, :, HD2]).then_inc(recip_ready, 1)
                dve.wait_ge(recip_ready, b + 1)
                dve.tensor_tensor(o_norm[:].rearrange("p (h d) -> p h d", h=H2), o[:, :, 0:HD2],
                                  recip[:].unsqueeze(2).to_broadcast([S, H2, HD2]), ALU.mult).then_inc(o_ready, 1)

            def residual(b):
                dve.wait_ge(y_ready, b + 1)
                dve.wait_ge(bo_added, b + 1)
                xb = at_batch(c.x, b, slice(0, D))
                dve.tensor_tensor(xb, ps_f[0:S, 0:D], xb, ALU.add).then_inc(x2_ready, 1)

            dve.wait_ge(w_lo_ready, 2)
            norm_stats(0)
            normalize(0)
            context(0, 0)
            queries(0, 0)
            keys(0, 0)
            values(0, 0)
            maxima(0, 0, 0)

            def step(b, p, last):
                first = isinstance(b, int) and b == 0
                if not last:
                    norm_stats(b + 1)
                maxima(b, p, 1)
                if not last:
                    normalize(b + 1)
                    context(b + 1, 1 - p)
                for h in range(8, 11):
                    maximum(b, p, h)
                if not last:
                    queries(b + 1, 1 - p)
                maximum(b, p, 11)
                if not first:
                    quotients(b - 1)
                if not last:
                    keys(b + 1, 1 - p)
                maxima(b, p, 3)
                if not last:
                    values(b + 1, 1 - p)
                    maxima(b + 1, 1 - p, 0)
                if not first:
                    residual(b - 1)

            paired(dve, step)
            quotients(B - 1)
            residual(B - 1)

        @block.tensor
        def _(pe):
            pe.wait_ge(w_loaded, 16 * 8)
            pe.wait_ge(w_hi_ready, 2)
            pe.wait_ge(w_lo_ready, 2)
            pe.wait_ge(pad_ready, 3)

            def context(pb, pp):
                reach(pe, ctx_loaded[pp], (pb - pp) * 16 + 32)
                for k in range(KD):
                    bank_free(pe, pb, C0 + k)
                    for kt in range(3):
                        ins = pe.transpose(bank(pp, k)[:, KT0[kt]:KT0[kt] + KT[kt]],
                                           c_tok[0:KT[kt], pp, kt, 128 * k:128 * (k + 1)],
                                           c.ident[0:KT[kt], 0:KT[kt]])
                    ins.then_inc(filled, 1)

            def turn_x(pb, pp):
                bank_free(pe, pb, XT)
                pe.wait_ge(xn_ready, pb + 1)
                for k in range(KD):
                    ins = pe.transpose(bank(pp, XT)[:, S * k:S * (k + 1)], xn[:, 128 * k:128 * (k + 1)],
                                       c.ident[0:S, 0:S])
                ins.then_inc(filled, 1)

            def queries(pb, pp):
                bank_free(pe, pb, Q0)
                pe.wait_ge(drained_act, pb * NA + ACT_OF[XT])
                for g in range(KD):
                    for k in range(KD):
                        ins = pe.matmul(bank(pp, Q0)[:, S * g:S * (g + 1)], wq_sb[:, k, 128 * g:128 * (g + 1)],
                                        x_t[:, S * k:S * (k + 1)], start=(k == 0), stop=(k == KD - 1))
                ins.then_inc(filled, 1)

            def keys(pb, pp):
                pe.wait_ge(drained_dve, pb * ND + DVE_OF[1])
                for g in range(KD):
                    bank_free(pe, pb, K0 + g)
                    for k in range(KD):
                        cols = slice(128 * g, 128 * (g + 1))
                        ins = split3(pe, bank(pp, K0 + g)[:, 0:S2E], wk_hi[:, k, cols], wk_lo[:, k, cols],
                                     c_hi[:, k], c_lo[:, k], k == 0, k == KD - 1)
                    ins.then_inc(filled, 1)

            def values(pb, pp):
                for kt in range(3):
                    bank_free(pe, pb, V0 + kt)
                    rows = slice(KT0[kt], KT0[kt] + KT[kt])
                    for k in range(KD):
                        ins = split3(pe, bank(pp, V0 + kt)[0:KT[kt], 0:D], c_hi[:, k, rows], c_lo[:, k, rows],
                                     wv_hi[:, k], wv_lo[:, k], k == 0, k == KD - 1)
                    ins.then_inc(filled, 1)

            def scores(b, p, h):
                if h == 0:
                    pe.wait_ge(drained_act, b * NA + ACT_OF[K0 + 1])
                if h % HG == 0:
                    pe.wait_ge(qd_ready, 4 * b + 2 * (h // HG) + 2)
                reach(pe, max_ready, b * H2 + (h - 1))
                pe.matmul(ps_s[h % 2][0:S, 0:S2E], qd_hi[:, p, h // HG, h % HG, :], k_hi[:, p, h // HG],
                          start=True, stop=True).then_inc(scores_ready, 1)

            def shifted(b, p, u, kt):
                if u == 0 and kt == 0:
                    pe.wait_ge(drained_dve, b * ND + DVE_OF[K0 + 1])
                g, heads = u // 2, slice(4 * (u % 2), 4 * (u % 2) + 4)
                i, n = 3 * u + kt, KT[kt]
                reach(pe, probs_ready, b * 12 + (i - 1))
                rows = slice(KT0[kt], KT0[kt] + n)
                out = ps_t[i % 2][0:n, 0:4 * S]
                split3(pe, out, k_hi[:, p, g, rows], k_lo[:, p, g, rows],
                       qd_hi[:, p, g, heads].rearrange("p h s -> p (h s)"),
                       qd_lo[:, p, g, heads].rearrange("p h s -> p (h s)"), True, False)
                if kt == 0:
                    pe.wait_ge(diag_ready, b * 4 + (u + 1))
                pe.matmul(out, c.ones_r[0:S, 0:n], diag[:, u % 2].rearrange("p h s -> p (h s)"),
                          start=False, stop=True).then_inc(shifted_ready, 1)

            def weighted(b, p, u):
                if u == 0:
                    reach(pe, raw_copied, b)
                    pe.wait_ge(drained_dve, b * ND + ND)
                    pe.wait_ge(ones_ready, b + 1)
                for kt in range(3):
                    pe.wait_ge(probs_ready, b * 12 + (3 * u + kt + 1))
                    n = KT[kt]
                    for h in range(4):
                        ins = pe.matmul(ps_o[32 * h:32 * (h + 1), S * u:S * (u + 1)], v_ext[0:n, p, kt, 4 * u + h, :],
                                        probs[0:n, u % 2, kt, S * h:S * (h + 1)], start=(kt == 0), stop=(kt == 2))
                ins.then_inc(pv_ready, 1)

            def turn_raw(b):
                pe.wait_ge(raw_copied, b + 1)
                reach(pe, x2_ready, b)
                for u in range(4):
                    ins = pe.transpose(ps_f[0:S, 128 * u:128 * (u + 1)], o_raw[:, S * u:S * (u + 1)], c.ident[:])
                ins.then_inc(raw_turned, 1)

            def turn_out(b):
                pe.wait_ge(o_ready, b + 1)
                for k in range(KD):
                    ins = pe.transpose(ps_f[:, S * k:S * (k + 1)], o_norm[:, 128 * k:128 * (k + 1)],
                                       c.ident[0:S, 0:S])
                ins.then_inc(ot_ready, 1)

            def project(b):
                pe.wait_ge(ot_copied, b + 1)
                for k in range(KD):
                    ins = pe.matmul(ps_f[0:S, 0:D], o_t[:, S * k:S * (k + 1)], wo_sb[:, k, :],
                                    start=(k == 0), stop=(k == KD - 1))
                ins.then_inc(y_ready, 1)

            context(0, 0)
            turn_x(0, 0)
            queries(0, 0)
            keys(0, 0)
            values(0, 0)
            for h in range(4):
                scores(0, 0, h)

            def step(b, p, last):
                first = isinstance(b, int) and b == 0

                shifted(b, p, 0, 0)
                scores(b, p, 4)
                shifted(b, p, 0, 1)
                scores(b, p, 5)
                shifted(b, p, 0, 2)
                scores(b, p, 6)
                if not last:
                    context(b + 1, 1 - p)
                scores(b, p, 7)
                if not first:
                    weighted(b - 1, 1 - p, 3)

                shifted(b, p, 1, 0)
                scores(b, p, 8)
                if not last:
                    turn_x(b + 1, 1 - p)
                shifted(b, p, 1, 1)
                scores(b, p, 9)
                if not last:
                    queries(b + 1, 1 - p)
                shifted(b, p, 1, 2)
                scores(b, p, 10)
                if not first:
                    turn_raw(b - 1)
                scores(b, p, 11)
                weighted(b, p, 0)
                if not last:
                    keys(b + 1, 1 - p)

                shifted(b, p, 2, 0)
                scores(b, p, 12)
                shifted(b, p, 2, 1)
                scores(b, p, 13)
                shifted(b, p, 2, 2)
                scores(b, p, 14)
                if not first:
                    turn_out(b - 1)
                scores(b, p, 15)
                weighted(b, p, 1)
                if not last:
                    values(b + 1, 1 - p)

                for kt in range(3):
                    shifted(b, p, 3, kt)
                    if not last:
                        scores(b + 1, 1 - p, kt)
                if not first:
                    project(b - 1)
                if not last:
                    scores(b + 1, 1 - p, 3)
                weighted(b, p, 2)

            paired(pe, step)
            weighted(B - 1, 1, 3)
            turn_raw(B - 1)
            turn_out(B - 1)
            project(B - 1)


def route(nc, c, centT, xs):
    with ExitStack() as ctx:
        def sb(name, shape, dt=F32):
            return ctx.enter_context(nc.sbuf_tensor(name, shape, dt))

        def psum(name, shape, dt=F32):
            return ctx.enter_context(nc.psum_tensor(name, shape, dt))

        def sem(name):
            return ctx.enter_context(nc.semaphore(name))

        MAXT = (B * S + T - 1) // T
        cent = sb("cent", [128, KD, E])
        stats = sb("stats3", [S, B, 6])
        mv = sb("mv3", [S, B, 2])
        var_eps = sb("var_eps3", [S, B])
        rstd = sb("rstd3", [S, B])
        feats = sb("feats3", [S, 2, QUAD, D])
        f_t = sb("f_t3", [128, 2, KD, QT_TOK])
        aff = sb("aff", [S, B, E])
        top = sb("top", [S, B])
        best = sb("best", [S, B, E])
        onehot = sb("onehot", [S, B, E])
        first_w = sb("first_w", [S, E])
        nan_w = sb("nan_w", [S, E])
        steps = sb("steps", [S, MAXT])
        tile_no = sb("tile_no", [1, TILES + 1])
        scan = [sb(f"scan{i}", [S, B, E]) for i in range(2)]
        totals = sb("totals", [S, B, E])
        more = sb("more", [S, E, MAXT])
        n_tiles = sb("n_tiles", [S, E])
        ends = [sb(f"ends{i}", [S, E]) for i in range(2)]
        start = sb("start", [S, E])
        pos = sb("pos", [S, B, E])
        slot_f = sb("slot_f", [S, B])
        slot = sb("slot", [S, B], U32)
        past = sb("past", [1, TILES + 1, E])
        expert_f = sb("expert_f", [1, TILES + 1])

        ps_x = [psum(f"psc_x{i}", [128, 512]) for i in range(4)]
        ps_a = [psum(f"psc_a{i}", [128, 512]) for i in range(2)]
        ps_b = psum("psc_b", [128, 512])
        ps_n = psum("psc_n", [128, 512])

        cent_loaded = sem("cent_loaded")
        tables_ready = sem("tables_ready")
        stats_ready = sem("stats3_ready")
        mv_ready = sem("mv3_ready")
        eps_added = sem("eps3_added")
        rstd_ready = sem("rstd3_ready")
        feats_ready = sem("feats3_ready")
        turned = sem("turned3")
        copied = sem("copied3")
        aff_ready = sem("aff_ready")
        aff_copied = sem("aff_copied")
        chain = sem("route_chain")
        onehot_ready = sem("onehot_ready")
        before_ready = sem("before_ready")
        slot_ready = sem("slot_ready")
        routed = sem("routed")

        block = ctx.enter_context(nc.Block())

        @block.sync
        def _(sp):
            sp.dma_start(cent[:], centT.rearrange("(k p) e -> p k e", p=128)).then_inc(cent_loaded, 16)

        @block.gpsimd
        def _(pool):
            pool.iota(c.x[:, :, D:ROWW].rearrange("s b o -> s (b o)"), pattern=[[S, B]], base=0, channel_multiplier=1,
                      allow_small_or_imprecise_dtypes=True).then_inc(tables_ready, 1)
            pool.iota(first_w[:], pattern=[[-1, E]], base=E, channel_multiplier=0,
                      allow_small_or_imprecise_dtypes=True).then_inc(tables_ready, 1)
            pool.memset(nan_w[:, 0:1], 0.5).then_inc(tables_ready, 1)
            pool.memset(nan_w[:, 1:E], 0.0).then_inc(tables_ready, 1)
            pool.iota(steps[:], pattern=[[T, MAXT]], base=0, channel_multiplier=0,
                      allow_small_or_imprecise_dtypes=True).then_inc(tables_ready, 1)
            pool.iota(tile_no[:], pattern=[[1, TILES + 1]], base=0, channel_multiplier=0,
                      allow_small_or_imprecise_dtypes=True).then_inc(tables_ready, 1)
            pool.wait_ge(mv_ready, B)
            pool.tensor_scalar(var_eps[:], mv[:, :, 1], EPS, None, ALU.add).then_inc(eps_added, 1)
            pool.wait_ge(eps_added, 1)
            pool.tensor_tensor(rstd[:], var_eps[:], c.minus_half[0:S, :], ALU.pow).then_inc(rstd_ready, 1)
            pool.wait_ge(slot_ready, 1)
            pool.wait_ge(c.xs_cleared, 16)
            pool.wait_ge(tables_ready, 1)
            for b in range(B):
                pool.indirect_dma_start(out=xs, out_offset=bass.IndirectOffsetOnAxis(ap=slot[:, b:b + 1], axis=0),
                                        in_=c.x[:, b, :], in_offset=None).then_inc(routed, 16)
            pool.wait_ge(routed, 16 * B)

        @block.scalar
        def _(act):
            for q in range(QUADS):
                act.wait_ge(turned, q + 1)
                if q >= 2:
                    act.wait_ge(aff_ready, q - 1)
                for k in range(KD):
                    ins = act.copy(f_t[:, q % 2, k], ps_x[2 * (q % 2) + k][:, 0:QT_TOK])
                ins.then_inc(copied, 1)

        @block.tensor
        def _(pe):
            def turn(q):
                pe.wait_ge(feats_ready, q + 1)
                if q >= 2:
                    pe.wait_ge(copied, q - 1)
                for k in range(KD):
                    for i in range(QUAD):
                        ins = pe.transpose(ps_x[2 * (q % 2) + k][:, S * i:S * (i + 1)],
                                           feats[:, q % 2, i, 128 * k:128 * (k + 1)], c.ident[0:S, 0:S])
                ins.then_inc(turned, 1)

            def affinity(q):
                pe.wait_ge(copied, q + 1)
                if q >= 2:
                    pe.wait_ge(aff_copied, q - 1)
                for i in range(QUAD):
                    for k in range(KD):
                        ins = pe.matmul(ps_a[q % 2][0:S, E * i:E * (i + 1)], f_t[:, q % 2, k, S * i:S * (i + 1)],
                                        cent[:, k, :], start=(k == 0), stop=(k == KD - 1))
                ins.then_inc(aff_ready, 1)

            pe.wait_ge(cent_loaded, 16)
            turn(0)
            for q in range(QUADS):
                if q + 1 < QUADS:
                    turn(q + 1)
                affinity(q)
            pe.wait_ge(onehot_ready, 1)
            one = onehot[:].rearrange("s b e -> s (b e)")
            pe.matmul(ps_b[0:S, 0:B * E], c.before[:], one, start=True, stop=True)
            pe.matmul(ps_n[0:S, 0:B * E], c.ones_f[0:S, 0:S], one, start=True, stop=True).then_inc(before_ready, 1)

        @block.vector
        def _(dve):
            for b in range(B):
                dve.bn_stats(stats[:, b], c.x[:, b, 0:D]).then_inc(stats_ready, 1)
            for b in range(B):
                dve.wait_ge(stats_ready, b + 1)
                dve.bn_aggr(mv[:, b], stats[:, b]).then_inc(mv_ready, 1)
            dve.wait_ge(rstd_ready, 1)
            def collect(q):
                dve.wait_ge(aff_ready, q + 1)
                dve.tensor_copy(aff[:, QUAD * q:QUAD * (q + 1)],
                                ps_a[q % 2][0:S, 0:QUAD * E].rearrange("p (b e) -> p b e", e=E)).then_inc(aff_copied, 1)

            for q in range(QUADS):
                if q >= 2:
                    dve.wait_ge(turned, q - 1)
                for i in range(QUAD):
                    b = QUAD * q + i
                    ins = dve.tensor_scalar(feats[:, q % 2, i], c.x[:, b, 0:D], mv[:, b, 0:1], rstd[:, b:b + 1],
                                            ALU.subtract, ALU.mult)
                ins.then_inc(feats_ready, 1)
                if q >= 1:
                    collect(q - 1)
            collect(QUADS - 1)

            n = [0]

            def link(ins):
                n[0] += 1
                ins.then_inc(chain, 1)
                dve.wait_ge(chain, n[0])

            def over_e(t):
                return t.unsqueeze(2).to_broadcast([S, B, E])

            def over_b(t):
                return t.unsqueeze(1).to_broadcast([S, B, E])

            dve.wait_ge(aff_copied, QUADS)
            dve.wait_ge(tables_ready, 6)
            link(dve.tensor_reduce(top[:], aff[:], AX_X, ALU.max))
            link(dve.tensor_tensor(best[:], aff[:], over_e(top[:]), ALU.is_ge))
            link(dve.tensor_tensor(best[:], best[:], over_b(first_w[:]), ALU.mult))
            link(dve.tensor_tensor(best[:], best[:], over_b(nan_w[:]), ALU.add))
            link(dve.tensor_reduce(top[:], best[:], AX_X, ALU.max))
            dve.tensor_tensor(onehot[:], best[:], over_e(top[:]), ALU.is_equal).then_inc(onehot_ready, 1)
            dve.wait_ge(before_ready, 1)
            link(dve.tensor_copy(totals[:], ps_n[0:S, 0:B * E].rearrange("p (b e) -> p b e", e=E)))
            src, step, k = totals, 1, 0
            while step < B:
                dst = scan[k % 2]
                dve.tensor_copy(dst[:, 0:step], src[:, 0:step])
                link(dve.tensor_tensor(dst[:, step:B], src[:, step:B], src[:, 0:B - step], ALU.add))
                src, step, k = dst, 2 * step, k + 1
            link(dve.tensor_tensor(more[:], src[:, B - 1].unsqueeze(2).to_broadcast([S, E, MAXT]),
                                   steps[:].unsqueeze(1).to_broadcast([S, E, MAXT]), ALU.is_gt))
            link(dve.tensor_reduce(n_tiles[:], more[:], AX_X, ALU.add))
            end, step, j = n_tiles, 1, 0
            while step < E:
                dst = ends[j % 2]
                dve.tensor_copy(dst[:, 0:step], end[:, 0:step])
                link(dve.tensor_tensor(dst[:, step:E], end[:, step:E], end[:, 0:E - step], ALU.add))
                end, step, j = dst, 2 * step, j + 1
            link(dve.tensor_tensor(start[:], end[:], n_tiles[:], ALU.subtract))
            link(dve.tensor_scalar(start[:], start[:], float(T), None, ALU.mult))
            link(dve.tensor_tensor(pos[:], src[:], totals[:], ALU.subtract))
            link(dve.tensor_tensor(pos[:], ps_b[0:S, 0:B * E].rearrange("p (b e) -> p b e", e=E), pos[:], ALU.add))
            link(dve.tensor_tensor(pos[:], pos[:], over_b(start[:]), ALU.add))
            link(dve.tensor_tensor(pos[:], pos[:], onehot[:], ALU.mult))
            link(dve.tensor_reduce(slot_f[:], pos[:], AX_X, ALU.add))
            dve.tensor_copy(slot[:], slot_f[:]).then_inc(slot_ready, 1)
            link(dve.tensor_tensor(past[:], end[0:1].unsqueeze(1).to_broadcast([1, TILES + 1, E]),
                                   tile_no[:].unsqueeze(2).to_broadcast([1, TILES + 1, E]), ALU.is_le))
            link(dve.tensor_reduce(expert_f[:], past[:], AX_X, ALU.add))
            link(dve.tensor_scalar(expert_f[:], expert_f[:], float(E - 1), None, ALU.min))
            dve.tensor_copy(c.tile_expert[:], expert_f[:])


def experts(nc, c, xs, w1, w2, gamma, beta, b1, b2, centroids, out):
    with ExitStack() as ctx:
        def sb(name, shape, dt=F32):
            return ctx.enter_context(nc.sbuf_tensor(name, shape, dt))

        def psum(name, shape, dt=F32):
            return ctx.enter_context(nc.psum_tensor(name, shape, dt))

        def sem(name):
            return ctx.enter_context(nc.semaphore(name))

        NH = T // 128
        w1_sb = sb("w1_sb", [128, 2, KD, F])
        w2_sb = sb("w2_sb", [128, 2, NF, D])
        gam = sb("gam", [128, KD, E])
        bet = sb("bet", [128, KD, E])
        b1_sb = sb("b1_sb", [128, NF, E])
        b2_sb = sb("b2_sb", [128, E, D])
        cen = sb("cen", [128, E, D])
        rows = sb("rows", [128, 2, NH, ROWW])
        stats = sb("stats4", [128, NH, 6])
        mv = sb("mv4", [128, NH, 2])
        var_eps = sb("var_eps4", [128, NH])
        rstd = sb("rstd4", [128, NH])
        feats = sb("feats4", [128, NH, D])
        xhat = sb("xhat", [128, NH, D])
        prod = sb("prod", [128, NH, D])
        z = sb("z", [128, NH])
        ez = sb("ez", [128, NH])
        alpha = sb("alpha", [128, 2, NH])
        xf = sb("xf", [128, 2, NH, D])
        token = sb("token", [128, 2, NH], U32)
        h_in = sb("h_in", [128, 2, KD, T])
        hid = sb("hid", [128, NF, T])
        y = sb("y", [128, NH, D])
        res = sb("res", [128, 2, NH, D])

        ps_x = psum("psd_x", [128, KD * T])
        ps_h = [psum(f"psd_h{i}", [128, 512]) for i in range(4)]
        ps_y = [psum(f"psd_y{i}", [128, 512]) for i in range(NH)]

        act_passed = sem("act_passed4")
        dve_passed = sem("dve_passed4")
        pool_passed = sem("pool_passed4")
        tables = sem("tables4")
        w_loaded = [sem(f"w4_loaded{p}") for p in range(2)]
        rows_loaded = [sem(f"rows4_loaded{p}") for p in range(2)]
        stats_ready = sem("stats4_ready")
        mv_ready = sem("mv4_ready")
        eps_added = sem("eps4_added")
        rstd_ready = sem("rstd4_ready")
        feats_ready = sem("feats4_ready")
        xhat_ready = sem("xhat_ready")
        prod_ready = sem("prod_ready")
        z_ready = sem("z_ready")
        ez_ready = sem("ez_ready")
        alpha_step = sem("alpha_step")
        xf_ready = sem("xf_ready")
        token_ready = sem("token_ready")
        turned = sem("turned4")
        h_in_ready = sem("h_in_ready")
        hid_filled = sem("hid_filled")
        hid_act = sem("hid_act")
        hid_dve = sem("hid_dve")
        y_filled = sem("y_filled")
        y_ready = sem("y4_ready")
        res_ready = sem("res_ready")
        scattered = [sem(f"scattered{p}") for p in range(2)]

        def over_tiles(eng, emit):
            emit(0, 0, False)
            emit(1, 1, False)
            with eng.Fori(1, TILES // 2 - 1) as i:
                emit(i * 2, 0, False)
                emit(i * 2 + 1, 1, False)
            emit(TILES - 2, 0, False)
            emit(TILES - 1, 1, True)

        def expert_of(eng, j):
            return eng.value_load(c.tile_expert[0:1, j:j + 1] if isinstance(j, int)
                                  else c.tile_expert[0:1, bass.ds(j, 1)], min_val=0, max_val=E - 1)

        block = ctx.enter_context(nc.Block())

        @block.sync
        def _(sp):
            def load_rows(j, p):
                reach(sp, xf_ready, j - 1)
                reach(sp, token_ready, j - 1)
                src = xs[j * T:(j + 1) * T, :] if isinstance(j, int) else xs[bass.ds(j * T, T), :]
                sp.dma_start(rows[:, p], src.rearrange("(t r) d -> r t d", r=128)).then_inc(rows_loaded[p], 16)

            load_rows(0, 0)
            sp.dma_start(gam[:], gamma).then_inc(tables, 16)
            sp.dma_start(bet[:], beta).then_inc(tables, 16)
            sp.dma_start(b1_sb[:], b1).then_inc(tables, 16)
            sp.dma_start(cen[:], centroids.rearrange("(o e) d -> o e d", o=1).to_broadcast([128, E, D])
                         ).then_inc(tables, 16)
            sp.dma_start(b2_sb[:], b2.rearrange("(o e) d -> o e d", o=1).to_broadcast([128, E, D])
                         ).then_inc(tables, 16)

            def load(j, p, last):
                e = expert_of(sp, j)
                reach(sp, y_filled, NH * (j - 1))
                sp.dma_start(w1_sb[:, p], w1[bass.ds(e, 1)].rearrange("o (k p) n -> p (o k) n", p=128)
                             ).then_inc(w_loaded[p], 16)
                sp.dma_start(w2_sb[:, p], w2[bass.ds(e, 1)].rearrange("o (k p) n -> p (o k) n", p=128)
                             ).then_inc(w_loaded[p], 16)
                if not last:
                    load_rows(j + 1, 1 - p)

            over_tiles(sp, load)

        @block.gpsimd
        def _(pool):
            def inverse_root(n):
                pool.wait_ge(mv_ready, n * NH + NH)
                pool.sem_inc(pool_passed, 1)
                pool.tensor_scalar(var_eps[:], mv[:, :, 1], EPS, None, ALU.add).then_inc(eps_added, 1)
                pool.wait_ge(eps_added, n + 1)
                pool.tensor_tensor(rstd[:], var_eps[:], c.minus_half[:, 0:NH], ALU.pow).then_inc(rstd_ready, 1)

            def prepare(j, p):
                inverse_root(j * 2)
                pool.wait_ge(feats_ready, j + 1)
                reach(pool, res_ready, NH * (j - 1))
                pool.tensor_tensor(xf[:, p], rows[:, p, :, 0:D], feats[:], ALU.add).then_inc(xf_ready, 1)
                inverse_root(j * 2 + 1)

            def finish(j, p):
                for t in range(NH):
                    pool.wait_ge(res_ready, NH * j + (t + 1))
                    pool.sem_inc(pool_passed, 1)
                    pool.indirect_dma_start(
                        out=out, out_offset=bass.IndirectOffsetOnAxis(ap=token[:, p, t:t + 1], axis=0),
                        in_=res[:, p, t, :], in_offset=None, bounds_check=B * S - 1,
                        oob_is_err=False).then_inc(scattered[p], 16)

            prepare(0, 0)

            def step(j, p, last):
                if not last:
                    prepare(j + 1, 1 - p)
                finish(j, p)

            over_tiles(pool, step)
            for p in range(2):
                pool.wait_ge(scattered[p], 16 * NH * (TILES // 2))

        @block.scalar
        def _(act):
            act.wait_ge(tables, 16 * 5)

            def prepare(j, p):
                e = expert_of(act, j)
                act.wait_ge(turned, j + 1)
                act.sem_inc(act_passed, 1)
                for k in range(KD):
                    ins = act.activation(h_in[:, p, k], ps_x[:, T * k:T * (k + 1)], ACT.Identity,
                                         bias=bet[:, k, bass.ds(e, 1)], scale=gam[:, k, bass.ds(e, 1)])
                ins.then_inc(h_in_ready, 1)
                act.wait_ge(z_ready, j + 1)
                act.activation(ez[:], z[:], ACT.Exp, scale=-1.0).then_inc(ez_ready, 1)

            prepare(0, 0)

            def step(j, p, last):
                e = expert_of(act, j)
                for f in range(0, NF, 2):
                    act.wait_ge(hid_filled, NF * j + (f + 1))
                    if f == 0:
                        reach(act, y_filled, NH * j)
                    act.sem_inc(act_passed, 1)
                    act.activation(hid[:, f], ps_h[f % 4][:, 0:T], ACT.Relu,
                                   bias=b1_sb[:, f, bass.ds(e, 1)]).then_inc(hid_act, 1)
                if not last:
                    prepare(j + 1, 1 - p)

            over_tiles(act, step)

        @block.vector
        def _(dve):
            dve.wait_ge(tables, 16 * 5)

            def moments(n, src):
                for t in range(NH):
                    dve.bn_stats(stats[:, t], src[:, t, 0:D]).then_inc(stats_ready, 1)
                dve.wait_ge(stats_ready, n * NH + NH)
                dve.sem_inc(dve_passed, 1)
                for t in range(NH):
                    dve.bn_aggr(mv[:, t], stats[:, t]).then_inc(mv_ready, 1)

            def normalize(n, dst, src, ready):
                dve.wait_ge(rstd_ready, n + 1)
                for t in range(NH):
                    ins = dve.tensor_scalar(dst[:, t], src[:, t, 0:D], mv[:, t, 0:1], rstd[:, t:t + 1], ALU.subtract,
                                            ALU.mult)
                ins.then_inc(ready, 1)

            def features(j, p):
                dve.wait_ge(rows_loaded[p], (j - p) * 8 + 16)
                reach(dve, xf_ready, j)
                moments(j * 2, rows[:, p])

            def again(j, p):
                normalize(j * 2, feats, rows[:, p], feats_ready)
                dve.wait_ge(feats_ready, j + 1)
                dve.sem_inc(dve_passed, 1)
                moments(j * 2 + 1, feats)

            def center(j, p):
                reach(dve, turned, j)
                normalize(j * 2 + 1, xhat, feats, xhat_ready)

            def weigh(j, p):
                e = expert_of(dve, j)
                reach(dve, ez_ready, j)
                dve.tensor_tensor(prod[:], feats[:], cen[:, bass.ds(e, 1), :].to_broadcast([128, NH, D]),
                                  ALU.mult).then_inc(prod_ready, 1)
                dve.wait_ge(prod_ready, j + 1)
                dve.tensor_reduce(z[:], prod[:], AX_X, ALU.add).then_inc(z_ready, 1)
                reach(dve, res_ready, NH * (j - 1))
                dve.wait_ge(rows_loaded[p], (j - p) * 8 + 16)
                reach(dve, scattered[p], (j - p) * 16)
                dve.tensor_copy(token[:, p], rows[:, p, :, D]).then_inc(token_ready, 1)
                dve.wait_ge(ez_ready, j + 1)
                dve.tensor_scalar(ez[:], ez[:], 1.0, None, ALU.add).then_inc(alpha_step, 1)
                dve.wait_ge(alpha_step, 2 * j + 1)
                dve.reciprocal(alpha[:, p], ez[:]).then_inc(alpha_step, 1)

            features(0, 0)
            again(0, 0)
            center(0, 0)
            weigh(0, 0)

            def step(j, p, last):
                if not last:
                    features(j + 1, 1 - p)
                e = expert_of(dve, j)
                for f in range(1, NF, 2):
                    dve.wait_ge(hid_filled, NF * j + (f + 1))
                    if f == 1:
                        reach(dve, y_filled, NH * j)
                    dve.tensor_scalar(hid[:, f], ps_h[f % 4][:, 0:T], b1_sb[:, f, bass.ds(e, 1)], 0.0, ALU.add,
                                      ALU.max).then_inc(hid_dve, 1)
                    if f == 1 and not last:
                        again(j + 1, 1 - p)
                    if f == 5 and not last:
                        center(j + 1, 1 - p)
                if not last:
                    weigh(j + 1, 1 - p)
                e = expert_of(dve, j)
                dve.wait_ge(alpha_step, 2 * j + 2)
                dve.wait_ge(xf_ready, j + 1)
                reach(dve, scattered[p], (j - p) * 16)
                for t in range(NH):
                    dve.wait_ge(y_filled, NH * j + (t + 1))
                    dve.tensor_tensor(y[:, t], ps_y[t][:, 0:D], b2_sb[:, bass.ds(e, 1), :].rearrange(
                        "p o d -> p (o d)"), ALU.add).then_inc(y_ready, 1)
                for t in range(NH):
                    dve.wait_ge(y_ready, NH * j + (t + 1))
                    dve.scalar_tensor_tensor(out=res[:, p, t], in0=y[:, t], scalar=alpha[:, p, t:t + 1],
                                             in1=xf[:, p, t], op0=ALU.mult, op1=ALU.add).then_inc(res_ready, 1)

            over_tiles(dve, step)

        @block.tensor
        def _(pe):
            def turn(j, p):
                pe.wait_ge(xhat_ready, j + 1)
                reach(pe, h_in_ready, j)
                for k in range(KD):
                    for t in range(NH):
                        ins = pe.transpose(ps_x[:, T * k + 128 * t:T * k + 128 * (t + 1)],
                                           xhat[:, t, 128 * k:128 * (k + 1)], c.ident[:])
                ins.then_inc(turned, 1)

            turn(0, 0)

            def step(j, p, last):
                pe.wait_ge(w_loaded[p], (j - p) * 16 + 32)
                pe.wait_ge(h_in_ready, j + 1)
                for f in range(NF):
                    reach(pe, hid_act if f % 2 == 0 else hid_dve, NF // 2 * j + (f // 2 - 1))
                    for k in range(KD):
                        ins = pe.matmul(ps_h[f % 4][:, 0:T], w1_sb[:, p, k, 128 * f:128 * (f + 1)], h_in[:, p, k],
                                        start=(k == 0), stop=(k == KD - 1))
                    ins.then_inc(hid_filled, 1)
                if not last:
                    turn(j + 1, 1 - p)
                pe.wait_ge(hid_act, NF // 2 * (j + 1))
                pe.wait_ge(hid_dve, NF // 2 * (j + 1))
                reach(pe, y_ready, NH * j)
                for t in range(NH):
                    for f in range(NF):
                        ins = pe.matmul(ps_y[t][:, 0:D], hid[:, f, 128 * t:128 * (t + 1)], w2_sb[:, p, f, :],
                                        start=(f == 0), stop=(f == NF - 1))
                    ins.then_inc(y_filled, 1)

            over_tiles(pe, step)


def build(nc, ins, out):
    c = Shared()
    with ExitStack() as ctx:
        def sb(name, shape, dt=F32):
            return ctx.enter_context(nc.sbuf_tensor(name, shape, dt))

        c.x = sb("x_all", [S, B, ROWW])
        c.ident = sb("ident", [128, 128])
        c.neg_ident = sb("neg_ident", [128, 128])
        c.ones_f = sb("ones_f", [128, 128])
        c.ones_r = sb("ones_r", [128, 128], F32R)
        c.before = sb("before", [S, S])
        c.head_of = sb("head_of", [128, HG])
        c.minus_half = sb("minus_half", [128, B])
        v_dram = nc.dram_tensor("v_rows", (B, S, O1), F32, kind="Internal").ap()
        xs = nc.dram_tensor("routed_rows", (SLOTS, ROWW), F32, kind="Internal").ap()
        c.tile_expert = sb("tile_expert", [1, TILES + 1], I32)
        c.empty = sb("empty", [128, ROWW])
        c.xs_cleared = ctx.enter_context(nc.semaphore("xs_cleared"))
        constants(nc, c)
        self_attention(nc, c, ins["x"], ins["wqkT"], ins["wvT"], ins["woT"], v_dram, xs)
        cross_attention(nc, c, ins["context"], ins["mask"], ins["maskT"], ins["wq2T"], ins["wk2T"], ins["wv2T"],
                        ins["wo2T"], ins["bq"], ins["bk"], ins["bv"], ins["bo"])
        route(nc, c, ins["centT"], xs)
        experts(nc, c, xs, ins["w1"], ins["w2"], ins["gamma"], ins["beta"], ins["b1"], ins["b2"], ins["centroids"],
                out.rearrange("b s d -> (b s) d"))


def kernel(**inputs):
    import numpy as _np
    import concourse.bacc as _bacc
    from concourse import mybir as _mybir
    from concourse.bass_utils import run_bass_kernel_spmd as _run

    a = {k: _np.asarray(v) for k, v in inputs.items()}
    lay = {
        "x": a["x"],
        "wqkT": _np.concatenate([a["L0_attn_wq"].T, a["L0_attn_wk"].T], axis=1),
        "wvT": a["L0_attn_wv"].T,
        "woT": a["L0_attn_wo"].T,
        "context": a["ctx_1024"],
        "mask": a["mask_Bx1x1xS2_if1"].reshape(B, S2),
        "maskT": a["mask_Bx1x1xS2_if1"].reshape(B, S2).T,
        "wq2T": a["L0_xattn_Wq"].T,
        "wk2T": a["L0_xattn_Wk"].T,
        "wv2T": a["L0_xattn_Wv"].T,
        "wo2T": a["L0_xattn_Wo"].T,
        "bq": a["L0_xattn_bq"].reshape(KD, 128).T,
        "bk": a["L0_xattn_bk"].reshape(KD, 128).T,
        "bv": a["L0_xattn_bv"],
        "bo": a["L0_xattn_bo"],
        "centT": a["L0_ffn_centroids"].T,
        "centroids": a["L0_ffn_centroids"],
        "w1": a["L0_ffn_w1"],
        "w2": a["L0_ffn_w2"],
        "gamma": a["L0_ffn_gamma"].reshape(E, KD, 128).transpose(2, 1, 0),
        "beta": a["L0_ffn_beta"].reshape(E, KD, 128).transpose(2, 1, 0),
        "b1": a["L0_ffn_b1"].reshape(E, NF, 128).transpose(2, 1, 0),
        "b2": a["L0_ffn_b2"],
    }
    nc = _bacc.Bacc("TRN2", target_bir_lowering=False, num_devices=1)
    arrays, ins = {}, {}
    for name, v in lay.items():
        v = _np.ascontiguousarray(v)
        arrays[f"in_{name}"] = v
        ins[name] = nc.dram_tensor(f"in_{name}", v.shape, _mybir.dt.from_np(v.dtype), kind="ExternalInput").ap()
    out = nc.dram_tensor("out_0", (B, S, D), F32, kind="ExternalOutput").ap()
    build(nc, ins, out)
    r = _run(nc, [arrays], core_ids=[0])
    return r.results[0]["out_0"]
```

```python
from contextlib import ExitStack

import concourse.bass as bass
from concourse import mybir

F32 = mybir.dt.float32
F32R = mybir.dt.float32r
I32 = mybir.dt.int32
U32 = mybir.dt.uint32
ALU = mybir.AluOpType
ACT = mybir.ActivationFunctionType
AX_X = mybir.AxisListType.X

B, S, D = 32, 100, 256
KD = D // 128
EPS = 1e-5

H1, HD1 = 16, 64
O1 = H1 * HD1
QUAD = 4
QUADS = B // QUAD
QT_TOK = QUAD * S
GH = 4
GB = H1 // GH
GQ = QUAD * GB
ROWS = S * O1 // HD1
NT = O1 // 128

S2 = 361
S2E = S2 + 1
H2, HD2 = 16, 16
KT = [121, 121, 119]
KT0 = [0, 121, 242]
HG = 8
NEG = -1.0e30

E, F = 8, 1024
NF = F // 128
T = 256
TILES = (B * S + E * (T - 1)) // T
SLOTS = TILES * T
ROWW = D + 1
NO_TOKEN = 100000.0


def split3(pe, out, hi_l, lo_l, hi_r, lo_r, first, last):
    pe.matmul(out, hi_l, lo_r, start=first, stop=False)
    pe.matmul(out, lo_l, hi_r, start=False, stop=False)
    return pe.matmul(out, hi_l, hi_r, start=False, stop=last)


def constants(nc, c):
    with nc.semaphore("pool_step") as pool_step, nc.Block() as block:
        @block.gpsimd
        def _(pool):
            pool.memset(c.empty[:, 0:D], 0.0).then_inc(pool_step, 1)
            pool.memset(c.empty[:, D:ROWW], NO_TOKEN).then_inc(pool_step, 1)
            pool.memset(c.ident[:], 0.0).then_inc(pool_step, 1)
            pool.memset(c.neg_ident[:], 0.0).then_inc(pool_step, 1)
            pool.memset(c.minus_half[:], -0.5).then_inc(pool_step, 1)
            pool.memset(c.ones_f[:], 1.0).then_inc(pool_step, 1)
            pool.memset(c.before[:], 1.0).then_inc(pool_step, 1)
            pool.memset(c.head_of_8[:], 1.0).then_inc(pool_step, 1)
            pool.wait_ge(pool_step, 8)
            pool.affine_select(out=c.ident[:], in_=c.ident[:], compare_op=ALU.not_equal, fill=1.0, base=0,
                               pattern=[[-1, 128]], channel_multiplier=1).then_inc(pool_step, 1)
            pool.affine_select(out=c.neg_ident[:], in_=c.neg_ident[:], compare_op=ALU.not_equal, fill=-1.0, base=0,
                               pattern=[[-1, 128]], channel_multiplier=1).then_inc(pool_step, 1)
            pool.affine_select(out=c.before[:], in_=c.before[:], compare_op=ALU.is_gt, fill=0.0, base=0,
                               pattern=[[1, S]], channel_multiplier=-1).then_inc(pool_step, 1)
            pool.affine_select(out=c.head_of_8[:], in_=c.head_of_8[:], compare_op=ALU.is_ge, fill=0.0, base=0,
                               pattern=[[-HD2, HG]], channel_multiplier=1).then_inc(pool_step, 1)
            pool.wait_ge(pool_step, 12)
            pool.affine_select(out=c.head_of_8[:], in_=c.head_of_8[:], compare_op=ALU.is_ge, fill=0.0, base=HD2 - 1,
                               pattern=[[HD2, HG]], channel_multiplier=-1).then_inc(pool_step, 1)
            pool.wait_ge(pool_step, 13)
            pool.tensor_tensor(c.head_of[:], c.head_of_8[:, 0:4], c.head_of_8[:, 4:8], ALU.add).then_inc(pool_step, 1)

        @block.vector
        def _(dve):
            dve.wait_ge(pool_step, 8)
            dve.tensor_copy(c.ones_r[:], c.ones_f[:])


class Shared:
    pass


def reach(eng, semaphore, value):
    if isinstance(value, int) and value <= 0:
        return
    eng.wait_ge(semaphore, value)


def at_batch(tensor, b, cols):
    if isinstance(b, int):
        return tensor[:, b, cols]
    return tensor[:, bass.ds(b, 1), cols].rearrange("p b d -> p (b d)")


def self_attention(nc, c, x, wqkT, wvT, woT, v_dram, xs):
    with ExitStack() as ctx:
        def sb(name, shape, dt=F32):
            return ctx.enter_context(nc.sbuf_tensor(name, shape, dt))

        def psum(name, shape, dt=F32):
            return ctx.enter_context(nc.psum_tensor(name, shape, dt))

        def sem(name):
            return ctx.enter_context(nc.semaphore(name))

        PAD = 256 - 2 * S
        w_stage = sb("w_stage", [128, 2, KD, O1])
        w_hi = sb("w_hi", [128, 4, KD, O1], F32R)
        w_lo = sb("w_lo", [128, 4, KD, O1], F32R)
        stats = sb("stats", [S, QUAD, 6])
        mv = sb("mv", [S, QUAD, 2])
        var_eps = sb("var_eps", [S, QUAD])
        rstd = sb("rstd", [S, QUAD])
        xn = sb("xn", [S, QUAD, D])
        x_hi = sb("x_hi", [128, KD, QT_TOK], F32R)
        x_lo = sb("x_lo", [128, KD, QT_TOK], F32R)
        q_t = sb("q_t", [128, 2, ROWS])
        k_t = sb("k_t", [128, 2, ROWS])
        v_tok = sb("v_tok", [S, 2, O1])
        v_ext = sb("v_ext", [S, QUAD, H1, HD1 + 1])
        q_hi = sb("q_hi1", [128, 2, GH * S], F32R)
        k_pair = sb("k_pair", [128, 2, GH * 2 * S + PAD], F32R)
        row_max = sb("row_max", [S, 2, 2, GH])
        diag = sb("diag", [S, 2, GH, S], F32R)
        probs = sb("probs", [S, 2, GH * S])
        recip = sb("recip", [S, 2, GH])
        o_norm = sb("o_norm", [S, 2, GH * HD1])
        o_hi = sb("o_hi", [128, 2, ROWS // 2], F32R)
        o_lo = sb("o_lo", [128, 2, ROWS // 2], F32R)

        ps_p = [psum(f"ps_p{i}", [128, 512]) for i in range(2)]
        ps_s = [psum(f"ps_s{i}", [128, 512]) for i in range(2)]
        ps_t = [psum(f"ps_t{i}", [128, 512]) for i in range(2)]
        ps_o = [psum("ps_o", [128, 512]), ps_p[1]]
        ps_ot = psum("ps_ot", [128, 512])

        ps_y = [ps_p[0], ps_ot]

        dve_passed = sem("dve_passed_a")
        pool_passed = sem("pool_passed_a")
        x_first = sem("x_first")
        x_loaded = sem("x_loaded")
        w_loaded = [sem(f"w_loaded{i}") for i in range(4)]
        w_hi_ready = sem("w_hi_ready")
        w_lo_ready = sem("w_lo_ready")
        ones_ready = sem("ones_ready")
        stats_ready = sem("stats_ready")
        mv_ready = sem("mv_ready")
        eps_added = sem("eps_added")
        rstd_ready = sem("rstd_ready")
        xn_ready = sem("xn_ready")
        filled = sem("filled")
        drained_act = sem("drained_act")
        drained_dve = sem("drained_dve")
        v_stored = [sem(f"v_stored{i}") for i in range(QUAD)]
        v_loaded = [sem(f"v_loaded{i}") for i in range(QUAD)]
        pairs_cleared = sem("pairs_cleared")
        q_hi_ready = sem("q_hi_ready")
        k_pair_act = sem("k_pair_act")
        k_pair_dve = sem("k_pair_dve")
        scores_ready = sem("scores_ready")
        max_ready = sem("max_ready")
        diag_ready = sem("diag_ready")
        shifted_ready = sem("shifted_ready")
        probs_ready = sem("probs_ready")
        pv_ready = sem("pv_ready")
        recip_ready = sem("recip_ready")
        o_ready = sem("o_ready")
        ot_ready = sem("ot_ready")
        ot_copied_act = sem("ot_copied_act")
        ot_copied_dve = sem("ot_copied_dve")
        y_ready = sem("y_ready")
        x1_ready = sem("x1_ready")

        FQ, FV = KD, KD + 2 * NT
        FILLS = FV + 2 * QUAD


        def pair_keys(copy, r, a):
            rows = slice(64 * a, 64 * a + 64)
            out = k_pair[rows, r % 2, 0:GH * 2 * S].rearrange("p (h g j) -> p h g j", h=GH, g=2)[:, :, a, :]
            src = k_t[rows, r // GB, GH * S * (r % GB):GH * S * (r % GB + 1)]
            return copy(out, src.rearrange("p (h j) -> p h j", h=GH))

        def bank(f):
            return ps_s[f] if f < KD else ps_t[f % 2] if f < FQ + 2 else ps_p[f % 2]

        def values_in(r):
            return range(FV, FV + 4) if r < 0 else range(FV + 4 + 2 * r, FV + 6 + 2 * r) if r < 2 else ()

        ROUNDS = GQ // 2
        AHEAD = {ROUNDS + 1: (FQ, FQ + 1), ROUNDS + 2: (FQ + 2, FQ + 3)}
        TAIL = 3

        def batch_of(g):
            return 2 * (g // (2 * GB)) + g % 2

        def quarter_of(g):
            return g % (2 * GB) // 2

        def in_round(r):
            return (2 * r, 2 * r + 1) if 0 <= r < ROUNDS else ()

        def last_round_of_pair(r):
            return 0 <= r < ROUNDS and r % GB == GB - 1

        def spread(copy, f, a):
            t, dst = (f - FQ) // 2, (q_t if (f - FQ) % 2 == 0 else k_t)
            src = bank(f)[64 * a:64 * a + 64, 0:QT_TOK].rearrange("p (i s) -> p i s", s=S)
            for odd in range(2):
                out = dst[64 * odd:64 * odd + 64, :, :].rearrange("p i (s c) -> p i s c", c=H1)[:, :, :, 2 * t + a]
                ins = copy(out, src[:, odd::2, :])
            return ins

        def turned_part(g, a, odd):
            src = ps_ot[64 * a:64 * a + 64, 0:4 * S].rearrange("p (g w k two) -> p g w k two", g=2, w=2, two=2)
            base = quarter_of(g) * GH * S // 2
            hi, lo = (t[64 * odd:64 * odd + 64, :, base:base + GH * S // 2].rearrange(
                "p g (w a k) -> p g w a k", w=2, a=2)[:, :, :, a, :] for t in (o_hi, o_lo))
            return src[:, :, :, :, odd], hi, lo

        block = ctx.enter_context(nc.Block())

        @block.sync
        def _(sp):
            for q in range(QUADS):
                sp.dma_start(c.x[:, QUAD * q:QUAD * (q + 1), 0:D],
                             x[QUAD * q:QUAD * (q + 1)].rearrange("b s d -> s b d")
                             ).then_inc(x_loaded if q else x_first, 16)
            sp.wait_ge(x_loaded, 16 * (QUADS - 1))
            sp.dma_start(xs.rearrange("(k p) d -> p k d", p=128),
                         c.empty[:].unsqueeze(1).to_broadcast([128, SLOTS // 128, ROWW])).then_inc(c.xs_cleared, 16)
            with sp.Fori(0, QUADS) as q:
                for pair in (0, 2):
                    for i in (pair, pair + 1):
                        sp.wait_ge(drained_act, q * FILLS + (FV + 2 * i + 2))
                        sp.wait_ge(drained_dve, q * FILLS + (FV + 2 * i + 2))
                        sp.dma_start(v_dram[bass.ds(q * QUAD + i, 1)].rearrange("b s n -> s (b n)"),
                                     v_tok[:, i % 2, :]).then_inc(v_stored[i], 16)
                    for i in (pair, pair + 1):
                        sp.wait_ge(v_stored[i], q * 16 + 16)
                        sp.dma_start(v_ext[:, i, :, 0:HD1],
                                     v_dram[bass.ds(q * QUAD + i, 1)].rearrange(
                                         "b s n -> (b s n)").rearrange(
                                         "(h j d) -> j h d", j=S, d=HD1)).then_inc(v_loaded[i], 16)

        @block.scalar
        def _(act):
            for i, w in enumerate((wqkT[:, 0:O1], wqkT[:, O1:2 * O1], wvT, woT)):
                if i >= 2:
                    act.wait_ge(w_lo_ready, i - 1)
                act.dma_start(w_stage[:, i % 2].rearrange("p k n -> p (k n)").rearrange(
                    "p (k n) -> p k n", n=w.shape[1]), w.rearrange("(k p) n -> p k n", p=128)
                              ).then_inc(w_loaded[i], 16)
                if i >= 1:
                    act.wait_ge(w_loaded[i - 1], 16)
                    act.copy(w_hi[:, i - 1], w_stage[:, (i - 1) % 2]).then_inc(w_hi_ready, 1)
            act.wait_ge(pairs_cleared, 1)
            act.wait_ge(w_loaded[3], 16)
            act.copy(w_hi[:, 3], w_stage[:, 1]).then_inc(w_hi_ready, 1)

            def leading_bits(q):
                for k in range(KD):
                    act.wait_ge(filled, q * FILLS + (k + 1))
                    act.copy(x_hi[:, k], bank(k)[:, 0:QT_TOK]).then_inc(drained_act, 1)

            def heads_out(q, f):
                act.wait_ge(filled, q * FILLS + (f + 1))
                spread(act.copy, f, 0).then_inc(drained_act, 1)

            def round_operands(q, r):
                if r >= 2:
                    act.wait_ge(scores_ready, q * GQ + 2 * (r - 1))
                pair_keys(act.copy, r, 0).then_inc(k_pair_act, 1)
                act.copy(q_hi[:, r % 2], q_t[:, r // GB, GH * S * (r % GB):GH * S * (r % GB + 1)]
                         ).then_inc(q_hi_ready, 1)

            def quad(q, last):
                for f in range(FQ + 4, FV):
                    heads_out(q, f)
                act.wait_ge(drained_act, q * FILLS + FV)
                act.wait_ge(drained_dve, q * FILLS + FV)
                round_operands(q, 0)
                for r in range(-1, ROUNDS + TAIL):
                    for f in values_in(r):
                        i, v = (f - FV) // 2, (f - FV) % 2
                        act.wait_ge(filled, q * FILLS + (f + 1))
                        if i >= 2:
                            act.wait_ge(v_stored[i - 2], q * 16 + 16)
                        act.copy(v_tok[0:64, i % 2, 512 * v:512 * (v + 1)], bank(f)[0:64, :]).then_inc(drained_act, 1)
                    if r == ROUNDS and not last:
                        leading_bits(q + 1)
                    for f in AHEAD.get(r, ()):
                        if not last:
                            heads_out(q + 1, f)
                    for g in in_round(r - 1):
                        act.wait_ge(shifted_ready, q * GQ + (g + 1))
                        if g >= 2:
                            act.wait_ge(pv_ready, q * GQ + (g - 1))
                        act.activation(probs[:, g % 2], ps_t[g % 2][0:S, 0:GH * S], ACT.Exp,
                                       scale=HD1 ** -0.5).then_inc(probs_ready, 1)
                    for g in in_round(r - 2)[0:1]:
                        act.wait_ge(ot_ready, q * GQ + (g + 2))
                        if g == 2 * GB:
                            act.wait_ge(y_ready, q * QUAD + 2)
                        for a in range(2):
                            for odd in range(2):
                                src, hi, _ = turned_part(g, a, odd)
                                act.copy(hi, src).then_inc(ot_copied_act, 1)
                    if -1 <= r < ROUNDS - 2:
                        round_operands(q, r + 2)

            leading_bits(0)
            for f in range(FQ, FQ + 4):
                heads_out(0, f)
            with act.Fori(0, QUADS - 1) as q:
                quad(q, False)
            quad(QUADS - 1, True)

        @block.gpsimd
        def _(pool):
            pool.memset(v_ext[:, :, :, HD1:HD1 + 1], 1.0).then_inc(ones_ready, 1)
            pool.memset(k_pair[:].bitcast(F32), 0.0).then_inc(pairs_cleared, 1)

            def inverse_root(q):
                pool.wait_ge(mv_ready, q * QUAD + QUAD)
                pool.sem_inc(pool_passed, 1)
                pool.tensor_scalar(var_eps[:], mv[:, :, 1], EPS, None, ALU.add).then_inc(eps_added, 1)
                pool.wait_ge(eps_added, q + 1)
                pool.tensor_tensor(rstd[:], var_eps[:], c.minus_half[0:S, 0:QUAD], ALU.pow).then_inc(rstd_ready, 1)

            inverse_root(0)

            def quad(q, last):
                if not last:
                    inverse_root(q + 1)
                for g in range(GQ):
                    pool.wait_ge(max_ready, q * GQ + (g - g % 2 + 2))
                    if g >= 2:
                        pool.wait_ge(shifted_ready, q * GQ + (g - 1))
                    pool.tensor_tensor(diag[:, g % 2],
                                       c.neg_ident[0:S, 0:S].unsqueeze(1).to_broadcast([S, GH, S]),
                                       row_max[:, g // 2 % 2, g % 2].unsqueeze(2).to_broadcast([S, GH, S]),
                                       ALU.mult).then_inc(diag_ready, 1)

            with pool.Fori(0, QUADS - 1) as q:
                quad(q, False)
            quad(QUADS - 1, True)

        @block.vector
        def _(dve):
            def add_stats(q, i):
                dve.bn_stats(stats[:, i], at_batch(c.x, q * QUAD + i, slice(0, D))).then_inc(stats_ready, 1)

            def moments(q):
                dve.wait_ge(stats_ready, q * QUAD + QUAD)
                dve.sem_inc(dve_passed, 1)
                for i in range(QUAD):
                    dve.bn_aggr(mv[:, i], stats[:, i]).then_inc(mv_ready, 1)

            def low_bits(i):
                dve.wait_ge(w_hi_ready, i + 1)
                dve.tensor_tensor(w_lo[:, i], w_stage[:, i % 2], w_hi[:, i].bitcast(F32),
                                  ALU.subtract).then_inc(w_lo_ready, 1)

            dve.wait_ge(x_first, 16)
            for i in range(QUAD):
                add_stats(0, i)
            moments(0)
            low_bits(0)

            def normalize(q, i):
                dve.wait_ge(rstd_ready, q + 1)
                dve.tensor_scalar(xn[:, i], at_batch(c.x, q * QUAD + i, slice(0, D)), mv[:, i, 0:1],
                                  rstd[:, i:i + 1], ALU.subtract, ALU.mult).then_inc(xn_ready, 1)

            for i in range(QUAD):
                normalize(0, i)
            low_bits(1)
            low_bits(2)
            low_bits(3)
            dve.wait_ge(x_loaded, 16 * (QUADS - 1))
            dve.wait_ge(pairs_cleared, 1)

            def trailing_bits(q):
                for k in range(KD):
                    dve.wait_ge(drained_act, q * FILLS + (k + 1))
                    dve.tensor_tensor(x_lo[:, k], bank(k)[:, 0:QT_TOK], x_hi[:, k].bitcast(F32),
                                      ALU.subtract).then_inc(drained_dve, 1)

            def heads_out(q, f):
                dve.wait_ge(filled, q * FILLS + (f + 1))
                spread(dve.tensor_copy, f, 1).then_inc(drained_dve, 1)

            def quad(q, last):
                for f in range(FQ + 4, FV):
                    heads_out(q, f)
                    n = f - (FQ + 4)
                    if n < QUAD and not last:
                        add_stats(q + 1, n)
                    if n == QUAD and not last:
                        moments(q + 1)
                    if FV - QUAD <= f and not last:
                        normalize(q + 1, f - (FV - QUAD))
                dve.wait_ge(drained_act, q * FILLS + FV)
                dve.wait_ge(drained_dve, q * FILLS + FV)
                pair_keys(dve.tensor_copy, 0, 1).then_inc(k_pair_dve, 1)
                for r in range(-1, ROUNDS + TAIL):
                    for n, g in enumerate(in_round(r)):
                        dve.wait_ge(scores_ready, q * GQ + (g + 1))
                        if r >= 2:
                            dve.wait_ge(diag_ready, q * GQ + 2 * (r - 1))
                        dve.reduce_max(row_max[:, r % 2, :, 2 * n:2 * n + 2].rearrange("p g h -> p h g"),
                                       ps_s[n][0:S, :].rearrange("p (h j) -> p h j", h=2)[:, :, 0:2 * S].rearrange(
                                           "p h (g j) -> p h g j", g=2), AX_X).then_inc(max_ready, 1)
                    for g in in_round(r - 3)[0:1]:
                        if g == 2 * GB:
                            dve.wait_ge(y_ready, q * QUAD + 2)
                        for a in range(2):
                            dve.wait_ge(ot_copied_act, q * 2 * GQ + (2 * g + 2 * a + 2))
                            for odd in range(2):
                                src, hi, lo = turned_part(g, a, odd)
                                dve.tensor_tensor(lo, src, hi.bitcast(F32), ALU.subtract).then_inc(ot_copied_dve, 1)
                    for f in values_in(r):
                        i, v = (f - FV) // 2, (f - FV) % 2
                        dve.wait_ge(filled, q * FILLS + (f + 1))
                        if i >= 2:
                            dve.wait_ge(v_stored[i - 2], q * 16 + 16)
                        dve.tensor_copy(v_tok[64:S, i % 2, 512 * v:512 * (v + 1)],
                                        bank(f)[64:S, :]).then_inc(drained_dve, 1)
                    for g in in_round(r - 2):
                        dve.wait_ge(pv_ready, q * GQ + (g + 1))
                        o = ps_o[g % 2][0:S, 0:GH * (HD1 + 1)].rearrange("p (h d) -> p h d", h=GH)
                        dve.reciprocal(recip[:, g % 2], o[:, :, HD1]).then_inc(recip_ready, 1)
                        dve.wait_ge(recip_ready, q * GQ + (g + 1))
                        if g >= 2:
                            dve.wait_ge(ot_ready, q * GQ + (g - 1))
                        dve.tensor_tensor(o_norm[:, g % 2].rearrange("p (h d) -> p h d", h=GH), o[:, :, 0:HD1],
                                          recip[:, g % 2].unsqueeze(2).to_broadcast([S, GH, HD1]),
                                          ALU.mult).then_inc(o_ready, 1)
                    if r == ROUNDS and not last:
                        trailing_bits(q + 1)
                    for f in AHEAD.get(r, ()):
                        if not last:
                            heads_out(q + 1, f)
                    for g in in_round(r - 3):
                        if last_round_of_pair(r - 3):
                            i = batch_of(g)
                            dve.wait_ge(y_ready, q * QUAD + (i - i % 2 + 2))
                            xb = at_batch(c.x, q * QUAD + i, slice(0, D))
                            dve.tensor_tensor(xb, ps_y[i // 2][0:S, D * (i % 2):D * (i % 2 + 1)], xb,
                                              ALU.add).then_inc(x1_ready, 1)
                    if -1 <= r < ROUNDS - 2:
                        pair_keys(dve.tensor_copy, r + 2, 1).then_inc(k_pair_dve, 1)

            trailing_bits(0)
            for f in range(FQ, FQ + 4):
                heads_out(0, f)
            with dve.Fori(0, QUADS - 1) as q:
                quad(q, False)
            quad(QUADS - 1, True)

        @block.tensor
        def _(pe):
            pe.wait_ge(ones_ready, 1)

            def turn_x(q):
                pe.wait_ge(xn_ready, q * QUAD + QUAD)
                for k in range(KD):
                    for i in range(QUAD):
                        ins = pe.transpose(bank(k)[:, S * i:S * (i + 1)], xn[:, i, 128 * k:128 * (k + 1)],
                                           c.ident[0:S, 0:S])
                    ins.then_inc(filled, 1)

            def heads_in(q, f):
                t, qk = (f - FQ) // 2, (f - FQ) % 2
                if f >= FQ + 4:
                    pe.wait_ge(drained_act, q * FILLS + (f - 1))
                    pe.wait_ge(drained_dve, q * FILLS + (f - 1))
                else:
                    pe.wait_ge(drained_dve, q * FILLS + KD)
                for k in range(KD):
                    ins = split3(pe, bank(f)[:, 0:QT_TOK], w_hi[:, qk, k, 128 * t:128 * (t + 1)],
                                 w_lo[:, qk, k, 128 * t:128 * (t + 1)], x_hi[:, k], x_lo[:, k],
                                 k == 0, k == KD - 1)
                ins.then_inc(filled, 1)

            def quad(q, last):
                for f in range(FQ + 4, FV):
                    heads_in(q, f)

                def values(f):
                    i, v = (f - FV) // 2, (f - FV) % 2
                    pe.wait_ge(drained_act, q * FILLS + (f - 1))
                    pe.wait_ge(drained_dve, q * FILLS + (f - 1))
                    if f == FV and isinstance(q, int) and q == 0:
                        pe.wait_ge(w_lo_ready, 4)
                    for k in range(KD):
                        ins = split3(pe, bank(f)[0:S, :], x_hi[:, k, S * i:S * (i + 1)],
                                     x_lo[:, k, S * i:S * (i + 1)], w_hi[:, 2, k, 512 * v:512 * (v + 1)],
                                     w_lo[:, 2, k, 512 * v:512 * (v + 1)], k == 0, k == KD - 1)
                    ins.then_inc(filled, 1)

                def head(src, g, h):
                    i = batch_of(g)
                    lo, r = 64 * (i % 2), (quarter_of(g) * GH + h) * S
                    return src[lo:lo + 64, i // 2, r:r + S]

                for r in range(-1, ROUNDS + TAIL):
                    pair = in_round(r)
                    if r == 0:
                        pe.wait_ge(drained_act, q * FILLS + FV)
                        pe.wait_ge(drained_dve, q * FILLS + FV)
                    if pair:
                        pe.wait_ge(q_hi_ready, q * ROUNDS + (r + 1))
                        pe.wait_ge(k_pair_act, q * ROUNDS + (r + 1))
                        pe.wait_ge(k_pair_dve, q * ROUNDS + (r + 1))
                        reach(pe, max_ready, q * GQ + 2 * r)
                    for h in range(GH if pair else 0):
                        n = h // 2
                        ins = pe.matmul(ps_s[n][0:S, 256 * (h % 2):256 * (h % 2 + 1)],
                                        q_hi[:, r % 2, S * h:S * (h + 1)],
                                        k_pair[:, r % 2, 2 * S * h:2 * S * h + 2 * S + PAD], start=True, stop=True)
                        if h % 2 == 1:
                            ins.then_inc(scores_ready, 1)
                    for f in values_in(r):
                        values(f)
                    if r == 2:
                        pe.wait_ge(drained_act, q * FILLS + FILLS)
                        pe.wait_ge(drained_dve, q * FILLS + FILLS)
                    for g in in_round(r - 2):
                        i = batch_of(g)
                        if quarter_of(g) == 0:
                            pe.wait_ge(v_loaded[i], q * 16 + 16)
                        pe.wait_ge(probs_ready, q * GQ + (g + 1))
                        if g >= 2:
                            pe.wait_ge(o_ready, q * GQ + (g - 1))
                        for h in range(GH):
                            ins = pe.matmul(ps_o[g % 2][0:S, (HD1 + 1) * h:(HD1 + 1) * (h + 1)],
                                            probs[:, g % 2, S * h:S * (h + 1)],
                                            v_ext[:, i, quarter_of(g) * GH + h, :], start=True, stop=True)
                        ins.then_inc(pv_ready, 1)
                    if r == ROUNDS and not last:
                        pe.wait_ge(max_ready, q * GQ + GQ)
                        turn_x(q + 1)
                    if r == ROUNDS + 1 and not last:
                        pe.wait_ge(probs_ready, q * GQ + GQ)
                        for f in AHEAD[r]:
                            heads_in(q + 1, f)
                    if r == ROUNDS + 2 and not last:
                        pe.wait_ge(x1_ready, q * QUAD + 2)
                        pe.wait_ge(o_ready, q * GQ + GQ)
                        for f in AHEAD[r]:
                            heads_in(q + 1, f)
                    pair = in_round(r - 1)
                    if pair and r >= 2:
                        pe.wait_ge(probs_ready, q * GQ + 2 * (r - 1))
                    for h in range(GH):
                        for g in pair:
                            pe.matmul(ps_t[g % 2][0:S, S * h:S * (h + 1)], head(k_t, g, h), head(q_t, g, h),
                                      start=(h == 0), stop=False, skip_group_check=True)
                    for g in pair:
                        pe.wait_ge(diag_ready, q * GQ + (g + 1))
                        pe.matmul(ps_t[g % 2][0:S, 0:GH * S], c.ones_r[0:S, 0:S],
                                  diag[:, g % 2].rearrange("p h j -> p (h j)"), start=False, stop=True,
                                  skip_group_check=True).then_inc(shifted_ready, 1)
                    for g in in_round(r - 3):
                        if last_round_of_pair(r - 3):
                            i = batch_of(g)
                            pe.wait_ge(ot_copied_dve, q * 2 * GQ + 2 * (2 * (r - 3) + 2))
                            if i >= 2:
                                pe.wait_ge(x1_ready, q * QUAD + 2)
                            hi, lo = (t[:, i % 2, :].rearrange("p (s t) -> p t s", t=NT) for t in (o_hi, o_lo))
                            wo_hi, wo_lo = (w[:, 3].rearrange("p k n -> p (k n)").rearrange(
                                "p (t n) -> p t n", n=D) for w in (w_hi, w_lo))
                            for t in range(NT):
                                ins = split3(pe, ps_y[i // 2][0:S, D * (i % 2):D * (i % 2 + 1)], hi[:, t, :],
                                             lo[:, t, :], wo_hi[:, t, :], wo_lo[:, t, :], t == 0, t == NT - 1)
                            ins.then_inc(y_ready, 1)
                    for g in in_round(r - 2):
                        pe.wait_ge(o_ready, q * GQ + (g + 1))
                        if g == 0:
                            reach(pe, x1_ready, q * QUAD)
                        if g >= 2:
                            pe.wait_ge(ot_copied_dve, q * 2 * GQ + 2 * (g - g % 2))
                        for w in range(2):
                            ins = pe.transpose(ps_ot[:, 2 * S * (g % 2) + S * w:2 * S * (g % 2) + S * (w + 1)],
                                               o_norm[:, g % 2, 128 * w:128 * (w + 1)], c.ident[0:S, 0:S])
                        ins.then_inc(ot_ready, 1)

            turn_x(0)
            pe.wait_ge(w_lo_ready, 2)
            for f in range(FQ, FQ + 4):
                heads_in(0, f)
            quad(0, False)
            with pe.Fori(1, QUADS - 1) as q:
                quad(q, False)
            quad(QUADS - 1, True)


def paired(eng, emit):
    emit(0, 0, False)
    emit(1, 1, False)
    with eng.Fori(1, B // 2 - 1) as i:
        emit(i * 2, 0, False)
        emit(i * 2 + 1, 1, False)
    emit(B - 2, 0, False)
    emit(B - 1, 1, True)


def row(b):
    return b if isinstance(b, int) else bass.ds(b, 1)


def cross_attention(nc, c, ctx_in, mask, maskT, wq, wk, wv, wo, bq, bk, bv, bo):
    with ExitStack() as ctx:
        def sb(name, shape, dt=F32):
            return ctx.enter_context(nc.sbuf_tensor(name, shape, dt))

        def psum(name, shape, dt=F32):
            return ctx.enter_context(nc.psum_tensor(name, shape, dt))

        def sem(name):
            return ctx.enter_context(nc.semaphore(name))

        KP = KT[0]
        wq_sb = sb("wq2", [128, KD, D])
        wk_st = sb("wk_stage", [128, KD, D])
        wv_st = sb("wv_stage", [128, KD, D])
        wk_hi = sb("wk_hi", [128, KD, D], F32R)
        wk_lo = sb("wk_lo", [128, KD, D], F32R)
        wv_hi = sb("wv_hi", [128, KD, D], F32R)
        wv_lo = sb("wv_lo", [128, KD, D], F32R)
        wo_sb = sb("wo2", [128, KD, D])
        bq_sb = sb("bq", [128, KD])
        bk_sb = sb("bk", [128, KD])
        bv_sb = sb("bv", [KP, D])
        bo_sb = sb("bo", [S, D])
        mask_t = sb("mask_t", [KP, 3, B], I32)
        key_live = sb("key_live", [KP, 3, B])
        key_bias = sb("key_bias", [KP, 3, B])
        mask_i = sb("mask_i", [S, 2, S2], I32)
        mask_f = sb("mask_f", [S, 2, S2])
        c_tok = sb("c_tok", [KP, 2, 3, D])
        c_hi = sb("c_hi", [128, KD, S2E], F32R)
        c_lo = sb("c_lo", [128, KD, S2E], F32R)
        stats = sb("stats2", [S, 6])
        mv = sb("mv2", [S, 2])
        var_eps = sb("var_eps2", [S, 1])
        rstd = sb("rstd2", [S, 1])
        xn = sb("xn2", [S, D])
        x_t = sb("x_t2", [128, KD * S])
        q_b = sb("q_b", [128, KD * S])
        q_hi = sb("q_hi", [128, 4, S])
        q_lo = sb("q_lo", [128, KD, S])
        qd_hi = sb("qd_hi", [128, 2, 4, 4, S], F32R)
        qd_lo = sb("qd_lo", [128, 2, KD, 4, S], F32R)
        k_both = sb("k_both", [128, 2, 4, S2E], F32R)
        v_ext = sb("v_ext2", [KP, 2, 3, H2, 32])
        masked = sb("masked", [S, 2, S2])
        row_max = sb("row_max2", [S, 2, 4])
        diag = sb("diag2", [S, 2, 4, S], F32R)
        probs = sb("probs2", [KP, 2, 3, 4 * S])
        recip = sb("recip2", [S, H2])
        o_raw = sb("o_raw", [128, 4 * S])
        o_norm = sb("o_norm2", [S, D])
        o_t = sb("o_t2", [128, KD * S])

        ps_p = [psum(f"psb_p{i}", [128, 512]) for i in range(2)]
        ps_s = [psum(f"psb_s{i}", [128, 512]) for i in range(2)]
        ps_t = [psum(f"psb_t{i}", [128, 512]) for i in range(2)]
        ps_o = psum("psb_o", [128, 512])
        ps_f = psum("psb_f", [128, 512])

        act_passed = sem("act_passed")
        dve_passed = sem("dve_passed")
        pool_passed = sem("pool_passed")
        w_loaded = sem("w2_loaded")
        w_hi_ready = sem("w2_hi_ready")
        w_lo_ready = sem("w2_lo_ready")
        mask_t_loaded = sem("mask_t_loaded")
        key_mask_cleared = sem("key_mask_cleared")
        key_mask_ready = sem("key_mask_ready")
        pad_ready = sem("pad_ready")
        ctx_loaded = [sem(f"ctx_loaded{p}") for p in range(2)]
        mask_loaded = [sem(f"mask_loaded{p}") for p in range(2)]
        mask_ready = sem("mask_ready")
        ones_ready = sem("ones2_ready")
        stats_ready = sem("stats2_ready")
        mv_ready = sem("mv2_ready")
        eps_added = sem("eps2_added")
        rstd_ready = sem("rstd2_ready")
        xn_ready = sem("xn2_ready")
        bo_added = sem("bo_added")
        filled = sem("filled2")
        drained_act = sem("drained2_act")
        drained_dve = sem("drained2_dve")
        q_rounded = sem("q_rounded")
        q_split = sem("q_split")
        qd_ready = sem("qd_ready")
        scores_ready = sem("scores2_ready")
        max_ready = sem("max2_ready")
        diag_ready = sem("diag2_ready")
        shifted_ready = sem("shifted2_ready")
        probs_ready = sem("probs2_ready")
        pv_ready = sem("pv2_ready")
        raw_copied = sem("raw_copied")
        raw_turned = sem("raw_turned")
        recip_ready = sem("recip2_ready")
        o_ready = sem("o2_ready")
        ot_ready = sem("ot2_ready")
        ot_copied = sem("ot2_copied")
        y_ready = sem("y2_ready")
        x2_ready = sem("x2_ready")

        C0, XT, Q0, K0, V0, FILLS = 0, 2, 3, 4, 6, 9
        ACT_OF = {0: 1, 1: 2, XT: 3, Q0: 4, K0: 5, K0 + 1: 6}
        DVE_OF = {0: 1, 1: 2, K0: 3, K0 + 1: 4, V0: 5, V0 + 1: 6, V0 + 2: 7}
        NA, ND = len(ACT_OF), len(DVE_OF)

        def bank(pp, f):
            return ps_p[(FILLS * pp + f) % 2]

        def bank_free(pe, pb, f):
            pb, f = (pb, f - 2) if f >= 2 else (pb - 1, f - 2 + FILLS)
            if f in DVE_OF:
                reach(pe, drained_dve, pb * ND + DVE_OF[f])
            else:
                reach(pe, drained_act, pb * NA + ACT_OF[f])

        block = ctx.enter_context(nc.Block())

        @block.sync
        def _(sp):
            for dst, src in ((wk_st, wk), (wv_st, wv), (wq_sb, wq), (wo_sb, wo)):
                sp.dma_start(dst[:], src.rearrange("(k p) n -> p k n", p=128)).then_inc(w_loaded, 16)
            sp.dma_start(bq_sb[:], bq).then_inc(w_loaded, 16)
            sp.dma_start(bk_sb[:], bk).then_inc(w_loaded, 16)
            sp.dma_start(bv_sb[:], bv.rearrange("(o n) -> o n", o=1).to_broadcast([KP, D])).then_inc(w_loaded, 16)
            sp.dma_start(bo_sb[:], bo.rearrange("(o n) -> o n", o=1).to_broadcast([S, D])).then_inc(w_loaded, 16)
            sp.wait_ge(key_mask_cleared, 1)
            for kt in range(3):
                sp.dma_start(mask_t[0:KT[kt], kt, :], maskT[KT0[kt]:KT0[kt] + KT[kt], :]).then_inc(mask_t_loaded, 16)

            def load(pb, p, _):
                reach(sp, filled, (pb - 2) * FILLS + 2)
                sp.dma_start(c_tok[:, p, 0:2, :], ctx_in[row(pb), 0:2 * KP, :].rearrange(
                    "(k r) d -> r k d" if isinstance(pb, int) else "b (k r) d -> r (b k) d",
                    r=KP)).then_inc(ctx_loaded[p], 16)
                last = ctx_in[row(pb), 2 * KP:S2, :]
                sp.dma_start(c_tok[0:KT[2], p, 2, :],
                             last if isinstance(pb, int) else last.rearrange("b r d -> (b r) d")
                             ).then_inc(ctx_loaded[p], 16)
                reach(sp, mask_ready, pb - 1)
                m = mask[row(pb), :]
                m = m.rearrange("(o n) -> o n", o=1) if isinstance(pb, int) else m
                sp.dma_start(mask_i[:, p, :], m.to_broadcast([S, S2])).then_inc(mask_loaded[p], 16)

            paired(sp, load)

        @block.gpsimd
        def _(pool):
            pool.memset(mask_t[:], 0).then_inc(key_mask_cleared, 1)
            pool.memset(c_hi[:, :, S2:S2E].bitcast(F32), 0.0).then_inc(pad_ready, 1)
            pool.memset(c_lo[:, :, S2:S2E].bitcast(F32), 0.0).then_inc(pad_ready, 1)
            pool.memset(v_ext[:, :, :, :, HD2:32], 0.0).then_inc(pad_ready, 1)
            pool.wait_ge(pad_ready, 3)
            pool.wait_ge(mask_t_loaded, 48)
            pool.wait_ge(w_loaded, 16 * 8)
            pool.tensor_scalar(key_bias[:], mask_t[:], 0.0, NEG, ALU.is_equal, ALU.mult).then_inc(key_mask_ready, 1)
            pool.wait_ge(key_mask_ready, 1)
            pool.tensor_scalar(key_live[:], key_bias[:], 0.0, None, ALU.is_equal).then_inc(key_mask_ready, 1)
            pool.wait_ge(key_mask_ready, 2)

            def ln_step(pb):
                pool.wait_ge(mv_ready, pb + 1)
                pool.sem_inc(pool_passed, 1)
                pool.tensor_scalar(var_eps[:], mv[:, 1:2], EPS, None, ALU.add).then_inc(eps_added, 1)
                pool.wait_ge(eps_added, pb + 1)
                pool.tensor_tensor(rstd[:], var_eps[:], c.minus_half[0:S, 0:1], ALU.pow).then_inc(rstd_ready, 1)

            def mask_step(pb, pp):
                pool.wait_ge(mask_loaded[pp], (pb - pp) * 8 + 16)
                pool.sem_inc(pool_passed, 1)
                pool.tensor_scalar(mask_f[:, pp], mask_i[:, pp], 0.0, NEG, ALU.is_equal,
                                   ALU.mult).then_inc(mask_ready, 1)

            def live_step(pb, pp):
                live = (key_live[:, :, pb:pb + 1] if isinstance(pb, int) else key_live[:, :, bass.ds(pb, 1)])
                pool.tensor_copy(v_ext[:, pp, :, :, HD2:HD2 + 1].rearrange("p k h o -> p k (h o)"),
                                 live.to_broadcast([KP, 3, H2])).then_inc(ones_ready, 1)

            def bo_step(pb):
                pool.wait_ge(xn_ready, pb + 1)
                xb = at_batch(c.x, pb, slice(0, D))
                pool.tensor_tensor(xb, xb, bo_sb[:], ALU.add).then_inc(bo_added, 1)

            def place(pb, pp, g):
                pool.wait_ge(q_split, 2 * pb + 2)
                own = c.head_of[:].unsqueeze(2).to_broadcast([128, 4, S])
                for u in (2 * g, 2 * g + 1):
                    pool.tensor_tensor(qd_hi[:, pp, u], q_hi[:, u:u + 1, :].to_broadcast([128, 4, S]), own,
                                       ALU.mult).then_inc(qd_ready, 1)
                pool.tensor_tensor(qd_lo[:, pp, g], q_lo[:, g:g + 1, :].to_broadcast([128, 4, S]), own,
                                   ALU.mult).then_inc(qd_ready, 1)

            def diagonal(b, u):
                pool.wait_ge(max_ready, b * H2 + 4 * (u + 1))
                reach(pool, shifted_ready, b * 12 + 3 * (u - 1))
                pool.tensor_tensor(diag[:, u % 2], c.neg_ident[0:S, 0:S].unsqueeze(1).to_broadcast([S, 4, S]),
                                   row_max[:, u % 2].unsqueeze(2).to_broadcast([S, 4, S]),
                                   ALU.mult).then_inc(diag_ready, 1)

            ln_step(0)
            mask_step(0, 0)
            live_step(0, 0)
            bo_step(0)
            place(0, 0, 0)
            place(0, 0, 1)
            diagonal(0, 0)

            def step(b, p, last):
                if not last:
                    ln_step(b + 1)
                diagonal(b, 1)
                if not last:
                    mask_step(b + 1, 1 - p)
                    bo_step(b + 1)
                diagonal(b, 2)
                if not last:
                    place(b + 1, 1 - p, 0)
                    place(b + 1, 1 - p, 1)
                diagonal(b, 3)
                if not last:
                    live_step(b + 1, 1 - p)
                    diagonal(b + 1, 0)

            paired(pool, step)

        @block.scalar
        def _(act):
            act.wait_ge(w_loaded, 16 * 8)
            act.copy(wk_hi[:], wk_st[:]).then_inc(w_hi_ready, 1)
            act.copy(wv_hi[:], wv_st[:]).then_inc(w_hi_ready, 1)
            act.wait_ge(key_mask_ready, 2)

            def context(pb, pp):
                for k in range(KD):
                    act.wait_ge(filled, pb * FILLS + (k + 1))
                    act.copy(c_hi[:, k, 0:S2], bank(pp, k)[:, 0:S2]).then_inc(drained_act, 1)

            def x_turned(pb, pp):
                act.wait_ge(filled, pb * FILLS + (XT + 1))
                act.copy(x_t[:], bank(pp, XT)[:, 0:KD * S]).then_inc(drained_act, 1)

            def queries(pb, pp):
                act.wait_ge(filled, pb * FILLS + (Q0 + 1))
                reach(act, q_split, 2 * pb)
                for g in range(KD):
                    ins = act.activation(q_b[:, S * g:S * (g + 1)], bank(pp, Q0)[:, S * g:S * (g + 1)], ACT.Identity,
                                         bias=bq_sb[:, g:g + 1])
                ins.then_inc(drained_act, 1)

            def keys(pb, pp):
                for g in range(KD):
                    act.wait_ge(filled, pb * FILLS + (K0 + g + 1))
                    for a in (slice(0, 64), slice(64, 128)):
                        ins = act.activation(k_both[a, pp, 2 * g + a.start // 64], bank(pp, K0 + g)[a, 0:S2E],
                                             ACT.Identity, bias=bk_sb[a, g:g + 1])
                    ins.then_inc(drained_act, 1)

            def exps(b, u, kt):
                if kt == 0:
                    reach(act, pv_ready, b * 4 + (u - 1))
                i = 3 * u + kt
                act.wait_ge(shifted_ready, b * 12 + (i + 1))
                act.sem_inc(act_passed, 1)
                bias = key_bias[0:KT[kt], kt, b:b + 1] if isinstance(b, int) else key_bias[0:KT[kt], kt, bass.ds(b, 1)]
                act.activation(probs[0:KT[kt], u % 2, kt], ps_t[i % 2][0:KT[kt], 0:4 * S], ACT.Exp,
                               bias=bias, scale=HD2 ** -0.5).then_inc(probs_ready, 1)

            def raw_out(b):
                act.wait_ge(pv_ready, b * 4 + 4)
                act.copy(o_raw[:], ps_o[:, 0:4 * S]).then_inc(raw_copied, 1)

            def turned_out(b):
                act.wait_ge(ot_ready, b + 1)
                act.copy(o_t[:], ps_f[:, 0:KD * S]).then_inc(ot_copied, 1)

            context(0, 0)
            x_turned(0, 0)
            queries(0, 0)
            keys(0, 0)

            def step(b, p, last):
                first = isinstance(b, int) and b == 0
                exps(b, 0, 0)
                exps(b, 0, 1)
                if not last:
                    context(b + 1, 1 - p)
                exps(b, 0, 2)
                if not first:
                    raw_out(b - 1)
                exps(b, 1, 0)
                if not last:
                    x_turned(b + 1, 1 - p)
                exps(b, 1, 1)
                if not last:
                    queries(b + 1, 1 - p)
                exps(b, 1, 2)
                if not last:
                    keys(b + 1, 1 - p)
                for kt in range(3):
                    exps(b, 2, kt)
                if not first:
                    turned_out(b - 1)
                for kt in range(3):
                    exps(b, 3, kt)

            paired(act, step)
            raw_out(B - 1)
            turned_out(B - 1)

        @block.vector
        def _(dve):
            for j, (hi, lo, st) in enumerate(((wk_hi, wk_lo, wk_st), (wv_hi, wv_lo, wv_st))):
                dve.wait_ge(w_hi_ready, j + 1)
                dve.tensor_tensor(lo[:], st[:], hi[:].bitcast(F32), ALU.subtract).then_inc(w_lo_ready, 1)

            def norm_stats(pb):
                dve.bn_stats(stats[:], at_batch(c.x, pb, slice(0, D))).then_inc(stats_ready, 1)
                dve.wait_ge(stats_ready, pb + 1)
                dve.sem_inc(dve_passed, 1)
                dve.bn_aggr(mv[:], stats[:]).then_inc(mv_ready, 1)

            def normalize(pb):
                dve.wait_ge(rstd_ready, pb + 1)
                dve.tensor_scalar(xn[:], at_batch(c.x, pb, slice(0, D)), mv[:, 0:1], rstd[:], ALU.subtract,
                                  ALU.mult).then_inc(xn_ready, 1)

            def context(pb, pp):
                for k in range(KD):
                    dve.wait_ge(drained_act, pb * NA + ACT_OF[k])
                    dve.tensor_tensor(c_lo[:, k, 0:S2], bank(pp, k)[:, 0:S2], c_hi[:, k, 0:S2].bitcast(F32),
                                      ALU.subtract).then_inc(drained_dve, 1)

            def queries(pb, pp):
                dve.wait_ge(drained_act, pb * NA + ACT_OF[Q0])
                reach(dve, qd_ready, 6 * pb)
                natural = q_b[:].rearrange("p (g s) -> p g s", g=KD)
                for a in range(2):
                    for half in range(2):
                        ins = dve.tensor_copy(q_hi[64 * half:64 * half + 64, a::2, :].bitcast(F32R),
                                              natural[64 * a:64 * a + 64])
                ins.then_inc(q_split, 1)
                dve.wait_ge(q_split, 2 * pb + 1)
                for a in range(2):
                    rows = slice(64 * a, 64 * a + 64)
                    ins = dve.tensor_tensor(q_lo[rows], natural[rows], q_hi[rows, a::2, :], ALU.subtract)
                ins.then_inc(q_split, 1)

            def keys(pb, pp):
                for g in range(KD):
                    dve.wait_ge(drained_act, pb * NA + ACT_OF[K0 + g])
                    for a in range(2):
                        rows, others, u = slice(64 * a, 64 * a + 64), slice(64 - 64 * a, 128 - 64 * a), 2 * g + a
                        ins = dve.scalar_tensor_tensor(out=k_both[others, pp, u], in0=bank(pp, K0 + g)[rows, 0:S2E],
                                                       scalar=bk_sb[rows, g:g + 1],
                                                       in1=k_both[rows, pp, u].bitcast(F32),
                                                       op0=ALU.add, op1=ALU.subtract)
                    ins.then_inc(drained_dve, 1)

            def values(pb, pp):
                for kt in range(3):
                    dve.wait_ge(filled, pb * FILLS + (V0 + kt + 1))
                    n = KT[kt]
                    dve.tensor_tensor(v_ext[0:n, pp, kt, :, 0:HD2],
                                      bank(pp, V0 + kt)[0:n, 0:D].rearrange("p (h d) -> p h d", h=H2),
                                      bv_sb[0:n, :].rearrange("p (h d) -> p h d", h=H2),
                                      ALU.add).then_inc(drained_dve, 1)

            def maximum(b, p, h):
                if h == 0:
                    dve.wait_ge(mask_ready, b + 1)
                if h % 4 == 0:
                    reach(dve, diag_ready, b * 4 + (h // 4 - 1))
                dve.wait_ge(scores_ready, b * H2 + (h + 1))
                dve.sem_inc(dve_passed, 1)
                dve.tensor_tensor_reduce(masked[:, h % 2], ps_s[h % 2][0:S, 0:S2], mask_f[:, p], 1.0, -3.0e38,
                                         ALU.add, ALU.max,
                                         row_max[:, (h // 4) % 2, h % 4:h % 4 + 1]).then_inc(max_ready, 1)

            def maxima(b, p, first, end):
                for h in range(first, end):
                    maximum(b, p, h)

            def quotients(b):
                o = ps_f[0:S, 0:H2 * 32].rearrange("p (h d) -> p h d", h=H2)
                dve.wait_ge(raw_turned, b + 1)
                dve.reciprocal(recip[:], o[:, :, HD2]).then_inc(recip_ready, 1)
                dve.wait_ge(recip_ready, b + 1)
                dve.tensor_tensor(o_norm[:].rearrange("p (h d) -> p h d", h=H2), o[:, :, 0:HD2],
                                  recip[:].unsqueeze(2).to_broadcast([S, H2, HD2]), ALU.mult).then_inc(o_ready, 1)

            def residual(b):
                dve.wait_ge(y_ready, b + 1)
                dve.wait_ge(bo_added, b + 1)
                xb = at_batch(c.x, b, slice(0, D))
                dve.tensor_tensor(xb, ps_f[0:S, 0:D], xb, ALU.add).then_inc(x2_ready, 1)

            def route_stats(b):
                dve.wait_ge(x2_ready, b + 1)
                stats = (c.route_stats[:, b] if isinstance(b, int)
                         else c.route_stats[:, bass.ds(b, 1), :].rearrange("p b s -> p (b s)"))
                dve.bn_stats(stats, at_batch(c.x, b, slice(0, D)))

            dve.wait_ge(w_lo_ready, 2)
            norm_stats(0)
            normalize(0)
            context(0, 0)
            queries(0, 0)
            keys(0, 0)
            values(0, 0)
            maxima(0, 0, 0, 5)

            def step(b, p, last):
                first = isinstance(b, int) and b == 0
                if not last:
                    norm_stats(b + 1)
                maxima(b, p, 5, 8)
                if not last:
                    normalize(b + 1)
                    context(b + 1, 1 - p)
                maxima(b, p, 8, 11)
                if not last:
                    queries(b + 1, 1 - p)
                maxima(b, p, 11, 13)
                if not first:
                    quotients(b - 1)
                if not (isinstance(b, int) and b < 2):
                    route_stats(b - 2)
                maximum(b, p, 13)
                if not last:
                    keys(b + 1, 1 - p)
                maxima(b, p, 14, 16)
                if not last:
                    values(b + 1, 1 - p)
                    maxima(b + 1, 1 - p, 0, 4)
                if not first:
                    residual(b - 1)
                if not last:
                    maximum(b + 1, 1 - p, 4)

            paired(dve, step)
            quotients(B - 1)
            residual(B - 1)
            route_stats(B - 2)
            route_stats(B - 1)

        @block.tensor
        def _(pe):
            pe.wait_ge(w_loaded, 16 * 8)
            pe.wait_ge(w_hi_ready, 2)
            pe.wait_ge(w_lo_ready, 2)
            pe.wait_ge(pad_ready, 3)

            def context(pb, pp):
                reach(pe, ctx_loaded[pp], (pb - pp) * 16 + 32)
                for k in range(KD):
                    bank_free(pe, pb, C0 + k)
                    for kt in range(3):
                        ins = pe.transpose(bank(pp, k)[:, KT0[kt]:KT0[kt] + KT[kt]],
                                           c_tok[0:KT[kt], pp, kt, 128 * k:128 * (k + 1)],
                                           c.ident[0:KT[kt], 0:KT[kt]])
                    ins.then_inc(filled, 1)

            def turn_x(pb, pp):
                bank_free(pe, pb, XT)
                pe.wait_ge(xn_ready, pb + 1)
                for k in range(KD):
                    ins = pe.transpose(bank(pp, XT)[:, S * k:S * (k + 1)], xn[:, 128 * k:128 * (k + 1)],
                                       c.ident[0:S, 0:S])
                ins.then_inc(filled, 1)

            def queries(pb, pp):
                bank_free(pe, pb, Q0)
                pe.wait_ge(drained_act, pb * NA + ACT_OF[XT])
                for g in range(KD):
                    for k in range(KD):
                        ins = pe.matmul(bank(pp, Q0)[:, S * g:S * (g + 1)], wq_sb[:, k, 128 * g:128 * (g + 1)],
                                        x_t[:, S * k:S * (k + 1)], start=(k == 0), stop=(k == KD - 1))
                ins.then_inc(filled, 1)

            def keys(pb, pp):
                pe.wait_ge(drained_dve, pb * ND + DVE_OF[1])
                for g in range(KD):
                    bank_free(pe, pb, K0 + g)
                    for k in range(KD):
                        cols = slice(128 * g, 128 * (g + 1))
                        ins = split3(pe, bank(pp, K0 + g)[:, 0:S2E], wk_hi[:, k, cols], wk_lo[:, k, cols],
                                     c_hi[:, k], c_lo[:, k], k == 0, k == KD - 1)
                    ins.then_inc(filled, 1)

            def values(pb, pp):
                for kt in range(3):
                    bank_free(pe, pb, V0 + kt)
                    rows = slice(KT0[kt], KT0[kt] + KT[kt])
                    for k in range(KD):
                        ins = split3(pe, bank(pp, V0 + kt)[0:KT[kt], 0:D], c_hi[:, k, rows], c_lo[:, k, rows],
                                     wv_hi[:, k], wv_lo[:, k], k == 0, k == KD - 1)
                    ins.then_inc(filled, 1)

            def scores(b, p, h):
                if h % HG == 0:
                    pe.wait_ge(drained_dve, b * ND + DVE_OF[K0 + h // HG])
                    pe.wait_ge(qd_ready, 6 * b + 3 * (h // HG) + 3)
                reach(pe, max_ready, b * H2 + (h - 1))
                pe.matmul(ps_s[h % 2][0:S, 0:S2E], qd_hi[:, p, h // 4, h % 4, :], k_both[:, p, h // 4],
                          start=True, stop=True).then_inc(scores_ready, 1)

            def shifted(b, p, u, kt):
                i, n = 3 * u + kt, KT[kt]
                reach(pe, probs_ready, b * 12 + (i - 1))
                rows, half = slice(KT0[kt], KT0[kt] + n), slice(64 * (u % 2), 64 * (u % 2) + 64)
                out = ps_t[i % 2][0:n, 0:4 * S]
                pe.matmul(out, k_both[half, p, u, rows], qd_lo[half, p, u // 2].rearrange("p h s -> p (h s)"),
                          start=True, stop=False)
                pe.matmul(out, k_both[:, p, u, rows], qd_hi[:, p, u].rearrange("p h s -> p (h s)"),
                          start=False, stop=False)
                if kt == 0:
                    pe.wait_ge(diag_ready, b * 4 + (u + 1))
                pe.matmul(out, c.ones_r[0:S, 0:n], diag[:, u % 2].rearrange("p h s -> p (h s)"),
                          start=False, stop=True).then_inc(shifted_ready, 1)

            def weighted(b, p, u):
                if u == 0:
                    reach(pe, raw_copied, b)
                    pe.wait_ge(drained_dve, b * ND + ND)
                    pe.wait_ge(ones_ready, b + 1)
                for kt in range(3):
                    pe.wait_ge(probs_ready, b * 12 + (3 * u + kt + 1))
                    n = KT[kt]
                    for h in range(4):
                        ins = pe.matmul(ps_o[32 * h:32 * (h + 1), S * u:S * (u + 1)], v_ext[0:n, p, kt, 4 * u + h, :],
                                        probs[0:n, u % 2, kt, S * h:S * (h + 1)], start=(kt == 0), stop=(kt == 2))
                ins.then_inc(pv_ready, 1)

            def turn_raw(b):
                pe.wait_ge(raw_copied, b + 1)
                reach(pe, x2_ready, b)
                for u in range(4):
                    ins = pe.transpose(ps_f[0:S, 128 * u:128 * (u + 1)], o_raw[:, S * u:S * (u + 1)], c.ident[:])
                ins.then_inc(raw_turned, 1)

            def turn_out(b):
                pe.wait_ge(o_ready, b + 1)
                for k in range(KD):
                    ins = pe.transpose(ps_f[:, S * k:S * (k + 1)], o_norm[:, 128 * k:128 * (k + 1)],
                                       c.ident[0:S, 0:S])
                ins.then_inc(ot_ready, 1)

            def project(b):
                pe.wait_ge(ot_copied, b + 1)
                for k in range(KD):
                    ins = pe.matmul(ps_f[0:S, 0:D], o_t[:, S * k:S * (k + 1)], wo_sb[:, k, :],
                                    start=(k == 0), stop=(k == KD - 1))
                ins.then_inc(y_ready, 1)

            context(0, 0)
            turn_x(0, 0)
            queries(0, 0)
            keys(0, 0)
            values(0, 0)
            for h in range(5):
                scores(0, 0, h)

            def step(b, p, last):
                first = isinstance(b, int) and b == 0

                shifted(b, p, 0, 0)
                scores(b, p, 5)
                shifted(b, p, 0, 1)
                scores(b, p, 6)
                if not last:
                    context(b + 1, 1 - p)
                scores(b, p, 7)
                shifted(b, p, 0, 2)
                scores(b, p, 8)
                if not first:
                    weighted(b - 1, 1 - p, 3)

                shifted(b, p, 1, 0)
                scores(b, p, 9)
                if not last:
                    turn_x(b + 1, 1 - p)
                shifted(b, p, 1, 1)
                scores(b, p, 10)
                if not last:
                    queries(b + 1, 1 - p)
                shifted(b, p, 1, 2)
                scores(b, p, 11)
                if not first:
                    turn_raw(b - 1)
                scores(b, p, 12)
                weighted(b, p, 0)
                if not last:
                    keys(b + 1, 1 - p)

                shifted(b, p, 2, 0)
                scores(b, p, 13)
                shifted(b, p, 2, 1)
                scores(b, p, 14)
                if not first:
                    turn_out(b - 1)
                shifted(b, p, 2, 2)
                scores(b, p, 15)
                weighted(b, p, 1)
                if not last:
                    values(b + 1, 1 - p)

                shifted(b, p, 3, 0)
                if not last:
                    scores(b + 1, 1 - p, 0)
                shifted(b, p, 3, 1)
                if not last:
                    scores(b + 1, 1 - p, 1)
                if not first:
                    project(b - 1)
                if not last:
                    scores(b + 1, 1 - p, 2)
                    scores(b + 1, 1 - p, 3)
                shifted(b, p, 3, 2)
                weighted(b, p, 2)
                if not last:
                    scores(b + 1, 1 - p, 4)

            paired(pe, step)
            weighted(B - 1, 1, 3)
            turn_raw(B - 1)
            turn_out(B - 1)
            project(B - 1)


def expert_buffers(nc, c, ctx):
    def sb(name, shape):
        return ctx.enter_context(nc.sbuf_tensor(name, shape, F32))

    c.w1_sb = sb("w1_sb", [128, 2, KD, F])
    c.w2_sb = sb("w2_sb", [128, 2, NF, D])
    c.gam = sb("gam", [128, KD, E])
    c.bet = sb("bet", [128, KD, E])
    c.b1_sb = sb("b1_sb", [128, NF, E])
    c.b2_sb = sb("b2_sb", [128, E, D])
    c.cen = sb("cen", [128, E, D])
    c.tables = ctx.enter_context(nc.semaphore("tables4"))
    c.w_loaded = [ctx.enter_context(nc.semaphore(f"w4_loaded{p}")) for p in range(2)]


def expert_of(eng, c, j):
    return eng.value_load(c.tile_expert[0:1, j:j + 1] if isinstance(j, int)
                          else c.tile_expert[0:1, bass.ds(j, 1)], min_val=0, max_val=E - 1)


def load_weights(sp, c, e, p, w1, w2):
    sp.dma_start(c.w1_sb[:, p], w1[bass.ds(e, 1)].rearrange("o (k p) n -> p (o k) n", p=128)
                 ).then_inc(c.w_loaded[p], 16)
    sp.dma_start(c.w2_sb[:, p], w2[bass.ds(e, 1)].rearrange("o (k p) n -> p (o k) n", p=128)
                 ).then_inc(c.w_loaded[p], 16)


def route(nc, c, centT, xs, w1, w2, gamma, beta, b1, b2, centroids):
    with ExitStack() as ctx:
        def sb(name, shape, dt=F32):
            return ctx.enter_context(nc.sbuf_tensor(name, shape, dt))

        def psum(name, shape, dt=F32):
            return ctx.enter_context(nc.psum_tensor(name, shape, dt))

        def sem(name):
            return ctx.enter_context(nc.semaphore(name))

        MAXT = (B * S + T - 1) // T
        cent = sb("cent", [128, KD, E])
        mv = sb("mv3", [S, B, 2])
        var_eps = sb("var_eps3", [S, B])
        rstd = sb("rstd3", [S, B])
        feats = sb("feats3", [S, 2, QUAD, D])
        f_t = sb("f_t3", [128, 2, KD, QT_TOK])
        aff = sb("aff", [S, B, E])
        top = sb("top", [S, B])
        best = sb("best", [S, B, E])
        onehot = sb("onehot", [S, B, E])
        first_w = sb("first_w", [S, E])
        nan_w = sb("nan_w", [S, E])
        steps = sb("steps", [S, MAXT])
        tile_no = sb("tile_no", [1, TILES + 1])
        scan = [sb(f"scan{i}", [S, B, E]) for i in range(2)]
        totals = sb("totals", [S, B, E])
        more = sb("more", [S, E, MAXT])
        n_tiles = sb("n_tiles", [S, E])
        ends = [sb(f"ends{i}", [S, E]) for i in range(2)]
        start = sb("start", [S, E])
        pos = sb("pos", [S, B, E])
        slot_f = sb("slot_f", [S, B])
        slot = sb("slot", [S, B], U32)
        past = sb("past", [1, TILES + 1, E])
        expert_f = sb("expert_f", [1, TILES + 1])

        ps_x = [psum(f"psc_x{i}", [128, 512]) for i in range(4)]
        ps_a = [psum(f"psc_a{i}", [128, 512]) for i in range(2)]
        ps_b = psum("psc_b", [128, 512])
        ps_n = psum("psc_n", [128, 512])

        cent_loaded = sem("cent_loaded")
        tables_ready = sem("tables_ready")
        mv_ready = sem("mv3_ready")
        eps_added = sem("eps3_added")
        rstd_ready = sem("rstd3_ready")
        feats_ready = sem("feats3_ready")
        turned = sem("turned3")
        copied = sem("copied3")
        aff_ready = sem("aff_ready")
        aff_copied = sem("aff_copied")
        chain = sem("route_chain")
        onehot_ready = sem("onehot_ready")
        before_ready = sem("before_ready")
        slot_ready = sem("slot_ready")
        experts_ready = sem("experts_ready")
        routed = sem("routed")

        block = ctx.enter_context(nc.Block())

        @block.sync
        def _(sp):
            sp.dma_start(cent[:], centT.rearrange("(k p) e -> p k e", p=128)).then_inc(cent_loaded, 16)
            for dst, src in ((c.gam, gamma), (c.bet, beta), (c.b1_sb, b1)):
                sp.dma_start(dst[:], src).then_inc(c.tables, 16)
            for dst, src in ((c.cen, centroids), (c.b2_sb, b2)):
                sp.dma_start(dst[:], src.rearrange("(o e) d -> o e d", o=1).to_broadcast([128, E, D])
                             ).then_inc(c.tables, 16)
            sp.wait_ge(experts_ready, 1)
            for j in range(2):
                load_weights(sp, c, expert_of(sp, c, j), j, w1, w2)

        @block.gpsimd
        def _(pool):
            pool.iota(c.x[:, :, D:ROWW].rearrange("s b o -> s (b o)"), pattern=[[S, B]], base=0, channel_multiplier=1,
                      allow_small_or_imprecise_dtypes=True).then_inc(tables_ready, 1)
            pool.iota(first_w[:], pattern=[[-1, E]], base=E, channel_multiplier=0,
                      allow_small_or_imprecise_dtypes=True).then_inc(tables_ready, 1)
            pool.memset(nan_w[:, 0:1], 0.5).then_inc(tables_ready, 1)
            pool.memset(nan_w[:, 1:E], 0.0).then_inc(tables_ready, 1)
            pool.iota(steps[:], pattern=[[T, MAXT]], base=0, channel_multiplier=0,
                      allow_small_or_imprecise_dtypes=True).then_inc(tables_ready, 1)
            pool.iota(tile_no[:], pattern=[[1, TILES + 1]], base=0, channel_multiplier=0,
                      allow_small_or_imprecise_dtypes=True).then_inc(tables_ready, 1)
            for q in range(QUADS):
                cols = slice(QUAD * q, QUAD * (q + 1))
                pool.wait_ge(mv_ready, QUAD * (q + 1))
                pool.tensor_scalar(var_eps[:, cols], mv[:, cols, 1], EPS, None, ALU.add).then_inc(eps_added, 1)
                pool.wait_ge(eps_added, q + 1)
                pool.tensor_tensor(rstd[:, cols], var_eps[:, cols], c.minus_half[0:S, cols],
                                   ALU.pow).then_inc(rstd_ready, 1)
            pool.wait_ge(slot_ready, 1)
            pool.wait_ge(c.xs_cleared, 16)
            pool.wait_ge(tables_ready, 1)
            for b in range(B):
                pool.indirect_dma_start(out=xs, out_offset=bass.IndirectOffsetOnAxis(ap=slot[:, b:b + 1], axis=0),
                                        in_=c.x[:, b, :], in_offset=None).then_inc(routed, 16)
            pool.wait_ge(routed, 16 * B)

        @block.scalar
        def _(act):
            for q in range(QUADS):
                act.wait_ge(turned, q + 1)
                if q >= 2:
                    act.wait_ge(aff_ready, q - 1)
                for k in range(KD):
                    ins = act.copy(f_t[:, q % 2, k], ps_x[2 * (q % 2) + k][:, 0:QT_TOK])
                ins.then_inc(copied, 1)

        @block.tensor
        def _(pe):
            def turn(q):
                pe.wait_ge(feats_ready, q + 1)
                if q >= 2:
                    pe.wait_ge(copied, q - 1)
                for k in range(KD):
                    for i in range(QUAD):
                        ins = pe.transpose(ps_x[2 * (q % 2) + k][:, S * i:S * (i + 1)],
                                           feats[:, q % 2, i, 128 * k:128 * (k + 1)], c.ident[0:S, 0:S])
                ins.then_inc(turned, 1)

            def affinity(q):
                pe.wait_ge(copied, q + 1)
                if q >= 2:
                    pe.wait_ge(aff_copied, q - 1)
                for i in range(QUAD):
                    for k in range(KD):
                        ins = pe.matmul(ps_a[q % 2][0:S, E * i:E * (i + 1)], f_t[:, q % 2, k, S * i:S * (i + 1)],
                                        cent[:, k, :], start=(k == 0), stop=(k == KD - 1))
                ins.then_inc(aff_ready, 1)

            pe.wait_ge(cent_loaded, 16)
            turn(0)
            for q in range(QUADS):
                if q + 1 < QUADS:
                    turn(q + 1)
                affinity(q)
            pe.wait_ge(onehot_ready, 1)
            one = onehot[:].rearrange("s b e -> s (b e)")
            pe.matmul(ps_b[0:S, 0:B * E], c.before[:], one, start=True, stop=True)
            pe.matmul(ps_n[0:S, 0:B * E], c.ones_f[0:S, 0:S], one, start=True, stop=True).then_inc(before_ready, 1)

        @block.vector
        def _(dve):
            for b in range(B):
                dve.bn_aggr(mv[:, b], c.route_stats[:, b]).then_inc(mv_ready, 1)
            def collect(q):
                dve.wait_ge(aff_ready, q + 1)
                dve.tensor_copy(aff[:, QUAD * q:QUAD * (q + 1)],
                                ps_a[q % 2][0:S, 0:QUAD * E].rearrange("p (b e) -> p b e", e=E)).then_inc(aff_copied, 1)

            for q in range(QUADS):
                if q >= 2:
                    dve.wait_ge(turned, q - 1)
                dve.wait_ge(rstd_ready, q + 1)
                for i in range(QUAD):
                    b = QUAD * q + i
                    ins = dve.tensor_scalar(feats[:, q % 2, i], c.x[:, b, 0:D], mv[:, b, 0:1], rstd[:, b:b + 1],
                                            ALU.subtract, ALU.mult)
                ins.then_inc(feats_ready, 1)
                if q >= 1:
                    collect(q - 1)
            collect(QUADS - 1)

            n = [0]

            def link(ins):
                n[0] += 1
                ins.then_inc(chain, 1)
                dve.wait_ge(chain, n[0])

            def over_e(t):
                return t.unsqueeze(2).to_broadcast([S, B, E])

            def over_b(t):
                return t.unsqueeze(1).to_broadcast([S, B, E])

            dve.wait_ge(aff_copied, QUADS)
            dve.wait_ge(tables_ready, 6)
            link(dve.tensor_reduce(top[:], aff[:], AX_X, ALU.max))
            link(dve.tensor_tensor(best[:], aff[:], over_e(top[:]), ALU.is_ge))
            link(dve.tensor_tensor(best[:], best[:], over_b(first_w[:]), ALU.mult))
            link(dve.tensor_tensor(best[:], best[:], over_b(nan_w[:]), ALU.add))
            link(dve.tensor_reduce(top[:], best[:], AX_X, ALU.max))
            dve.tensor_tensor(onehot[:], best[:], over_e(top[:]), ALU.is_equal).then_inc(onehot_ready, 1)
            dve.wait_ge(before_ready, 1)
            link(dve.tensor_copy(totals[:], ps_n[0:S, 0:B * E].rearrange("p (b e) -> p b e", e=E)))
            src, step, k = totals, 1, 0
            while step < B:
                dst = scan[k % 2]
                dve.tensor_copy(dst[:, 0:step], src[:, 0:step])
                link(dve.tensor_tensor(dst[:, step:B], src[:, step:B], src[:, 0:B - step], ALU.add))
                src, step, k = dst, 2 * step, k + 1
            link(dve.tensor_tensor(more[:], src[:, B - 1].unsqueeze(2).to_broadcast([S, E, MAXT]),
                                   steps[:].unsqueeze(1).to_broadcast([S, E, MAXT]), ALU.is_gt))
            link(dve.tensor_reduce(n_tiles[:], more[:], AX_X, ALU.add))
            end, step, j = n_tiles, 1, 0
            while step < E:
                dst = ends[j % 2]
                dve.tensor_copy(dst[:, 0:step], end[:, 0:step])
                link(dve.tensor_tensor(dst[:, step:E], end[:, step:E], end[:, 0:E - step], ALU.add))
                end, step, j = dst, 2 * step, j + 1
            link(dve.tensor_tensor(start[:], end[:], n_tiles[:], ALU.subtract))
            link(dve.tensor_scalar(start[:], start[:], float(T), None, ALU.mult))
            link(dve.tensor_tensor(pos[:], src[:], totals[:], ALU.subtract))
            link(dve.tensor_tensor(pos[:], ps_b[0:S, 0:B * E].rearrange("p (b e) -> p b e", e=E), pos[:], ALU.add))
            link(dve.tensor_tensor(pos[:], pos[:], over_b(start[:]), ALU.add))
            link(dve.tensor_tensor(pos[:], pos[:], onehot[:], ALU.mult))
            link(dve.tensor_reduce(slot_f[:], pos[:], AX_X, ALU.add))
            dve.tensor_copy(slot[:], slot_f[:]).then_inc(slot_ready, 1)
            link(dve.tensor_tensor(past[:], end[0:1].unsqueeze(1).to_broadcast([1, TILES + 1, E]),
                                   tile_no[:].unsqueeze(2).to_broadcast([1, TILES + 1, E]), ALU.is_le))
            link(dve.tensor_reduce(expert_f[:], past[:], AX_X, ALU.add))
            link(dve.tensor_scalar(expert_f[:], expert_f[:], float(E - 1), None, ALU.min))
            dve.tensor_copy(c.tile_expert[:], expert_f[:]).then_inc(experts_ready, 1)


def experts(nc, c, xs, w1, w2, out):
    with ExitStack() as ctx:
        def sb(name, shape, dt=F32):
            return ctx.enter_context(nc.sbuf_tensor(name, shape, dt))

        def psum(name, shape, dt=F32):
            return ctx.enter_context(nc.psum_tensor(name, shape, dt))

        def sem(name):
            return ctx.enter_context(nc.semaphore(name))

        NH = T // 128
        HID_ACT, HID_DVE = (0, 2, 4, 6, 7), (1, 3, 5)
        rows = sb("rows", [128, 2, NH, ROWW])
        stats = sb("stats4", [128, NH, 6])
        mv = sb("mv4", [128, NH, 2])
        var_eps = sb("var_eps4", [128, NH])
        rstd = sb("rstd4", [128, NH])
        feats = sb("feats4", [128, NH, D])
        xhat = sb("xhat", [128, NH, D])
        prod = sb("prod", [128, NH, D])
        z = sb("z", [128, NH])
        ez = sb("ez", [128, NH])
        alpha = sb("alpha", [128, 2, NH])
        xf = sb("xf", [128, 2, NH, D])
        token = sb("token", [128, 2, NH], U32)
        h_in = sb("h_in", [128, 2, KD, T])
        hid = sb("hid", [128, NF, T])
        y = sb("y", [128, NH, D])
        res = sb("res", [128, 2, NH, D])

        ps_x = psum("psd_x", [128, KD * T])
        ps_h = [psum(f"psd_h{i}", [128, 512]) for i in range(4)]
        ps_y = [psum(f"psd_y{i}", [128, 512]) for i in range(NH)]

        act_passed = sem("act_passed4")
        dve_passed = sem("dve_passed4")
        pool_passed = sem("pool_passed4")
        rows_loaded = [sem(f"rows4_loaded{p}") for p in range(2)]
        stats_ready = sem("stats4_ready")
        mv_ready = sem("mv4_ready")
        eps_added = sem("eps4_added")
        rstd_ready = sem("rstd4_ready")
        feats_ready = sem("feats4_ready")
        xhat_ready = sem("xhat_ready")
        prod_ready = sem("prod_ready")
        z_ready = sem("z_ready")
        ez_ready = sem("ez_ready")
        alpha_step = sem("alpha_step")
        xf_ready = sem("xf_ready")
        token_ready = sem("token_ready")
        turned = sem("turned4")
        h_in_ready = sem("h_in_ready")
        hid_filled = sem("hid_filled")
        hid_act = sem("hid_act")
        hid_dve = sem("hid_dve")
        y_filled = sem("y_filled")
        y_ready = sem("y4_ready")
        res_ready = sem("res_ready")
        scattered = [sem(f"scattered{p}") for p in range(2)]

        def over_tiles(eng, emit):
            emit(0, 0, False)
            emit(1, 1, False)
            with eng.Fori(1, TILES // 2 - 1) as i:
                emit(i * 2, 0, False)
                emit(i * 2 + 1, 1, False)
            emit(TILES - 2, 0, False)
            emit(TILES - 1, 1, True)

        block = ctx.enter_context(nc.Block())

        @block.sync
        def _(sp):
            def load_rows(j, p):
                reach(sp, xf_ready, j - 1)
                reach(sp, token_ready, j - 1)
                src = xs[j * T:(j + 1) * T, :] if isinstance(j, int) else xs[bass.ds(j * T, T), :]
                sp.dma_start(rows[:, p], src.rearrange("(t r) d -> r t d", r=128)).then_inc(rows_loaded[p], 16)

            load_rows(0, 0)

            def load(j, p, last):
                if not (isinstance(j, int) and j < 2):
                    e = expert_of(sp, c, j)
                    reach(sp, y_filled, NH * (j - 1))
                    load_weights(sp, c, e, p, w1, w2)
                if not last:
                    load_rows(j + 1, 1 - p)

            over_tiles(sp, load)

        @block.gpsimd
        def _(pool):
            def inverse_root(n):
                pool.wait_ge(mv_ready, n * NH + NH)
                pool.sem_inc(pool_passed, 1)
                pool.tensor_scalar(var_eps[:], mv[:, :, 1], EPS, None, ALU.add).then_inc(eps_added, 1)
                pool.wait_ge(eps_added, n + 1)
                pool.tensor_tensor(rstd[:], var_eps[:], c.minus_half[:, 0:NH], ALU.pow).then_inc(rstd_ready, 1)

            def prepare(j, p):
                inverse_root(j * 2)
                pool.wait_ge(feats_ready, j + 1)
                reach(pool, res_ready, NH * (j - 1))
                pool.tensor_tensor(xf[:, p], rows[:, p, :, 0:D], feats[:], ALU.add).then_inc(xf_ready, 1)
                inverse_root(j * 2 + 1)

            def finish(j, p):
                for t in range(NH):
                    pool.wait_ge(res_ready, NH * j + (t + 1))
                    pool.sem_inc(pool_passed, 1)
                    pool.indirect_dma_start(
                        out=out, out_offset=bass.IndirectOffsetOnAxis(ap=token[:, p, t:t + 1], axis=0),
                        in_=res[:, p, t, :], in_offset=None, bounds_check=B * S - 1,
                        oob_is_err=False).then_inc(scattered[p], 16)

            prepare(0, 0)

            def step(j, p, last):
                if not last:
                    prepare(j + 1, 1 - p)
                finish(j, p)

            over_tiles(pool, step)
            for p in range(2):
                pool.wait_ge(scattered[p], 16 * NH * (TILES // 2))

        @block.scalar
        def _(act):
            act.wait_ge(c.tables, 16 * 5)

            def prepare(j, p):
                e = expert_of(act, c, j)
                act.wait_ge(turned, j + 1)
                act.sem_inc(act_passed, 1)
                for k in range(KD):
                    ins = act.activation(h_in[:, p, k], ps_x[:, T * k:T * (k + 1)], ACT.Identity,
                                         bias=c.bet[:, k, bass.ds(e, 1)], scale=c.gam[:, k, bass.ds(e, 1)])
                ins.then_inc(h_in_ready, 1)
                act.wait_ge(z_ready, j + 1)
                act.activation(ez[:], z[:], ACT.Exp, scale=-1.0).then_inc(ez_ready, 1)

            prepare(0, 0)

            def step(j, p, last):
                e = expert_of(act, c, j)
                for f in HID_ACT:
                    act.wait_ge(hid_filled, NF * j + (f + 1))
                    if f == 0:
                        reach(act, y_filled, NH * j)
                    act.sem_inc(act_passed, 1)
                    act.activation(hid[:, f], ps_h[f % 4][:, 0:T], ACT.Relu,
                                   bias=c.b1_sb[:, f, bass.ds(e, 1)]).then_inc(hid_act, 1)
                if not last:
                    prepare(j + 1, 1 - p)

            over_tiles(act, step)

        @block.vector
        def _(dve):
            dve.wait_ge(c.tables, 16 * 5)

            def moments(n, src):
                for t in range(NH):
                    dve.bn_stats(stats[:, t], src[:, t, 0:D]).then_inc(stats_ready, 1)
                dve.wait_ge(stats_ready, n * NH + NH)
                dve.sem_inc(dve_passed, 1)
                for t in range(NH):
                    dve.bn_aggr(mv[:, t], stats[:, t]).then_inc(mv_ready, 1)

            def normalize(n, dst, src, ready):
                dve.wait_ge(rstd_ready, n + 1)
                for t in range(NH):
                    ins = dve.tensor_scalar(dst[:, t], src[:, t, 0:D], mv[:, t, 0:1], rstd[:, t:t + 1], ALU.subtract,
                                            ALU.mult)
                ins.then_inc(ready, 1)

            def features(j, p):
                dve.wait_ge(rows_loaded[p], (j - p) * 8 + 16)
                reach(dve, xf_ready, j)
                moments(j * 2, rows[:, p])

            def again(j, p):
                normalize(j * 2, feats, rows[:, p], feats_ready)
                dve.wait_ge(feats_ready, j + 1)
                dve.sem_inc(dve_passed, 1)
                moments(j * 2 + 1, feats)

            def center(j, p):
                reach(dve, turned, j)
                normalize(j * 2 + 1, xhat, feats, xhat_ready)

            def weigh(j, p):
                e = expert_of(dve, c, j)
                reach(dve, ez_ready, j)
                dve.tensor_tensor(prod[:], feats[:], c.cen[:, bass.ds(e, 1), :].to_broadcast([128, NH, D]),
                                  ALU.mult).then_inc(prod_ready, 1)
                dve.wait_ge(prod_ready, j + 1)
                dve.tensor_reduce(z[:], prod[:], AX_X, ALU.add).then_inc(z_ready, 1)
                reach(dve, res_ready, NH * (j - 1))
                dve.wait_ge(rows_loaded[p], (j - p) * 8 + 16)
                reach(dve, scattered[p], (j - p) * 16)
                dve.tensor_copy(token[:, p], rows[:, p, :, D]).then_inc(token_ready, 1)
                dve.wait_ge(ez_ready, j + 1)
                dve.tensor_scalar(ez[:], ez[:], 1.0, None, ALU.add).then_inc(alpha_step, 1)
                dve.wait_ge(alpha_step, 2 * j + 1)
                dve.reciprocal(alpha[:, p], ez[:]).then_inc(alpha_step, 1)

            features(0, 0)
            again(0, 0)
            center(0, 0)
            weigh(0, 0)

            def step(j, p, last):
                e = expert_of(dve, c, j)
                for f in HID_DVE:
                    dve.wait_ge(hid_filled, NF * j + (f + 1))
                    if f == 1:
                        reach(dve, y_filled, NH * j)
                    dve.tensor_scalar(hid[:, f], ps_h[f % 4][:, 0:T], c.b1_sb[:, f, bass.ds(e, 1)], 0.0, ALU.add,
                                      ALU.max).then_inc(hid_dve, 1)
                    if f == 1 and not last:
                        features(j + 1, 1 - p)
                if not last:
                    again(j + 1, 1 - p)
                    center(j + 1, 1 - p)
                    weigh(j + 1, 1 - p)
                e = expert_of(dve, c, j)
                dve.wait_ge(alpha_step, 2 * j + 2)
                dve.wait_ge(xf_ready, j + 1)
                reach(dve, scattered[p], (j - p) * 16)
                for t in range(NH):
                    dve.wait_ge(y_filled, NH * j + (t + 1))
                    dve.tensor_tensor(y[:, t], ps_y[t][:, 0:D], c.b2_sb[:, bass.ds(e, 1), :].rearrange(
                        "p o d -> p (o d)"), ALU.add).then_inc(y_ready, 1)
                for t in range(NH):
                    dve.wait_ge(y_ready, NH * j + (t + 1))
                    dve.scalar_tensor_tensor(out=res[:, p, t], in0=y[:, t], scalar=alpha[:, p, t:t + 1],
                                             in1=xf[:, p, t], op0=ALU.mult, op1=ALU.add).then_inc(res_ready, 1)

            over_tiles(dve, step)

        @block.tensor
        def _(pe):
            def turn(j, p):
                pe.wait_ge(xhat_ready, j + 1)
                reach(pe, h_in_ready, j)
                for k in range(KD):
                    for t in range(NH):
                        ins = pe.transpose(ps_x[:, T * k + 128 * t:T * k + 128 * (t + 1)],
                                           xhat[:, t, 128 * k:128 * (k + 1)], c.ident[:])
                ins.then_inc(turned, 1)

            def copied(j, f):
                if f in HID_ACT:
                    pe.wait_ge(hid_act, len(HID_ACT) * j + HID_ACT.index(f) + 1)
                else:
                    pe.wait_ge(hid_dve, len(HID_DVE) * j + HID_DVE.index(f) + 1)

            turn(0, 0)

            def step(j, p, last):
                pe.wait_ge(c.w_loaded[p], (j - p) * 16 + 32)
                pe.wait_ge(h_in_ready, j + 1)
                for f in range(NF):
                    if f >= 4:
                        copied(j, f - 4)
                    for k in range(KD):
                        ins = pe.matmul(ps_h[f % 4][:, 0:T], c.w1_sb[:, p, k, 128 * f:128 * (f + 1)], h_in[:, p, k],
                                        start=(k == 0), stop=(k == KD - 1))
                    ins.then_inc(hid_filled, 1)
                reach(pe, y_ready, NH * j)
                for t in range(NH):
                    for f in range(NF):
                        if t == 0:
                            copied(j, f)
                        ins = pe.matmul(ps_y[t][:, 0:D], hid[:, f, 128 * t:128 * (t + 1)], c.w2_sb[:, p, f, :],
                                        start=(f == 0), stop=(f == NF - 1))
                    ins.then_inc(y_filled, 1)
                    if t == 0 and not last:
                        turn(j + 1, 1 - p)

            over_tiles(pe, step)


def build(nc, ins, out):
    c = Shared()
    with ExitStack() as ctx:
        def sb(name, shape, dt=F32):
            return ctx.enter_context(nc.sbuf_tensor(name, shape, dt))

        c.x = sb("x_all", [S, B, ROWW])
        c.ident = sb("ident", [128, 128])
        c.neg_ident = sb("neg_ident", [128, 128])
        c.ones_f = sb("ones_f", [128, 128])
        c.ones_r = sb("ones_r", [128, 128], F32R)
        c.before = sb("before", [S, S])
        c.head_of_8 = sb("head_of_8", [128, HG])
        c.head_of = sb("head_of", [128, 4])
        c.route_stats = sb("route_stats", [S, B, 6])
        c.minus_half = sb("minus_half", [128, B])
        v_dram = nc.dram_tensor("v_rows", (B, S, O1), F32, kind="Internal").ap()
        xs = nc.dram_tensor("routed_rows", (SLOTS, ROWW), F32, kind="Internal").ap()
        c.tile_expert = sb("tile_expert", [1, TILES + 1], I32)
        c.empty = sb("empty", [128, ROWW])
        c.xs_cleared = ctx.enter_context(nc.semaphore("xs_cleared"))
        constants(nc, c)
        self_attention(nc, c, ins["x"], ins["wqkT"], ins["wvT"], ins["woT"], v_dram, xs)
        cross_attention(nc, c, ins["context"], ins["mask"], ins["maskT"], ins["wq2T"], ins["wk2T"], ins["wv2T"],
                        ins["wo2T"], ins["bq"], ins["bk"], ins["bv"], ins["bo"])
        with ExitStack() as late:
            expert_buffers(nc, c, late)
            route(nc, c, ins["centT"], xs, ins["w1"], ins["w2"], ins["gamma"], ins["beta"], ins["b1"], ins["b2"],
                  ins["centroids"])
            experts(nc, c, xs, ins["w1"], ins["w2"], out.rearrange("b s d -> (b s) d"))


def kernel(**inputs):
    import numpy as _np
    import concourse.bacc as _bacc
    from concourse import mybir as _mybir
    from concourse.bass_utils import run_bass_kernel_spmd as _run

    a = {k: _np.asarray(v) for k, v in inputs.items()}
    lay = {
        "x": a["x"],
        "wqkT": _np.concatenate([a["L0_attn_wq"].T, a["L0_attn_wk"].T], axis=1),
        "wvT": a["L0_attn_wv"].T,
        "woT": a["L0_attn_wo"].T,
        "context": a["ctx_1024"],
        "mask": a["mask_Bx1x1xS2_if1"].reshape(B, S2),
        "maskT": a["mask_Bx1x1xS2_if1"].reshape(B, S2).T,
        "wq2T": a["L0_xattn_Wq"].T,
        "wk2T": a["L0_xattn_Wk"].T,
        "wv2T": a["L0_xattn_Wv"].T,
        "wo2T": a["L0_xattn_Wo"].T,
        "bq": a["L0_xattn_bq"].reshape(KD, 128).T,
        "bk": a["L0_xattn_bk"].reshape(KD, 128).T,
        "bv": a["L0_xattn_bv"],
        "bo": a["L0_xattn_bo"],
        "centT": a["L0_ffn_centroids"].T,
        "centroids": a["L0_ffn_centroids"],
        "w1": a["L0_ffn_w1"],
        "w2": a["L0_ffn_w2"],
        "gamma": a["L0_ffn_gamma"].reshape(E, KD, 128).transpose(2, 1, 0),
        "beta": a["L0_ffn_beta"].reshape(E, KD, 128).transpose(2, 1, 0),
        "b1": a["L0_ffn_b1"].reshape(E, NF, 128).transpose(2, 1, 0),
        "b2": a["L0_ffn_b2"],
    }
    nc = _bacc.Bacc("TRN2", target_bir_lowering=False, num_devices=1)
    arrays, ins = {}, {}
    for name, v in lay.items():
        v = _np.ascontiguousarray(v)
        arrays[f"in_{name}"] = v
        ins[name] = nc.dram_tensor(f"in_{name}", v.shape, _mybir.dt.from_np(v.dtype), kind="ExternalInput").ap()
    out = nc.dram_tensor("out_0", (B, S, D), F32, kind="ExternalOutput").ap()
    build(nc, ins, out)
    r = _run(nc, [arrays], core_ids=[0])
    return r.results[0]["out_0"]
```
